# Optimizing a Trainium2 kernel written in Bass

```python
import numpy as np
import jax
import jax.numpy as jnp

def _softmax(x, axis=-1):
    return jax.nn.softmax(x, axis=axis)

def _gelu(x):
    return jax.nn.gelu(x, approximate=True)

def _silu(x):
    return jax.nn.silu(x)

def _sigmoid(x):
    return jax.nn.sigmoid(x)

def _layernorm(x, axis=-1, eps=1e-05):
    m = jnp.mean(x, axis=axis, keepdims=True)
    v = jnp.var(x, axis=axis, keepdims=True)
    return (x - m) / jnp.sqrt(v + eps)

def _scatter_add(tgt, idx, src, axis=0):
    return tgt.at[idx].add(src)

def _segment_sum(src, seg, n):
    return jax.ops.segment_sum(src, seg, n)
kernel_name = 'mk_seq_preln_d4_jaxref_r8_9c3d10'

def setup_inputs(seed: int=0):
    np.random.seed(seed)
    _w = jnp.asarray

    def _L0_attn_setup():
        import jax, jax.numpy as jnp
        import numpy as np
        B, S, D, H = (2, 256, 256, 16)
        HD = D // H
        key = jax.random.key(seed)
        ks = jax.random.split(key, 6)
        scale = 1.0 / np.sqrt(D)
        x = jax.random.normal(ks[0], (B, S, D), dtype=jnp.float32)
        wq = jax.random.normal(ks[1], (D, D), dtype=jnp.float32) * scale
        wk = jax.random.normal(ks[2], (D, D), dtype=jnp.float32) * scale
        wv = jax.random.normal(ks[3], (D, D), dtype=jnp.float32) * scale
        wo = jax.random.normal(ks[4], (D, D), dtype=jnp.float32) * scale
        bo = jnp.zeros((D,), dtype=jnp.float32)
        return {'x': x, 'wq': wq, 'wk': wk, 'wv': wv, 'wo': wo, 'bo': bo}
    _L0_attn_in = _L0_attn_setup()

    def _L0_ffn_setup():
        import jax, jax.numpy as jnp
        import numpy as np
        TOPK = 6
        CAP = 128
        ROUTE_SCALE = 1.0
        key = jax.random.key(seed)
        k = jax.random.split(key, 6)
        B, T, C = (2, 256, 256)
        E, H, HS = (64, 32, 64)
        std = 0.01
        return {'x': jax.random.normal(k[0], (B, T, C), jnp.float32), 'w_gate': jax.random.normal(k[1], (C, E), jnp.float32) * std, 'w_shared_up': jax.random.normal(k[2], (C, 2 * HS), jnp.float32) * std, 'w_shared_down': jax.random.normal(k[3], (HS, C), jnp.float32) * std, 'w_up': jax.random.normal(k[4], (E, C, 2 * H), jnp.float32) * std, 'w_down': jax.random.normal(k[5], (E, H, C), jnp.float32) * std}
    _L0_ffn_in = _L0_ffn_setup()

    def _L1_attn_setup():
        import jax, jax.numpy as jnp
        import numpy as np
        HIDDEN = 256
        HEADS = 32
        HEAD_DIM = HIDDEN // HEADS
        MAX_POS = 64
        TABLE = 2 * MAX_POS - 1

        def _rel_bias(rel_pos, seq_len):
            pos = jnp.arange(seq_len)
            rel = pos[None, :] - pos[:, None] + (MAX_POS - 1)
            rel = jnp.clip(rel, 0, TABLE - 1)
            return rel_pos[rel].mean(axis=-1)
        key = jax.random.key(seed)
        k = jax.random.split(key, 6)
        B, S = (16, 64)
        return {'hidden_states': jax.random.normal(k[0], (B, S, HIDDEN), dtype=jnp.float32), 'wq': jax.random.normal(k[1], (HIDDEN, HIDDEN), dtype=jnp.float32) * 0.02, 'wk': jax.random.normal(k[2], (HIDDEN, HIDDEN), dtype=jnp.float32) * 0.02, 'wv': jax.random.normal(k[3], (HIDDEN, HIDDEN), dtype=jnp.float32) * 0.02, 'wo': jax.random.normal(k[4], (HIDDEN, HIDDEN), dtype=jnp.float32) * 0.02, 'rel_pos': jax.random.normal(k[5], (TABLE, HEAD_DIM), dtype=jnp.float32)}
    _L1_attn_in = _L1_attn_setup()

    def _L1_ffn_setup():
        import jax, jax.numpy as jnp
        import numpy as np
        EPS = 1e-06
        K_STEPS = 4
        USE_GATING = True

        def layer_norm(x, gamma, beta):
            mu = jnp.mean(x, axis=-1, keepdims=True)
            var = jnp.mean(jnp.square(x - mu), axis=-1, keepdims=True)
            return (x - mu) * jax.lax.rsqrt(var + EPS) * gamma + beta
        key = jax.random.key(seed)
        B, L, D, H = (4, 512, 256, 1024)
        ks = jax.random.split(key, 16)
        s = 0.02
        return {'x': jax.random.normal(ks[0], (B, L, D), dtype=jnp.float32), 'in_gamma': jnp.ones((D,), jnp.float32), 'in_beta': jnp.zeros((D,), jnp.float32), 'agg_w': jax.random.normal(ks[1], (D, D), jnp.float32) * s, 'agg_b': jnp.zeros((D,), jnp.float32), 'pn_gamma': jnp.ones((D,), jnp.float32), 'pn_beta': jnp.zeros((D,), jnp.float32), 'd1_w': jax.random.normal(ks[2], (D, H), jnp.float32) * s, 'd1_b': jnp.zeros((H,), jnp.float32), 'd2_w': jax.random.normal(ks[3], (H, D), jnp.float32) * s, 'd2_b': jnp.zeros((D,), jnp.float32), 'bc_w': jax.random.normal(ks[4], (D, D), jnp.float32) * s, 'bc_b': jnp.zeros((D,), jnp.float32), 'gate_w': jax.random.normal(ks[5], (D, D), jnp.float32) * s, 'gate_b': jnp.zeros((D,), jnp.float32), 'out_gamma': jnp.ones((D,), jnp.float32), 'out_beta': jnp.zeros((D,), jnp.float32)}
    _L1_ffn_in = _L1_ffn_setup()

    def _L2_attn_setup():
        import jax, jax.numpy as jnp
        import numpy as np
        import math
        B, T, E = (2, 256, 256)
        G, QPG, D = (4, 4, 128)

        def sinusoidal_pe(t, d, dtype):
            pos = jnp.arange(t, dtype=jnp.float32)[:, None]
            i = jnp.arange(0, d, 2, dtype=jnp.float32)
            inv_freq = jnp.exp(-(jnp.log(10000.0) * i / d))
            ang = pos * inv_freq
            pe = jnp.zeros((t, d), dtype=jnp.float32)
            pe = pe.at[:, 0::2].set(jnp.sin(ang)).at[:, 1::2].set(jnp.cos(ang))
            return pe.astype(dtype)
        key = jax.random.key(seed)
        ks = jax.random.split(key, 6)
        s = lambda fan_in: 1.0 / math.sqrt(fan_in)
        return {'x': jax.random.normal(ks[0], (B, T, E), dtype=jnp.float32), 'wq': jax.random.uniform(ks[1], (E, G * QPG * D), jnp.float32, -s(E), s(E)), 'bq': jax.random.uniform(ks[2], (G * QPG * D,), jnp.float32, -s(E), s(E)), 'wkv': jax.random.uniform(ks[3], (E, 2 * G * D), jnp.float32, -s(E), s(E)), 'bkv': jax.random.uniform(ks[4], (2 * G * D,), jnp.float32, -s(E), s(E)), 'wo': jax.random.uniform(ks[5], (G * QPG * D, E), jnp.float32, -s(G * QPG * D), s(G * QPG * D))}
    _L2_attn_in = _L2_attn_setup()

    def _L2_ffn_setup():
        import jax, jax.numpy as jnp
        import numpy as np
        K_TOP = 2
        key = jax.random.key(seed)
        ks = jax.random.split(key, 6)
        s = 0.02
        B, S, H, D = (4, 128, 256, 128)
        E_SH, E_RT = (2, 16)
        return {'x': jax.random.normal(ks[0], (B, S, H), dtype=jnp.float32), 'Wsh_up': jax.random.normal(ks[1], (E_SH, H, D), dtype=jnp.float32) * s, 'Wsh_down': jax.random.normal(ks[2], (E_SH, D, H), dtype=jnp.float32) * s, 'Wrt_up': jax.random.normal(ks[3], (E_RT, H, D), dtype=jnp.float32) * s, 'Wrt_down': jax.random.normal(ks[4], (E_RT, D, H), dtype=jnp.float32) * s, 'W_router': jax.random.normal(ks[5], (H, E_RT), dtype=jnp.float32) * s}
    _L2_ffn_in = _L2_ffn_setup()

    def _L3_attn_setup():
        import jax, jax.numpy as jnp
        import numpy as np
        import math
        H = 16
        DN = 128
        DR = 64
        DV = 128
        ROPE_BASE = 10000.0

        def _rope_cos_sin(seq_len, dim, dtype):
            inv_freq = 1.0 / ROPE_BASE ** (jnp.arange(0, dim, 2, dtype=jnp.float32) / dim)
            t = jnp.arange(seq_len, dtype=jnp.float32)
            freqs = t[:, None] * inv_freq[None, :]
            return (jnp.cos(freqs).astype(dtype), jnp.sin(freqs).astype(dtype))

        def _apply_rope(x, cos, sin):
            half = x.shape[-1] // 2
            x1, x2 = (x[..., :half], x[..., half:])
            c = cos[None, :, None, :]
            s = sin[None, :, None, :]
            return jnp.concatenate([x1 * c - x2 * s, x1 * s + x2 * c], axis=-1)
        key = jax.random.key(seed)
        ks = jax.random.split(key, 5)
        hidden = 256
        B, S = (1, 256)
        q_size = H * (DN + DR)
        v_size = H * DV
        std = 0.02
        return {'hidden_states': jax.random.normal(ks[0], (B, S, hidden), jnp.float32), 'Wq': jax.random.normal(ks[1], (q_size, hidden), jnp.float32) * std, 'Wk': jax.random.normal(ks[2], (q_size, hidden), jnp.float32) * std, 'Wv': jax.random.normal(ks[3], (v_size, hidden), jnp.float32) * std, 'Wo': jax.random.normal(ks[4], (hidden, v_size), jnp.float32) * std}
    _L3_attn_in = _L3_attn_setup()

    def _L3_ffn_setup():
        import jax, jax.numpy as jnp
        import numpy as np
        NUM_EXPERTS = 32
        TOP_K = 6
        N_GROUPS = 4
        N_LIMITED_GROUPS = 2
        key = jax.random.key(seed)
        ks = jax.random.split(key, 8)
        H, M = (256, 176)
        SH = 2 * M
        s = 0.02
        return {'hidden_states': jax.random.normal(ks[0], (4, 256, H), jnp.float32), 'gate_w': jax.random.normal(ks[1], (H, NUM_EXPERTS), jnp.float32) * s, 'w_gate': jax.random.normal(ks[2], (NUM_EXPERTS, H, M), jnp.float32) * s, 'w_up': jax.random.normal(ks[3], (NUM_EXPERTS, H, M), jnp.float32) * s, 'w_down': jax.random.normal(ks[4], (NUM_EXPERTS, M, H), jnp.float32) * s, 'sw_gate': jax.random.normal(ks[5], (H, SH), jnp.float32) * s, 'sw_up': jax.random.normal(ks[6], (H, SH), jnp.float32) * s, 'sw_down': jax.random.normal(ks[7], (SH, H), jnp.float32) * s}
    _L3_ffn_in = _L3_ffn_setup()
    _d = {'L0_attn_x': _L0_attn_in['x'], 'L0_attn_wq': _L0_attn_in['wq'], 'L0_attn_wk': _L0_attn_in['wk'], 'L0_attn_wv': _L0_attn_in['wv'], 'L0_attn_wo': _L0_attn_in['wo'], 'L0_attn_bo': _L0_attn_in['bo'], 'L0_ffn_w_gate': _L0_ffn_in['w_gate'], 'L0_ffn_w_shared_up': _L0_ffn_in['w_shared_up'], 'L0_ffn_w_shared_down': _L0_ffn_in['w_shared_down'], 'L0_ffn_w_up': _L0_ffn_in['w_up'], 'L0_ffn_w_down': _L0_ffn_in['w_down'], 'L1_attn_wq': _L1_attn_in['wq'], 'L1_attn_wk': _L1_attn_in['wk'], 'L1_attn_wv': _L1_attn_in['wv'], 'L1_attn_wo': _L1_attn_in['wo'], 'L1_attn_rel_pos': _L1_attn_in['rel_pos'], 'L1_ffn_in_gamma': _L1_ffn_in['in_gamma'], 'L1_ffn_in_beta': _L1_ffn_in['in_beta'], 'L1_ffn_agg_w': _L1_ffn_in['agg_w'], 'L1_ffn_agg_b': _L1_ffn_in['agg_b'], 'L1_ffn_pn_gamma': _L1_ffn_in['pn_gamma'], 'L1_ffn_pn_beta': _L1_ffn_in['pn_beta'], 'L1_ffn_d1_w': _L1_ffn_in['d1_w'], 'L1_ffn_d1_b': _L1_ffn_in['d1_b'], 'L1_ffn_d2_w': _L1_ffn_in['d2_w'], 'L1_ffn_d2_b': _L1_ffn_in['d2_b'], 'L1_ffn_bc_w': _L1_ffn_in['bc_w'], 'L1_ffn_bc_b': _L1_ffn_in['bc_b'], 'L1_ffn_gate_w': _L1_ffn_in['gate_w'], 'L1_ffn_gate_b': _L1_ffn_in['gate_b'], 'L1_ffn_out_gamma': _L1_ffn_in['out_gamma'], 'L1_ffn_out_beta': _L1_ffn_in['out_beta'], 'L2_attn_wq': _L2_attn_in['wq'], 'L2_attn_bq': _L2_attn_in['bq'], 'L2_attn_wkv': _L2_attn_in['wkv'], 'L2_attn_bkv': _L2_attn_in['bkv'], 'L2_attn_wo': _L2_attn_in['wo'], 'L2_ffn_Wsh_up': _L2_ffn_in['Wsh_up'], 'L2_ffn_Wsh_down': _L2_ffn_in['Wsh_down'], 'L2_ffn_Wrt_up': _L2_ffn_in['Wrt_up'], 'L2_ffn_Wrt_down': _L2_ffn_in['Wrt_down'], 'L2_ffn_W_router': _L2_ffn_in['W_router'], 'L3_attn_Wq': _L3_attn_in['Wq'], 'L3_attn_Wk': _L3_attn_in['Wk'], 'L3_attn_Wv': _L3_attn_in['Wv'], 'L3_attn_Wo': _L3_attn_in['Wo'], 'L3_ffn_gate_w': _L3_ffn_in['gate_w'], 'L3_ffn_w_gate': _L3_ffn_in['w_gate'], 'L3_ffn_w_up': _L3_ffn_in['w_up'], 'L3_ffn_w_down': _L3_ffn_in['w_down'], 'L3_ffn_sw_gate': _L3_ffn_in['sw_gate'], 'L3_ffn_sw_up': _L3_ffn_in['sw_up'], 'L3_ffn_sw_down': _L3_ffn_in['sw_down']}
    _x0 = _d['L0_attn_x']
    _d['L0_attn_x'] = jax.random.normal(jax.random.fold_in(jax.random.key(seed), 1), (8, 256, 256), dtype=_x0.dtype)
    del _x0
    return _d

def reference(L0_attn_x, L0_attn_wq, L0_attn_wk, L0_attn_wv, L0_attn_wo, L0_attn_bo, L0_ffn_w_gate, L0_ffn_w_shared_up, L0_ffn_w_shared_down, L0_ffn_w_up, L0_ffn_w_down, L1_attn_wq, L1_attn_wk, L1_attn_wv, L1_attn_wo, L1_attn_rel_pos, L1_ffn_in_gamma, L1_ffn_in_beta, L1_ffn_agg_w, L1_ffn_agg_b, L1_ffn_pn_gamma, L1_ffn_pn_beta, L1_ffn_d1_w, L1_ffn_d1_b, L1_ffn_d2_w, L1_ffn_d2_b, L1_ffn_bc_w, L1_ffn_bc_b, L1_ffn_gate_w, L1_ffn_gate_b, L1_ffn_out_gamma, L1_ffn_out_beta, L2_attn_wq, L2_attn_bq, L2_attn_wkv, L2_attn_bkv, L2_attn_wo, L2_ffn_Wsh_up, L2_ffn_Wsh_down, L2_ffn_Wrt_up, L2_ffn_Wrt_down, L2_ffn_W_router, L3_attn_Wq, L3_attn_Wk, L3_attn_Wv, L3_attn_Wo, L3_ffn_gate_w, L3_ffn_w_gate, L3_ffn_w_up, L3_ffn_w_down, L3_ffn_sw_gate, L3_ffn_sw_up, L3_ffn_sw_down):

    def _L0_attn_ref(x, wq, wk, wv, wo, bo):
        import jax, jax.numpy as jnp
        import numpy as np
        B, S, D, H = (2, 256, 256, 16)
        HD = D // H
        b, s, d = x.shape
        q = (x @ wq.T).reshape(b, s, H, HD).transpose(0, 2, 1, 3)
        k = (x @ wk.T).reshape(b, s, H, HD).transpose(0, 2, 1, 3)
        v = (x @ wv.T).reshape(b, s, H, HD).transpose(0, 2, 1, 3)
        scores = jnp.einsum('bhqd,bhkd->bhqk', q, k) / jnp.sqrt(jnp.float32(HD))
        causal = jnp.triu(jnp.ones((s, s), dtype=bool), k=1)
        scores = jnp.where(causal[None, None], -jnp.inf, scores)
        attn = jax.nn.softmax(scores, axis=-1)
        out = jnp.einsum('bhqk,bhkd->bhqd', attn, v)
        out = out.transpose(0, 2, 1, 3).reshape(b, s, d)
        return out @ wo.T + bo

    def _L0_ffn_ref(x, w_gate, w_shared_up, w_shared_down, w_up, w_down):
        import jax, jax.numpy as jnp
        import numpy as np
        TOPK = 6
        CAP = 128
        ROUTE_SCALE = 1.0
        B, T, C = x.shape
        E = w_gate.shape[1]
        x_flat = x.reshape(-1, C)
        N = x_flat.shape[0]
        su = x_flat @ w_shared_up
        y_s, g_s = jnp.split(su, 2, axis=-1)
        shared = jax.nn.silu(g_s) * y_s @ w_shared_down
        scores = jax.nn.sigmoid(x_flat @ w_gate)
        _, topk_idx = jax.lax.top_k(scores, TOPK)
        w = jnp.take_along_axis(scores, topk_idx, axis=-1)
        w = w / w.sum(-1, keepdims=True) * ROUTE_SCALE
        flat_e = topk_idx.reshape(-1)
        oh = jax.nn.one_hot(flat_e, E, dtype=jnp.int32)
        pos = jnp.take_along_axis(jnp.cumsum(oh, axis=0), flat_e[:, None], axis=1)[:, 0] - 1
        valid = pos < CAP
        pos_c = jnp.where(valid, pos, CAP - 1)
        token_ids = jnp.repeat(jnp.arange(N), TOPK)
        x_disp = jnp.zeros((E, CAP, C), x.dtype).at[flat_e, pos].set(x_flat[token_ids], mode='drop')
        up = jnp.einsum('ecd,edh->ech', x_disp, w_up)
        g_r, v_r = jnp.split(up, 2, axis=-1)
        h_r = jax.nn.silu(g_r) * v_r
        out_r = jnp.einsum('ech,ehd->ecd', h_r, w_down)
        y_ts = out_r[flat_e, pos_c]
        y_ts = jnp.where(valid[:, None], y_ts, 0.0)
        routed = (y_ts.reshape(N, TOPK, C) * w[:, :, None]).sum(axis=1)
        return (shared + routed).reshape(B, T, C)

    def _L1_attn_ref(hidden_states, wq, wk, wv, wo, rel_pos):
        import jax, jax.numpy as jnp
        import numpy as np
        HIDDEN = 256
        HEADS = 32
        HEAD_DIM = HIDDEN // HEADS
        MAX_POS = 64
        TABLE = 2 * MAX_POS - 1

        def _rel_bias(rel_pos, seq_len):
            pos = jnp.arange(seq_len)
            rel = pos[None, :] - pos[:, None] + (MAX_POS - 1)
            rel = jnp.clip(rel, 0, TABLE - 1)
            return rel_pos[rel].mean(axis=-1)
        B, S, _ = hidden_states.shape
        scale = jnp.sqrt(jnp.float32(HEAD_DIM))
        q = (hidden_states @ wq.T).reshape(B, S, HEADS, HEAD_DIM).transpose(0, 2, 1, 3)
        k = (hidden_states @ wk.T).reshape(B, S, HEADS, HEAD_DIM).transpose(0, 2, 1, 3)
        v = (hidden_states @ wv.T).reshape(B, S, HEADS, HEAD_DIM).transpose(0, 2, 1, 3)
        scores = jnp.einsum('bhqd,bhkd->bhqk', q, k) / scale
        scores = scores + _rel_bias(rel_pos, S)[None, None]
        attn = jax.nn.softmax(scores, axis=-1)
        ctx = jnp.einsum('bhqk,bhkd->bhqd', attn, v)
        ctx = ctx.transpose(0, 2, 1, 3).reshape(B, S, HIDDEN)
        return ctx @ wo.T

    def _L1_ffn_ref(x, in_gamma, in_beta, agg_w, agg_b, pn_gamma, pn_beta, d1_w, d1_b, d2_w, d2_b, bc_w, bc_b, gate_w, gate_b, out_gamma, out_beta):
        import jax, jax.numpy as jnp
        import numpy as np
        EPS = 1e-06
        K_STEPS = 4
        USE_GATING = True

        def layer_norm(x, gamma, beta):
            mu = jnp.mean(x, axis=-1, keepdims=True)
            var = jnp.mean(jnp.square(x - mu), axis=-1, keepdims=True)
            return (x - mu) * jax.lax.rsqrt(var + EPS) * gamma + beta
        x_norm = layer_norm(x, in_gamma, in_beta)
        thought = x_norm[:, -1, :] @ agg_w + agg_b
        for _ in range(K_STEPS):
            t = layer_norm(thought, pn_gamma, pn_beta)
            t = jax.nn.gelu(t @ d1_w + d1_b, approximate=False)
            thought = thought + (t @ d2_w + d2_b)
        broadcast = (thought @ bc_w + bc_b)[:, None, :]
        if USE_GATING:
            gate = jax.nn.sigmoid(x @ gate_w + gate_b)
            out = x + gate * broadcast
        else:
            out = x + broadcast
        return layer_norm(out, out_gamma, out_beta)

    def _L2_attn_ref(x, wq, bq, wkv, bkv, wo):
        import jax, jax.numpy as jnp
        import numpy as np
        import math
        B, T, E = (2, 256, 256)
        G, QPG, D = (4, 4, 128)

        def sinusoidal_pe(t, d, dtype):
            pos = jnp.arange(t, dtype=jnp.float32)[:, None]
            i = jnp.arange(0, d, 2, dtype=jnp.float32)
            inv_freq = jnp.exp(-(jnp.log(10000.0) * i / d))
            ang = pos * inv_freq
            pe = jnp.zeros((t, d), dtype=jnp.float32)
            pe = pe.at[:, 0::2].set(jnp.sin(ang)).at[:, 1::2].set(jnp.cos(ang))
            return pe.astype(dtype)
        b, t, e = x.shape
        q = (x @ wq + bq).reshape(b, t, G, QPG, D).transpose(0, 2, 3, 1, 4)
        kv = (x @ wkv + bkv).reshape(b, t, G, 1, 2 * D).transpose(0, 2, 3, 1, 4)
        k, v = (kv[..., :D], kv[..., D:])
        pe = sinusoidal_pe(t, D, x.dtype)
        q = q + pe
        k = k + pe
        scores = jnp.einsum('bgqtd,bgksd->bgqts', q, k) / math.sqrt(D)
        causal = jnp.tril(jnp.ones((t, t), dtype=bool))
        scores = jnp.where(causal, scores, -jnp.inf)
        probs = jax.nn.softmax(scores, axis=-1)
        out = jnp.einsum('bgqts,bgksd->btgqd', probs, v).reshape(b, t, G * QPG * D)
        return out @ wo

    def _L2_ffn_ref(x, Wsh_up, Wsh_down, Wrt_up, Wrt_down, W_router):
        import jax, jax.numpy as jnp
        import numpy as np
        K_TOP = 2
        B, S, H = x.shape
        E_rt = Wrt_up.shape[0]
        xt = x.reshape(B * S, H)
        sh_mid = jax.nn.gelu(jnp.einsum('th,ehd->ted', xt, Wsh_up), approximate=False)
        shared_out = jnp.einsum('ted,edh->th', sh_mid, Wsh_down)
        probs = jax.nn.softmax(xt @ W_router, axis=-1)
        top_v, top_i = jax.lax.top_k(probs, K_TOP)
        gate = jnp.sum(jax.nn.one_hot(top_i, E_rt, dtype=xt.dtype) * top_v[..., None], axis=1)
        rt_mid = jax.nn.gelu(jnp.einsum('th,ehd->ted', xt, Wrt_up), approximate=False)
        routed_out = jnp.einsum('ted,edh->th', rt_mid * gate[:, :, None], Wrt_down)
        return (shared_out + routed_out).reshape(B, S, H)

    def _L3_attn_ref(hidden_states, Wq, Wk, Wv, Wo):
        import jax, jax.numpy as jnp
        import numpy as np
        import math
        H = 16
        DN = 128
        DR = 64
        DV = 128
        ROPE_BASE = 10000.0

        def _rope_cos_sin(seq_len, dim, dtype):
            inv_freq = 1.0 / ROPE_BASE ** (jnp.arange(0, dim, 2, dtype=jnp.float32) / dim)
            t = jnp.arange(seq_len, dtype=jnp.float32)
            freqs = t[:, None] * inv_freq[None, :]
            return (jnp.cos(freqs).astype(dtype), jnp.sin(freqs).astype(dtype))

        def _apply_rope(x, cos, sin):
            half = x.shape[-1] // 2
            x1, x2 = (x[..., :half], x[..., half:])
            c = cos[None, :, None, :]
            s = sin[None, :, None, :]
            return jnp.concatenate([x1 * c - x2 * s, x1 * s + x2 * c], axis=-1)
        B, S, _ = hidden_states.shape
        q = hidden_states @ Wq.T
        k = hidden_states @ Wk.T
        v = hidden_states @ Wv.T
        q_nope = q[:, :, :H * DN].reshape(B, S, H, DN)
        q_rope = q[:, :, H * DN:].reshape(B, S, H, DR)
        k_nope = k[:, :, :H * DN].reshape(B, S, H, DN)
        k_rope = k[:, :, H * DN:].reshape(B, S, H, DR)
        v = v.reshape(B, S, H, DV)
        cos, sin = _rope_cos_sin(S, DR, hidden_states.dtype)
        q_rope = _apply_rope(q_rope, cos, sin)
        k_rope = _apply_rope(k_rope, cos, sin)
        scores = jnp.einsum('bqhd,bkhd->bhqk', q_nope, k_nope) / math.sqrt(DN) + jnp.einsum('bqhd,bkhd->bhqk', q_rope, k_rope) / math.sqrt(DR)
        attn = jax.nn.softmax(scores, axis=-1)
        out = jnp.einsum('bhqk,bkhd->bqhd', attn, v)
        out = out.reshape(B, S, H * DV)
        return out @ Wo.T

    def _L3_ffn_ref(hidden_states, gate_w, w_gate, w_up, w_down, sw_gate, sw_up, sw_down):
        import jax, jax.numpy as jnp
        import numpy as np
        NUM_EXPERTS = 32
        TOP_K = 6
        N_GROUPS = 4
        N_LIMITED_GROUPS = 2
        B, S, H = hidden_states.shape
        E, K = (NUM_EXPERTS, TOP_K)
        x = hidden_states.reshape(-1, H)
        T = x.shape[0]
        scores = jax.nn.sigmoid(x @ gate_w)
        original_scores = scores
        epg = E // N_GROUPS
        sg = scores.reshape(T, N_GROUPS, epg)
        group_scores = jnp.max(sg, axis=-1)
        _, top_groups = jax.lax.top_k(group_scores, N_LIMITED_GROUPS)
        mask = jnp.ones((T, N_GROUPS), dtype=bool)
        mask = mask.at[jnp.arange(T)[:, None], top_groups].set(False)
        sg = jnp.where(mask[:, :, None], -jnp.inf, sg)
        masked_scores = sg.reshape(T, E)
        _, selected_experts = jax.lax.top_k(masked_scores, K)
        weights = jnp.take_along_axis(original_scores, selected_experts, axis=-1)
        weights = weights / jnp.sum(weights, axis=-1, keepdims=True)
        sel_flat = selected_experts.ravel()
        x_exp = jnp.repeat(x, K, axis=0)
        sort_idx = jnp.argsort(sel_flat)
        xs = x_exp[sort_idx]
        group_sizes = jnp.bincount(sel_flat, length=E).astype(jnp.int32)
        g = jax.lax.ragged_dot(xs, w_gate, group_sizes)
        u = jax.lax.ragged_dot(xs, w_up, group_sizes)
        d = jax.lax.ragged_dot(jax.nn.silu(g) * u, w_down, group_sizes)
        unsort_idx = jnp.argsort(sort_idx)
        out = d[unsort_idx].reshape(T, K, H)
        expert_out = jnp.sum(out * weights[..., None], axis=1)
        shared = jax.nn.silu(x @ sw_gate) * (x @ sw_up) @ sw_down
        return (expert_out + shared).reshape(B, S, H)
    x = L0_attn_x
    x = x + _L0_attn_ref(_layernorm(x, axis=-1), L0_attn_wq, L0_attn_wk, L0_attn_wv, L0_attn_wo, L0_attn_bo)
    x = x + _L0_ffn_ref(_layernorm(x, axis=-1), L0_ffn_w_gate, L0_ffn_w_shared_up, L0_ffn_w_shared_down, L0_ffn_w_up, L0_ffn_w_down)
    x = x + _L1_attn_ref(_layernorm(x, axis=-1), L1_attn_wq, L1_attn_wk, L1_attn_wv, L1_attn_wo, L1_attn_rel_pos)
    x = x + _L1_ffn_ref(_layernorm(x, axis=-1), L1_ffn_in_gamma, L1_ffn_in_beta, L1_ffn_agg_w, L1_ffn_agg_b, L1_ffn_pn_gamma, L1_ffn_pn_beta, L1_ffn_d1_w, L1_ffn_d1_b, L1_ffn_d2_w, L1_ffn_d2_b, L1_ffn_bc_w, L1_ffn_bc_b, L1_ffn_gate_w, L1_ffn_gate_b, L1_ffn_out_gamma, L1_ffn_out_beta)
    x = x + _L2_attn_ref(_layernorm(x, axis=-1), L2_attn_wq, L2_attn_bq, L2_attn_wkv, L2_attn_bkv, L2_attn_wo)
    x = x + _L2_ffn_ref(_layernorm(x, axis=-1), L2_ffn_Wsh_up, L2_ffn_Wsh_down, L2_ffn_Wrt_up, L2_ffn_Wrt_down, L2_ffn_W_router)
    x = x + _L3_attn_ref(_layernorm(x, axis=-1), L3_attn_Wq, L3_attn_Wk, L3_attn_Wv, L3_attn_Wo)
    x = x + _L3_ffn_ref(_layernorm(x, axis=-1), L3_ffn_gate_w, L3_ffn_w_gate, L3_ffn_w_up, L3_ffn_w_down, L3_ffn_sw_gate, L3_ffn_sw_up, L3_ffn_sw_down)
    return x

_drawn_inputs = setup_inputs


def setup_inputs(seed=0):
    import zlib

    import numpy as np

    out = dict(_drawn_inputs(seed))
    spreads = {'L0_attn_bo': (0.0, 0.1),
     'L1_ffn_in_gamma': (1.0, 0.6),
     'L1_ffn_in_beta': (0.0, 0.8),
     'L1_ffn_agg_b': (0.0, 0.516),
     'L1_ffn_pn_gamma': (1.0, 0.6),
     'L1_ffn_pn_beta': (0.0, 0.8),
     'L1_ffn_d1_b': (0.0, 0.589),
     'L1_ffn_d2_b': (0.0, 0.1),
     'L1_ffn_bc_b': (0.0, 0.304),
     'L1_ffn_gate_b': (0.0, 0.8),
     'L1_ffn_out_gamma': (1.0, 0.2),
     'L1_ffn_out_beta': (0.0, 0.1)}
    factors = {'L0_ffn_w_gate': 8.0,
     'L0_ffn_w_shared_up': 8.0,
     'L0_ffn_w_shared_down': 8.0,
     'L0_ffn_w_up': 8.0,
     'L0_ffn_w_down': 8.0,
     'L1_attn_wq': 8.0,
     'L1_attn_wk': 8.0,
     'L1_attn_wv': 3.897,
     'L1_attn_wo': 4.001,
     'L1_attn_rel_pos': 8.0,
     'L1_ffn_gate_w': 6.092,
     'L2_attn_wq': 4.778,
     'L2_attn_bq': 8.0,
     'L2_attn_bkv': 5.845,
     'L2_ffn_Wrt_up': 8.0,
     'L2_ffn_Wrt_down': 8.0,
     'L2_ffn_W_router': 8.0,
     'L3_attn_Wq': 8.0,
     'L3_attn_Wk': 8.0,
     'L3_ffn_gate_w': 8.0,
     'L3_ffn_w_gate': 8.0,
     'L3_ffn_w_up': 8.0,
     'L3_ffn_w_down': 8.0,
     'L3_ffn_sw_gate': 5.94,
     'L3_ffn_sw_up': 5.896,
     'L3_ffn_sw_down': 5.885}
    for name, (base, spread) in spreads.items():
        noise = np.random.default_rng([zlib.crc32(name.encode()), seed]).standard_normal(out[name].shape)
        drawn = base * np.exp(spread * noise) if base else spread * noise
        out[name] = jnp.asarray(drawn.astype(out[name].dtype))
    for name, factor in factors.items():
        out[name] = (out[name] * factor).astype(out[name].dtype)
    return out
```

```python
import math
from contextlib import ExitStack

import numpy as np

import concourse.bass as bass
from concourse import mybir

F32 = mybir.dt.float32
F32R = mybir.dt.float32r
BF16 = mybir.dt.bfloat16
ALU = mybir.AluOpType
ACT = mybir.ActivationFunctionType
AX = mybir.AxisListType

P = 128
B, S, C = 8, 256, 256
TILES = B * S // P
KT = C // P
QT = S // P
BIG = 3.0e38
MASKED = -1.0e30
PAIRS = B // 2


def need(eng, sem, value):
    if isinstance(value, int) and value <= 0:
        return
    eng.wait_ge(sem, value)


class Stage:

    def __init__(self, core):
        self.nc, self.core, self.stack, self.sems = core.nc, core, ExitStack(), []

    def __enter__(self):
        self.stack.__enter__()
        return self

    def __exit__(self, *error):
        self.stack.__exit__(*error)
        if not error[0]:
            self.nc.clear_and_free_semaphores(self.sems)
            self.nc.all_engine_barrier()

    def sb(self, name, shape, dtype=F32):
        return self.stack.enter_context(self.nc.sbuf_tensor(self.core.unique(name), shape, dtype))

    def sem(self, name):
        s = self.nc.alloc_semaphore(self.core.unique(name))
        self.sems.append(s)
        return s


class Core:

    def __init__(self, nc, stack):
        self.nc, self.count = nc, 0

        def sb(name, shape, dtype=F32):
            return stack.enter_context(nc.sbuf_tensor(name, shape, dtype))

        self.x = sb("x_sb", [P, TILES, C])
        self.norm_t_high = sb("norm_t_high", [P, KT, TILES * P], F32R)
        self.norm_t_low = sb("norm_t_low", [P, KT, TILES * P], F32R)
        self.rstd = sb("rstd", [P, TILES])
        self.shift = sb("shift", [P, TILES])
        self.ident = sb("ident_sb", [P, P])
        self.ident_bf = sb("ident_bf", [P, P], BF16)
        self.bank = [stack.enter_context(nc.psum_tensor(f"bank{i}", [P, 512], F32)) for i in range(8)]

    def unique(self, name):
        self.count += 1
        return f"{name}_{self.count}"


def load_stage(core, x_in, ident_in):
    nc = core.nc
    with Stage(core) as st:
        loaded = st.sem("loaded")
        with nc.Block() as block:

            @block.sync
            def _(sp):
                sp.dma_start(core.x[:], x_in).then_inc(loaded, 16)
                sp.dma_start(core.ident[:], ident_in).then_inc(loaded, 16)
                sp.wait_ge(loaded, 32)

            @block.vector
            def _(dve):
                dve.wait_ge(loaded, 32)
                nc.vector.tensor_copy(core.ident_bf[:], core.ident[:])


def store_stage(core, out):
    nc = core.nc
    with Stage(core) as st:
        stored = st.sem("stored")
        with nc.Block() as block:

            @block.sync
            def _(sp):
                sp.dma_start(out, core.x[:]).then_inc(stored, 16)
                sp.wait_ge(stored, 16)


def norm_stage(core, eps=1e-5):
    nc, x = core.nc, core.x
    with Stage(core) as st:
        stats = st.sb("stats", [P, TILES, 6])
        meanvar = st.sb("meanvar", [P, TILES, 2])
        var_eps = st.sb("var_eps", [P, TILES])
        minus_half = st.sb("minus_half", [P, TILES])
        normed = [[st.sb("normed", [P, C]) for _ in range(QT)] for _ in range(2)]
        stats_ready, meanvar_ready = st.sem("stats_ready"), st.sem("meanvar_ready")
        pool_step, rstd_ready, shift_ready = st.sem("pool_step"), st.sem("rstd_ready"), st.sem("shift_ready")
        normed_ready, transposed = st.sem("normed_ready"), st.sem("transposed")
        high_ready, low_ready = st.sem("high_ready"), st.sem("low_ready")
        bank = core.bank

        def columns(t, b):
            return t[:, :, bass.ds(b * S, S)]

        with nc.Block() as block:

            @block.gpsimd
            def _(pool):
                nc.gpsimd.memset(minus_half[:], -0.5).then_inc(pool_step, 1)
                pool.wait_ge(meanvar_ready, TILES)
                nc.gpsimd.tensor_scalar(var_eps[:], meanvar[:, :, 1], 1.0, float(eps), ALU.mult, ALU.add)\
                    .then_inc(pool_step, 1)
                pool.wait_ge(pool_step, 2)
                nc.gpsimd.tensor_tensor(core.rstd[:], var_eps[:], minus_half[:], ALU.pow).then_inc(rstd_ready, 1)

            @block.vector
            def _(dve):
                for t in range(TILES):
                    nc.vector.bn_stats(stats[:, t, :], x[:, t, :]).then_inc(stats_ready, 1)
                for t in range(TILES):
                    dve.wait_ge(stats_ready, t + 1)
                    nc.vector.bn_aggr(meanvar[:, t, :], stats[:, t, :]).then_inc(meanvar_ready, 1)
                dve.wait_ge(rstd_ready, 1)
                dve.wait_ge(meanvar_ready, TILES)
                nc.vector.scalar_tensor_tensor(core.shift[:], meanvar[:, :, 0], -1.0, core.rstd[:],
                                               ALU.mult, ALU.mult).then_inc(shift_ready, 1)
                dve.wait_ge(shift_ready, 1)

                def apply(b, par):
                    need(dve, transposed, b - 1)
                    for t in range(QT):
                        tile = b * QT + t
                        ins = nc.vector.tensor_scalar(
                            normed[par][t][:], x[:, bass.ds(tile, 1), :].rearrange("p a c -> p (a c)"),
                            core.rstd[:, bass.ds(tile, 1)], core.shift[:, bass.ds(tile, 1)], ALU.mult, ALU.add)
                    ins.then_inc(normed_ready, 1)

                def low(b, par):
                    dve.wait_ge(high_ready, b + 1)
                    nc.vector.tensor_tensor(columns(core.norm_t_low, b), bank[par][:].rearrange("p (k t) -> p k t", k=KT),
                                            columns(core.norm_t_high, b).bitcast(F32), ALU.subtract).then_inc(low_ready, 1)

                apply(0, 0)

                def pair(i, last=False):
                    apply(2 * i + 1, 1)
                    low(2 * i, 0)
                    if not last:
                        apply(2 * i + 2, 0)
                    low(2 * i + 1, 1)

                pair(0)
                with dve.Fori(1, PAIRS - 1) as i:
                    pair(i)
                pair(PAIRS - 1, last=True)

            @block.tensor
            def _(pe):
                def pair(i):
                    for par in range(2):
                        b = 2 * i + par
                        pe.wait_ge(normed_ready, b + 1)
                        need(pe, low_ready, b - 1)
                        for t in range(QT):
                            for k in range(KT):
                                ins = nc.tensor.transpose(bank[par][:, k * S + t * P:k * S + (t + 1) * P],
                                                          normed[par][t][:, k * P:(k + 1) * P], core.ident[:])
                        ins.then_inc(transposed, 1)

                pair(0)
                with pe.Fori(1, PAIRS) as i:
                    pair(i)

            @block.scalar
            def _(act):
                with act.Fori(0, PAIRS) as i:
                    for par in range(2):
                        b = 2 * i + par
                        act.wait_ge(transposed, b + 1)
                        nc.scalar.activation(columns(core.norm_t_high, b), bank[par][:].rearrange("p (k t) -> p k t", k=KT),
                                             ACT.Copy).then_inc(high_ready, 1)


class WideAttention:

    def __init__(self, heads, groups, shared_kv, rope, causal, scale):
        self.HG, self.G, self.rope, self.causal, self.scale = heads, groups, rope, causal, scale
        self.shared_kv, self.KV = shared_kv, 1 if shared_kv else heads
        widths = [2 * P, heads * P, self.KV * P, self.KV * P] if rope else [heads * P, P, P]
        scales = [1.0, scale, 1.0, 1.0] if rope else [scale, 1.0, 1.0]
        names = ["rope", "q", "k", "v"] if rope else ["q", "k", "v"]
        at, self.segment, self.parts = 0, {}, []
        for name, width, s in zip(names, widths, scales):
            self.segment[name] = (len(self.parts), at, width)
            self.parts.append((at, at + KT * width, s))
            at += KT * width
        self.wo_at, self.width = at, at + heads * C
        self.parts.append((at, self.width, 1.0))
        if rope:
            self.pieces = [("q", False, ["q"]), ("k", False, ["k"]), ("v", False, ["v"]), ("rope", True, ["rope"])]
            self.before = {0: [0], 1: [2]}
            self.after = {0: [1], 1: [3]}
        else:
            self.pieces = [("q", True, ["q"]), ("q2", True, ["q"]), ("kv", True, ["k", "v"])]
            self.before = {}
            self.after = {0: [0], 1: [1], 2: [2]}
        self.ahead = 1 if rope else 0
        self.sums = [i for i, p in enumerate(self.pieces) if p[1]]


def wide_attention_stage(core, cfg, w_in, consts_in):
    nc, x, bank = core.nc, core.x, core.bank
    norm_t = (core.norm_t_high, core.norm_t_low)
    HG, G, KV, rope, causal = cfg.HG, cfg.G, cfg.KV, cfg.rope, cfg.causal
    NP, NS, NW, AHEAD = len(cfg.pieces), len(cfg.sums), len(cfg.parts), cfg.ahead
    assert B % 2 == 0 and HG % 2 == 0
    p_bank, s_bank, t_bank, o_bank, y_bank = bank[0:2], bank[2:4], bank[4], bank[5], bank[6:8]
    NB = S + P if causal else QT * S

    with Stage(core) as st:
        staged = st.sb("staged", [P, cfg.width])
        w = [st.sb("w", [P, cfg.width], F32R) for _ in range(2)]
        z, q, k, v = (
            [[st.sb(name, shape, F32R) for _ in range(2)] for _ in range(2)]
            for name, shape in (("z", [P, KT, S]), ("q", [P, HG, S]), ("k", [P, KV, S]), ("v", [P, QT, KV * P])))
        if rope:
            tables = st.sb("tables", [P, 2, 2 * S])
            consts = [tables]
            turned = st.sb("turned", [P, 2, 2 * S])
            summed = [st.sb("summed", [P, 2 * S]) for _ in range(2)]
            halves = st.sb("halves", [P, 2, 2, S], F32R)
            rotated = [st.sb("rotated", [P, 2, 2, S], F32R) for _ in range(2)]
            moved = [st.sem("moved") for _ in range(2)]
            halves_high, halves_low = st.sem("halves_high"), st.sem("halves_low")
            MOVES = 8
        else:
            position = st.sb("position", [P, S])
            bias = st.sb("bias", [P, G, HG + 1])
            v_bias = st.sb("v_bias", [P, G, P])
            mask = st.sb("mask", [P, P])
            consts = [position, bias, v_bias, mask]
            scaled_position = st.sb("scaled_position", [P, S])
            scaled_bias = st.sb("scaled_bias", [P, G, HG])
            mask_bf = st.sb("mask_bf", [P, P], BF16)
            summed = [st.sb("summed", [P, 2 * S]) for _ in range(2)]
        probs = [st.sb("probs", [P, QT, S]) for _ in range(2)]
        probs_t = [[st.sb("probs_t", [P, NB], F32R) for _ in range(2)] for _ in range(2)]
        out_t = [[st.sb("out_t", [P, S], F32R) for _ in range(2)] for _ in range(2)]
        neg_max = [st.sb("neg_max", [P, QT]) for _ in range(2)]
        sums = [st.sb("sums", [P, QT]) for _ in range(2)]
        inv = [st.sb("inv", [P, QT]) for _ in range(2)]

        consts_loaded, consts_ready = st.sem("consts_loaded"), st.sem("consts_ready")
        w_loaded, w_high, w_low = st.sem("w_loaded"), st.sem("w_high"), st.sem("w_low")
        z_loaded = [st.sem("z_loaded") for _ in range(2)]
        piece_done, piece_read, piece_high = st.sem("piece_done"), st.sem("piece_read"), st.sem("piece_high")
        sum_ready, sum_low = st.sem("sum_ready"), st.sem("sum_low")
        scores_done, max_ready, probs_ready = st.sem("scores_done"), st.sem("max_ready"), st.sem("probs_ready")
        t_done, t_high, t_low = st.sem("t_done"), st.sem("t_high"), st.sem("t_low")
        o_done, o_high, o_low = st.sem("o_done"), st.sem("o_high"), st.sem("o_low")
        y_done, y_added, inv_ready = st.sem("y_done"), st.sem("y_added"), st.sem("inv_ready")

        class Unit:

            def __init__(self, g, i, parity, first=False, last=False):
                self.g, self.i, self.parity, self.first, self.last = g, i, parity, first, last
                self.b = 2 * i + parity
                self.n = g * B + self.b
                self.opens = isinstance(i, int) and i == 0 and parity == 0
                self.closes = isinstance(i, int) and i == PAIRS - 1 and parity == 1
                self.in_last_group = isinstance(g, int) and g == G - 1

            def next(self):
                if self.closes:
                    return Unit(self.g + 1, 0, 0)
                return Unit(self.g, self.i, 1) if self.parity == 0 else Unit(self.g, self.i + 1, 0)

            def before(self):
                if self.opens:
                    return Unit(self.g - 1, PAIRS - 1, 1)
                return Unit(self.g, self.i, 0) if self.parity == 1 else Unit(self.g, self.i - 1, 1)

            def slot(self, j):
                return self.n * HG + j

        def over_units(eng, work):
            def group(g, first=False, last=False):
                work(Unit(g, 0, 0, first=first))
                work(Unit(g, 0, 1))
                with eng.Fori(1, PAIRS - 1) as i:
                    work(Unit(g, i, 0))
                    work(Unit(g, i, 1))
                work(Unit(g, PAIRS - 1, 0))
                work(Unit(g, PAIRS - 1, 1, last=last))
            group(0, first=True)
            with eng.Fori(1, G - 1) as g:
                group(g)
            group(G - 1, last=True)

        def next_slot(u, j):
            return (u, j + 1) if j + 1 < HG else (u.next(), 0)

        def slot_before(u, j):
            return (u, j - 1) if j else (u.before(), HG - 1)

        def over_slots(eng, piece, value, transposed, score, output, slot_start=None, later_pieces_last=False,
                       finish=None):
            if rope:
                piece(Unit(-1, PAIRS - 1, 1), NP - 1)
                if finish:
                    finish(Unit(0, 0, 0))
            for i in range(NP):
                piece(Unit(0, 0, 0), i)
            score(Unit(0, 0, 0), 0)

            def work(u):
                for j in range(HG):
                    if slot_start:
                        slot_start(u, j)
                    if finish and j == 0 and not u.last:
                        finish(u.next())
                    if not u.last:
                        for i in cfg.before.get(j, []):
                            piece(u.next(), i)
                    if not (u.first and j == 0):
                        value(*slot_before(u, j))
                    if later_pieces_last:
                        transposed(u, j)
                    if not u.last:
                        for i in cfg.after.get(j, []):
                            if not (cfg.pieces[i][0] == "rope" and u.next().closes and u.in_last_group):
                                piece(u.next(), i)
                    if not later_pieces_last:
                        transposed(u, j)
                    if not (u.last and j == HG - 1):
                        score(*next_slot(u, j))
                    if not (u.first and j == 0):
                        output(*slot_before(u, j))

            over_units(eng, work)
            end = Unit(G - 1, PAIRS - 1, 1)
            value(end, HG - 1)
            output(end, HG - 1)

        def piece_number(u, i):
            return u.n * NP + i + 1 + AHEAD

        def piece_bank(u, i):
            return p_bank[(u.parity * NP + i) % 2]

        def sum_number(u, i):
            s = cfg.sums.index(i)
            if rope:
                u = u.next()
            return u.n * NS + s, summed[(u.parity * NS + s) % 2]

        def destination(u, i, part):
            name = cfg.pieces[i][0]
            if name == "q":
                return [(q[u.parity][part][:, 0:2, :], slice(0, 2 * S))]
            if name == "q2":
                return [(q[u.parity][part][:, 2:4, :], slice(0, 2 * S))]
            if name == "k":
                return [(k[u.parity][part][:, 0:2, :], slice(0, 2 * S))]
            if name == "v":
                return [(v[u.parity][part][:], slice(0, 2 * S))]
            return [(k[u.parity][part][:, 0, :], slice(0, S)), (v[u.parity][part][:], slice(S, 2 * S))]

        def shaped(source, target):
            return source.rearrange("p (a c) -> p a c", a=target.shape[1]) if len(target.shape) == 3 else source

        def wait_destination_free(eng, u, i):
            need(eng, scores_done, (u.n - 1) * HG)
            if "v" in cfg.pieces[i][2]:
                need(eng, o_done, (u.n - 1) * HG)

        def wait_moved(eng, u):
            if isinstance(u.n, int) and u.n < 0:
                return
            eng.wait_ge(moved[u.parity], (u.g * PAIRS + u.i + 1) * MOVES * 16)

        def wait_weights_free(eng, g, part):
            if rope and part == 0:
                need(eng, piece_done, (g * B - 1) * NP + AHEAD)
            elif part < NW - 1:
                need(eng, piece_done, g * B * NP)
            else:
                need(eng, y_done, g * B * HG)

        def split_parts_at(u, j):
            if rope and u.next().closes and not u.in_last_group and j == 0:
                return u.g + 1, [0]
            if u.closes and not u.last and j == 0:
                return u.g + 1, range(1 if rope else 0, NW - 1)
            if u.opens and not u.first and j == 1:
                return u.g, [NW - 1]
            return None, []

        with nc.Block() as block:

            @block.sync
            def _(sp):
                for t, source in zip(consts, consts_in):
                    sp.dma_start(t[:], source).then_inc(consts_loaded, 16)
                sp.dma_start(staged[:], w_in[0]).then_inc(w_loaded, 16)

                def load_z(u):
                    need(sp, piece_done, (u.n - 1) * NP)
                    for part, source in enumerate((core.norm_t_high, core.norm_t_low)):
                        sp.dma_start(z[u.parity][part][:].bitcast(F32), source[:, :, bass.ds(u.b * S, S)].bitcast(F32))\
                            .then_inc(z_loaded[u.parity], 16)

                def move(u):
                    sp.wait_ge(halves_low, u.n + 1)
                    for half in range(2):
                        for side in range(2):
                            for head in range(2):
                                at, to = (side * 2 + head) * 32, (head * 2 + half) * 32
                                sp.dma_start(rotated[u.parity][to:to + 32, side, :, :].bitcast(F32),
                                             halves[at:at + 32, half, :, :].bitcast(F32)).then_inc(moved[u.parity], 16)

                load_z(Unit(0, 0, 0))
                if rope:
                    move(Unit(0, 0, 0))

                def work(u):
                    if not u.last:
                        load_z(u.next())
                        if rope:
                            move(u.next())
                    if u.opens and not (isinstance(u.g, int) and u.g == G - 1):
                        sp.wait_ge(w_low, (u.g + 1) * NW)
                        sp.dma_start(staged[:], w_in[bass.ds(u.g + 1, 1)].rearrange("a p n -> p (a n)"))\
                            .then_inc(w_loaded, 16)

                over_units(sp, work)

            @block.tensor
            def _(pe):
                pe.wait_ge(consts_ready, 1)

                def weights(part, name, kt, first, width):
                    _, at, whole = cfg.segment[name]
                    at += kt * whole + first
                    return w[part][:, at:at + width]

                def group_of_passes(out, operands):
                    n = len(operands)
                    for kt, (stationary, moving) in enumerate(operands):
                        for m, (a, c) in enumerate(((0, 0), (0, 1), (1, 0))):
                            ins = nc.tensor.matmul(out, stationary(a), moving(c), start=(kt == 0 and m == 0),
                                                   stop=(kt == n - 1 and m == 2))
                    return ins

                def piece(u, i):
                    name, _, segments = cfg.pieces[i]
                    p = piece_bank(u, i)
                    need(pe, piece_read, piece_number(u, i) - 2)
                    if name == "rope":
                        u = u.next()
                    if "v" in segments:
                        pe.wait_ge(z_loaded[u.parity], (u.g * PAIRS + u.i + 1) * 32)
                    if u.opens:
                        for s in segments:
                            pe.wait_ge(w_low, u.g * NW + cfg.segment[s][0] + 1)
                    zz = z[u.parity]
                    if name != "v":
                        s = segments[0]
                        for c in range(1 if name == "kv" else 2):
                            first = (c + (2 if name == "q2" else 0)) * P
                            ins = group_of_passes(p[:, c * S:(c + 1) * S], [
                                (lambda a, kt=kt: weights(a, s, kt, first, P), lambda c_, kt=kt: norm_t[c_][:, kt, bass.ds(u.b * S, S)])
                                for kt in range(KT)])
                    if "v" in segments:
                        at = S if name == "kv" else 0
                        for t in range(QT):
                            ins = group_of_passes(p[:, at + t * KV * P:at + (t + 1) * KV * P], [
                                (lambda a, kt=kt: zz[a][:, kt, t * P:(t + 1) * P],
                                 lambda c_, kt=kt: weights(c_, "v", kt, 0, KV * P)) for kt in range(KT)])
                    ins.then_inc(piece_done, 1)

                def score(u, j):
                    if j == 0:
                        if rope:
                            pe.wait_ge(piece_read, piece_number(u, 1))
                            wait_moved(pe, u)
                        else:
                            pe.wait_ge(sum_low, (u.n + 1) * NS)
                    need(pe, probs_ready, u.slot(j) - 1)
                    s = s_bank[j % 2]
                    qq, kk, kj = q[u.parity], k[u.parity], 0 if cfg.shared_kv else j
                    for t in range(QT):
                        width = P if causal and t == 0 else S
                        operands = [(qq[a][:, j, t * P:(t + 1) * P], kk[c][:, kj, 0:width])
                                    for a, c in ((0, 0), (0, 1), (1, 0))]
                        if rope:
                            rows = slice(64 * j, 64 * j + 64)
                            r = rotated[u.parity]
                            operands += [(r[rows, 0, a, t * P:(t + 1) * P], r[rows, 1, c, 0:width])
                                         for a, c in ((0, 0), (0, 1), (1, 0))]
                        for n, (a, c) in enumerate(operands):
                            ins = nc.tensor.matmul(s[:, t * S:t * S + width], a, c, start=(n == 0),
                                                   stop=(n == len(operands) - 1 and not causal))
                        if causal:
                            at = t * (S + P)
                            ins = nc.tensor.matmul(s[:, at:at + P], core.ident_bf[:], mask_bf[:], start=False, stop=True)
                    ins.then_inc(scores_done, 1)

                def transposed(u, j):
                    pe.wait_ge(probs_ready, u.slot(j) + 1)
                    need(pe, t_low, u.slot(j))
                    for kt in range(QT):
                        for t in range(kt if causal else 0, QT):
                            at = kt * S + t * P - (P if causal and kt else 0)
                            ins = nc.tensor.transpose(t_bank[:, at:at + P], probs[j % 2][:, t, kt * P:(kt + 1) * P],
                                                      core.ident[:])
                    ins.then_inc(t_done, 1)

                def value(u, j):
                    m = u.slot(j)
                    pe.wait_ge(t_low, m + 1)
                    need(pe, o_low, m)
                    if j == 0 and rope:
                        pe.wait_ge(piece_read, piece_number(u, 2))
                    jv, vv, pp = 0 if cfg.shared_kv else j, v[u.parity], probs_t[j % 2]
                    for kt in range(QT):
                        to = slice(P, S) if causal and kt else slice(0, S)
                        of = slice(kt * S, NB if kt else S)
                        for n, (a, c) in enumerate(((0, 0), (0, 1), (1, 0))):
                            ins = nc.tensor.matmul(o_bank[:, to], vv[a][:, kt, jv * P:(jv + 1) * P], pp[c][:, of],
                                                   start=(kt == 0 and n == 0), stop=(kt == QT - 1 and n == 2))
                    ins.then_inc(o_done, 1)

                def output(u, j):
                    m = u.slot(j)
                    pe.wait_ge(o_low, m + 1)
                    need(pe, y_added, m - 1)
                    if u.opens:
                        pe.wait_ge(w_low, (u.g + 1) * NW)
                    for t in range(QT):
                        ins = group_of_passes(y_bank[j % 2][:, t * C:(t + 1) * C], [
                            (lambda a: out_t[j % 2][a][:, t * P:(t + 1) * P],
                             lambda c: w[c][:, cfg.wo_at + j * C:cfg.wo_at + (j + 1) * C])])
                    ins.then_inc(y_done, 1)

                over_slots(pe, piece, value, transposed, score, output)

            @block.scalar
            def _(act):
                def split_high(g, parts):
                    for part in parts:
                        first, end, scale = cfg.parts[part]
                        act.wait_ge(w_loaded, (g + 1) * 16)
                        wait_weights_free(act, g, part)
                        nc.scalar.activation(w[0][:, first:end], staged[:, first:end], ACT.Copy, scale=float(scale))\
                            .then_inc(w_high, 1)

                split_high(0, range(NW))

                def slot_start(u, j):
                    split_high(*split_parts_at(u, j))

                def piece(u, i):
                    if cfg.pieces[i][0] == "rope":
                        return
                    wait_destination_free(act, u, i)
                    if cfg.pieces[i][1]:
                        number, source = sum_number(u, i)
                        act.wait_ge(piece_read, piece_number(u, i))
                    else:
                        source = piece_bank(u, i)
                        act.wait_ge(piece_done, piece_number(u, i))
                    for target, columns in destination(u, i, 0):
                        ins = nc.scalar.activation(target, shaped(source[:, columns], target), ACT.Copy)
                    ins.then_inc(piece_high, 1)

                def finish(u):
                    wait_moved(act, u.before())
                    act.wait_ge(sum_ready, u.n + 1)
                    nc.scalar.activation(halves[:, :, 0, :], summed[u.parity][:].rearrange("p (h c) -> p h c", h=2), ACT.Copy)\
                        .then_inc(halves_high, 1)

                def score(u, j):
                    m = u.slot(j)
                    act.wait_ge(max_ready, m + 1)
                    need(act, t_done, m - 1)
                    need(act, inv_ready, m - 1)
                    for t in range(QT):
                        width = P if causal and t == 0 else S
                        ins = nc.scalar.activation(probs[j % 2][:, t, 0:width], s_bank[j % 2][:, t * S:t * S + width],
                                                   ACT.Exp, bias=neg_max[j % 2][:, t:t + 1],
                                                   accum_out=sums[j % 2][:, t:t + 1])
                    ins.then_inc(probs_ready, 1)

                def transposed(u, j):
                    act.wait_ge(t_done, u.slot(j) + 1)
                    need(act, o_done, u.slot(j) - 1)
                    nc.scalar.activation(probs_t[j % 2][0][:], t_bank[:, 0:NB], ACT.Copy).then_inc(t_high, 1)

                def value(u, j):
                    act.wait_ge(o_done, u.slot(j) + 1)
                    need(act, y_done, u.slot(j) - 1)
                    nc.scalar.activation(out_t[j % 2][0][:], o_bank[:, 0:S], ACT.Copy).then_inc(o_high, 1)

                over_slots(act, piece, value, transposed, score, lambda u, j: None, slot_start=slot_start,
                           later_pieces_last=True, finish=finish if rope else None)

            @block.vector
            def _(dve):
                dve.wait_ge(consts_loaded, 16 * len(consts))
                if rope:
                    nc.vector.memset(sums[0][:], 0.0).then_inc(consts_ready, 1)
                else:
                    nc.vector.tensor_copy(mask_bf[:], mask[:])
                    nc.vector.tensor_scalar(scaled_position[:], position[:], float(cfg.scale), None, ALU.mult)
                    nc.vector.tensor_scalar(scaled_bias[:], bias[:, :, 0:HG], float(cfg.scale), None, ALU.mult)\
                        .then_inc(consts_ready, 1)
                dve.wait_ge(consts_ready, 1)

                def split_low(g, parts):
                    for part in parts:
                        first, end, scale = cfg.parts[part]
                        dve.wait_ge(w_high, g * NW + part + 1)
                        nc.vector.scalar_tensor_tensor(w[1][:, first:end], staged[:, first:end], float(scale),
                                                       w[0][:, first:end].bitcast(F32), ALU.mult, ALU.subtract)\
                            .then_inc(w_low, 1)

                split_low(0, range(NW))

                def slot_start(u, j):
                    split_low(*split_parts_at(u, j))

                def piece(u, i):
                    name, through_sum, _ = cfg.pieces[i]
                    p = piece_bank(u, i)
                    if not through_sum:
                        dve.wait_ge(piece_high, u.n * (NP - AHEAD) + i + 1)
                        (target, columns), (high, _) = destination(u, i, 1)[0], destination(u, i, 0)[0]
                        nc.vector.tensor_tensor(target, shaped(p[:, columns], target), high.bitcast(F32), ALU.subtract)\
                            .then_inc(piece_read, 1)
                        return
                    dve.wait_ge(piece_done, piece_number(u, i))
                    number, target = sum_number(u, i)
                    if rope:
                        need(dve, sum_ready, number)
                        for half in range(2):
                            ins = nc.vector.tensor_tensor(turned[:, half, :], p[:], tables[:, half, :], ALU.mult)
                        ins.then_inc(piece_read, 1)
                        return
                    need(dve, sum_low, number - 1)
                    for c in range(1 if name == "kv" else 2):
                        head = c + (2 if name == "q2" else 0)
                        b_ap = bias[:, bass.ds(u.g, 1), HG:HG + 1] if name == "kv" else scaled_bias[:, bass.ds(u.g, 1), head:head + 1]
                        ins = nc.vector.scalar_tensor_tensor(
                            target[:, c * S:(c + 1) * S], p[:, c * S:(c + 1) * S], b_ap.rearrange("p a c -> p (a c)"),
                            (position if name == "kv" else scaled_position)[:], ALU.add, ALU.add)
                    if name == "kv":
                        b_ap = v_bias[:, bass.ds(u.g, 1), :].to_broadcast([P, QT, P])
                        ins = nc.vector.tensor_tensor(target[:, S:2 * S].rearrange("p (a c) -> p a c", a=QT),
                                                      p[:, S:2 * S].rearrange("p (a c) -> p a c", a=QT), b_ap, ALU.add)
                    ins.then_inc(piece_read, 1)

                def score(u, j):
                    m = u.slot(j)
                    dve.wait_ge(scores_done, m + 1)
                    need(dve, probs_ready, m - 1)
                    s = s_bank[j % 2][:].rearrange("p (a c) -> p a c", a=QT)
                    if causal:
                        nc.vector.tensor_reduce(neg_max[j % 2][:, 0:1], s[:, 0, 0:P], AX.X, ALU.max, negate=True)
                        ins = nc.vector.tensor_reduce(neg_max[j % 2][:, 1:2], s[:, 1, :], AX.X, ALU.max, negate=True)
                    else:
                        ins = nc.vector.tensor_reduce(neg_max[j % 2][:], s, AX.X, ALU.max, negate=True)
                    ins.then_inc(max_ready, 1)

                def transposed(u, j):
                    dve.wait_ge(t_high, u.slot(j) + 1)
                    nc.vector.tensor_tensor(probs_t[j % 2][1][:], t_bank[:, 0:NB], probs_t[j % 2][0][:].bitcast(F32),
                                            ALU.subtract).then_inc(t_low, 1)

                def value(u, j):
                    dve.wait_ge(o_high, u.slot(j) + 1)
                    nc.vector.tensor_tensor(out_t[j % 2][1][:], o_bank[:, 0:S], out_t[j % 2][0][:].bitcast(F32),
                                            ALU.subtract).then_inc(o_low, 1)

                def output(u, j):
                    m = u.slot(j)
                    dve.wait_ge(probs_ready, m + 1)
                    need(dve, y_added, m - 1)
                    nc.vector.reciprocal(inv[j % 2][:], sums[j % 2][:]).then_inc(inv_ready, 1)
                    dve.wait_ge(inv_ready, m + 1)
                    dve.wait_ge(y_done, m + 1)
                    need(dve, y_added, m)
                    for t in range(QT):
                        tile = x[:, bass.ds(u.b * QT + t, 1), :].rearrange("p a c -> p (a c)")
                        ins = nc.vector.scalar_tensor_tensor(tile, y_bank[j % 2][:, t * C:(t + 1) * C],
                                                             inv[j % 2][:, t:t + 1], tile, ALU.mult, ALU.add)
                    ins.then_inc(y_added, 1)

                def finish(u):
                    dve.wait_ge(halves_high, u.n + 1)
                    nc.vector.tensor_tensor(halves[:, :, 1, :], summed[u.parity][:].rearrange("p (h c) -> p h c", h=2),
                                            halves[:, :, 0, :].bitcast(F32), ALU.subtract).then_inc(halves_low, 1)

                over_slots(dve, piece, value, transposed, score, output, slot_start=slot_start,
                           finish=finish if rope else None)

            @block.gpsimd
            def _(pool):
                def piece(u, i):
                    if not cfg.pieces[i][1]:
                        return
                    number, total = sum_number(u, i)
                    if rope:
                        pool.wait_ge(piece_read, piece_number(u, i))
                        need(pool, halves_low, number - 1)
                        nc.gpsimd.tensor_tensor(total[:].rearrange("p (h c) -> p h c", h=2), turned[:, :, 0:S],
                                                turned[:, :, S:2 * S], ALU.add).then_inc(sum_ready, 1)
                        return
                    pool.wait_ge(piece_high, u.n * NP + i + 1)
                    wait_destination_free(pool, u, i)
                    for (target, columns), (high, _) in zip(destination(u, i, 1), destination(u, i, 0)):
                        ins = nc.gpsimd.tensor_tensor(target, shaped(total[:, columns], target), high.bitcast(F32), ALU.subtract)
                    ins.then_inc(sum_low, 1)

                none = lambda *a: None
                over_slots(pool, piece, none, none, none, none)


class NarrowAttention:

    def __init__(self, heads, causal):
        self.H, self.causal = heads, causal
        self.D = C // heads
        self.rows = 4 * self.D
        self.per_tile = P // self.rows
        self.stacks = heads // self.per_tile
        self.scale = (1 if causal else -1) / math.sqrt(self.D)
        pairs = [(kind, i) for i in range(self.stacks // 2) for kind in ("q_stack", "k_stack")]
        self.steps = [("q", 0), ("k", 0), ("v", 0)] + pairs
        spaces = list(range(5, heads - 3))
        self.at = {}
        for n, step in enumerate(self.steps):
            self.at.setdefault(spaces[n * len(spaces) // len(self.steps)], []).append(n)


def narrow_attention_stage(core, cfg, w_in, select_in, consts_in):
    nc, x, bank = core.nc, core.x, core.bank
    H, D, causal, NSTEP = cfg.H, cfg.D, cfg.causal, len(cfg.steps)
    p_bank, s_bank, t_bank, o_bank = bank[0:2], bank[2:4], bank[4:6], bank[6:8]
    NB = S + P if causal else QT * S
    W = KT * C
    RELATIVE = S + P

    by_act = [(h % 2 == 0) for h in range(H)] if not causal else [(h % 2 == 0) for h in range(H)]
    before_act = [sum(by_act[:h]) for h in range(H + 1)]

    with Stage(core) as st:
        staged = st.sb("staged", [P, 4 * W])
        w = [st.sb("w", [P, 4 * W], F32R) for _ in range(2)]
        select_staged = st.sb("select_staged", [P, 2, 4, 2, P])
        select = st.sb("select", [P, 2, 4, 2, P], F32R)
        z = [[st.sb("z", [P, KT, S], F32R) for _ in range(2)] for _ in range(2)]
        qk = [[st.sb("qk", [P, KT, S], F32R) for _ in range(2)] for _ in range(2)]
        stack = [[st.sb("stack", [P, cfg.stacks, S], F32R) for _ in range(2)] for _ in range(2)]
        values = [st.sb("values", [P, QT, H, D + 1]) for _ in range(2)]
        probs = [st.sb("probs", [P, QT, S]) for _ in range(2)]
        probs_t = [st.sb("probs_t", [P, NB]) for _ in range(2)]
        bound = [st.sb("bound", [P, QT]) for _ in range(2)]
        inv = st.sb("inv", [P, QT, H])
        out = st.sb("out", [P, QT, C])
        out_t = [st.sb("out_t", [P, KT, S], F32R) for _ in range(2)]
        if causal:
            mask, bias_row = st.sb("mask", [P, P]), st.sb("bias_row", [1, C])
            mask_bf, ones_row = st.sb("mask_bf", [P, P], BF16), st.sb("ones_row", [1, P])
            consts = [mask, bias_row]
        else:
            table = st.sb("table", [P, RELATIVE, D])
            neg_bias = st.sb("neg_bias", [P, RELATIVE])
            neg_scores = [st.sb("neg_scores", [P, QT, S]) for _ in range(2)]
            carrier = [st.sb("carrier", [1, 1]) for _ in range(2)]
            consts = [table]

        consts_loaded, w_loaded, z_loaded = st.sem("consts_loaded"), st.sem("w_loaded"), [st.sem("z_loaded") for _ in range(2)]
        w_high, w_low, select_ready = st.sem("w_high"), st.sem("w_low"), st.sem("select_ready")
        consts_step, consts_ready = st.sem("consts_step"), st.sem("consts_ready")
        step_done, step_high, step_read = st.sem("step_done"), st.sem("step_high"), st.sem("step_read")
        scores_done, bound_ready, probs_ready = st.sem("scores_done"), st.sem("bound_ready"), st.sem("probs_ready")
        t_done, t_by_act, t_by_dve = st.sem("t_done"), st.sem("t_by_act"), st.sem("t_by_dve")
        o_done, inv_ready, out_ready = st.sem("o_done"), st.sem("inv_ready"), st.sem("out_ready")
        out_t_done, out_t_high, out_t_low = st.sem("out_t_done"), st.sem("out_t_high"), st.sem("out_t_low")
        y_done, y_added = st.sem("y_done"), st.sem("y_added")

        OUT_T_SLOT, Y_SLOT = 3, 4

        class Batch:

            def __init__(self, i, parity, first=False, last=False):
                self.i, self.parity, self.first, self.last = i, parity, first, last
                self.b = 2 * i + parity

            def next(self):
                return Batch(self.i, 1) if self.parity == 0 else Batch(self.i + 1, 0)

            def before(self):
                return Batch(self.i, 0) if self.parity == 1 else Batch(self.i - 1, 1)

            def slot(self, h):
                return self.b * H + h

        def over_batches(eng, work):
            work(Batch(0, 0, first=True))
            work(Batch(0, 1))
            with eng.Fori(1, PAIRS - 1) as i:
                work(Batch(i, 0))
                work(Batch(i, 1))
            work(Batch(PAIRS - 1, 0))
            work(Batch(PAIRS - 1, 1, last=True))

        def over_slots(eng, step, transposed, score, value, finish, transpose_out, project_out):
            start = Batch(0, 0)
            for n in range(NSTEP):
                step(start, n)
            score(start, 0)
            score(start, 1)

            def work(u):
                for h in range(H):
                    transposed(u, h)
                    if not (u.last and h >= H - 2):
                        score(*((u, h + 2) if h < H - 2 else (u.next(), h + 2 - H)))
                    if not u.last:
                        for n in cfg.at.get(h, []):
                            step(u.next(), n)
                    if h or not u.first:
                        value(*((u, h - 1) if h else (u.before(), H - 1)))
                    if not u.first:
                        if h == 0:
                            finish(u.before())
                        if h == OUT_T_SLOT:
                            transpose_out(u.before())
                        if h == Y_SLOT:
                            project_out(u.before())

            over_batches(eng, work)
            end = Batch(PAIRS - 1, 1)
            value(end, H - 1)
            finish(end)
            transpose_out(end)
            project_out(end)

        def wait_t_copied(eng, u, h):
            if by_act[h]:
                eng.wait_ge(t_by_act, u.b * before_act[H] + before_act[h] + 1)
            else:
                eng.wait_ge(t_by_dve, u.b * (H - before_act[H]) + h - before_act[h] + 1)

        def head_two_before(u, h):
            if h >= 2:
                return u, h - 2
            return None if u.first else (u.before(), H + h - 2)

        with nc.Block() as block:

            @block.sync
            def _(sp):
                sp.dma_start(staged[:], w_in).then_inc(w_loaded, 16)
                sp.dma_start(select_staged[:], select_in).then_inc(w_loaded, 16)

                def load_z(u):
                    need(sp, step_done, (u.b - 2) * NSTEP + 3)
                    for part, source in enumerate((core.norm_t_high, core.norm_t_low)):
                        sp.dma_start(z[u.parity][part][:].bitcast(F32), source[:, :, bass.ds(u.b * S, S)].bitcast(F32))\
                            .then_inc(z_loaded[u.parity], 16)

                load_z(Batch(0, 0))
                for t, source in zip(consts, consts_in):
                    sp.dma_start(t[:], source).then_inc(consts_loaded, 16)
                over_batches(sp, lambda u: None if u.last else load_z(u.next()))
                if len(consts) == 1:
                    sp.wait_ge(consts_loaded, 16)

            @block.tensor
            def _(pe):
                def three_passes(out, operands, close=True):
                    n = len(operands)
                    for kt, (stationary, moving) in enumerate(operands):
                        for m, (a, c) in enumerate(((0, 0), (0, 1), (1, 0))):
                            ins = nc.tensor.matmul(out, stationary(a), moving(c), start=(kt == 0 and m == 0),
                                                   stop=(close and kt == n - 1 and m == 2))
                    return ins

                pe.wait_ge(w_low, 2)
                pe.wait_ge(select_ready, 1)
                pe.wait_ge(consts_ready, 1)

                def step(u, n):
                    kind, i = cfg.steps[n]
                    need(pe, step_read, u.b * NSTEP + max(n - 1, 0))
                    if n < 2:
                        need(pe, (out_t_low, y_added)[n], u.b - 1)
                    p, zz = p_bank[n % 2], z[u.parity]
                    if n == 0:
                        pe.wait_ge(z_loaded[u.parity], (u.i + 1) * 32)
                    if kind in ("q", "k"):
                        at = 0 if kind == "q" else W
                        for c in range(KT):
                            ins = three_passes(p[:, c * S:(c + 1) * S], [
                                (lambda a, kt=kt: w[a][:, at + kt * C + c * P:at + kt * C + (c + 1) * P],
                                 lambda c_, kt=kt: zz[c_][:, kt, :]) for kt in range(KT)])
                    elif kind == "v":
                        for t in range(QT):
                            ins = three_passes(p[:, t * C:(t + 1) * C], [
                                (lambda a, kt=kt: zz[a][:, kt, t * P:(t + 1) * P],
                                 lambda c_, kt=kt: w[c_][:, 2 * W + kt * C:2 * W + (kt + 1) * C]) for kt in range(KT)])
                    else:
                        which = 0 if kind == "q_stack" else 1
                        pe.wait_ge(step_read, u.b * NSTEP + which + 1)
                        for c in range(2):
                            tile = 2 * i + c
                            for part in range(2):
                                ins = nc.tensor.matmul(p[:, c * S:(c + 1) * S], select[:, which, tile % 4, part, :],
                                                       qk[which][part][:, tile // 4, :], start=(part == 0), stop=(part == 1))
                    ins.then_inc(step_done, 1)

                def score(u, h):
                    m = u.slot(h)
                    tile, row = h // cfg.per_tile, (h % cfg.per_tile) * cfg.rows
                    if tile % 2 == 0 and row == 0:
                        pe.wait_ge(step_read, u.b * NSTEP + cfg.steps.index(("k_stack", tile // 2)) + 1)
                    need(pe, probs_ready, m - 1)
                    rows = slice(row, row + cfg.rows)
                    qs, ks = stack[0][u.parity], stack[1][u.parity]
                    for t in range(QT):
                        width = P if causal and t == 0 else S
                        ins = nc.tensor.matmul(s_bank[h % 2][:, t * S:t * S + width], qs[rows, tile, t * P:(t + 1) * P],
                                               ks[rows, tile, 0:width], start=True, stop=not causal)
                        if causal:
                            at = t * (S + P)
                            ins = nc.tensor.matmul(s_bank[h % 2][:, at:at + P], core.ident_bf[:], mask_bf[:],
                                                   start=False, stop=True)
                    ins.then_inc(scores_done, 1)

                def transposed(u, h):
                    pe.wait_ge(probs_ready, u.slot(h) + 1)
                    if head_two_before(u, h):
                        wait_t_copied(pe, *head_two_before(u, h))
                    for kt in range(QT):
                        for t in range(kt if causal else 0, QT):
                            at = kt * S + t * P - (P if causal and kt else 0)
                            ins = nc.tensor.transpose(t_bank[h % 2][:, at:at + P], probs[h % 2][:, t, kt * P:(kt + 1) * P],
                                                      core.ident[:])
                    ins.then_inc(t_done, 1)

                def value(u, h):
                    wait_t_copied(pe, u, h)
                    if h == 0:
                        need(pe, out_ready, u.b)
                        pe.wait_ge(step_read, u.b * NSTEP + 3)
                    for t in range(QT):
                        kts = range(t + 1 if causal else QT)
                        for kt in kts:
                            at = kt * S + t * P - (P if causal and kt else 0)
                            ins = nc.tensor.matmul(o_bank[t][:, h * (D + 1):(h + 1) * (D + 1)], probs_t[h % 2][:, at:at + P],
                                                   values[u.parity][:, kt, h, :], start=(kt == 0), stop=(kt == kts[-1]))
                    ins.then_inc(o_done, 1)

                def transpose_out(u):
                    pe.wait_ge(out_ready, u.b + 1)
                    ends = isinstance(u.i, int) and u.b == B - 1
                    pe.wait_ge(step_read, (u.b + (1 if ends else 2)) * NSTEP)
                    for t in range(QT):
                        for kt in range(KT):
                            ins = nc.tensor.transpose(p_bank[0][:, kt * S + t * P:kt * S + (t + 1) * P],
                                                      out[:, t, kt * P:(kt + 1) * P], core.ident[:])
                    ins.then_inc(out_t_done, 1)

                def project_out(u):
                    pe.wait_ge(out_t_low, u.b + 1)
                    for t in range(QT):
                        to = p_bank[1][:, t * C:(t + 1) * C]
                        ins = three_passes(to, [
                            (lambda a, kt=kt: out_t[a][:, kt, t * P:(t + 1) * P],
                             lambda c_, kt=kt: w[c_][:, 3 * W + kt * C:3 * W + (kt + 1) * C]) for kt in range(KT)],
                            close=not causal)
                        if causal:
                            ins = nc.tensor.matmul(to, ones_row[:], bias_row[:], start=False, stop=True)
                    ins.then_inc(y_done, 1)

                over_slots(pe, step, transposed, score, value, lambda u: None, transpose_out, project_out)

            @block.scalar
            def _(act):
                act.wait_ge(w_loaded, 32)
                nc.scalar.activation(w[0][:, 0:W], staged[:, 0:W], ACT.Copy, scale=float(cfg.scale)).then_inc(w_high, 1)
                nc.scalar.activation(w[0][:, W:4 * W], staged[:, W:4 * W], ACT.Copy).then_inc(w_high, 1)
                nc.scalar.activation(select[:], select_staged[:], ACT.Copy).then_inc(select_ready, 1)

                def step(u, n):
                    kind, i = cfg.steps[n]
                    if n < 2:
                        act.wait_ge(step_done, u.b * NSTEP + n + 1)
                        need(act, step_done, u.b * NSTEP)
                        nc.scalar.activation(qk[n][0][:], p_bank[n][:].rearrange("p (k t) -> p k t", k=KT), ACT.Copy)\
                            .then_inc(step_high, 1)

                def score(u, h):
                    m = u.slot(h)
                    act.wait_ge(bound_ready, m + 1)
                    need(act, t_done, m - 1)
                    for t in range(QT):
                        width = P if causal and t == 0 else S
                        source = s_bank[h % 2][:, t * S:t * S + width] if causal else neg_scores[h % 2][:, t, :]
                        ins = nc.scalar.activation(probs[h % 2][:, t, 0:width], source, ACT.Exp,
                                                   bias=bound[h % 2][:, t:t + 1], scale=1.0 if causal else -1.0)
                    ins.then_inc(probs_ready, 1)

                def transposed(u, h):
                    if by_act[h]:
                        act.wait_ge(t_done, u.slot(h) + 1)
                        need(act, o_done, u.slot(h) - 1)
                        nc.scalar.activation(probs_t[h % 2][:], t_bank[h % 2][:, 0:NB], ACT.Copy).then_inc(t_by_act, 1)

                def transpose_out(u):
                    act.wait_ge(out_t_done, u.b + 1)
                    need(act, y_done, u.b)
                    nc.scalar.activation(out_t[0][:], p_bank[0][:].rearrange("p (k t) -> p k t", k=KT), ACT.Copy)\
                        .then_inc(out_t_high, 1)

                none = lambda *a: None
                over_slots(act, step, transposed, score, none, none, transpose_out, none)

            @block.vector
            def _(dve):
                for n, (first, end, scale) in enumerate(((0, W, cfg.scale), (W, 4 * W, 1.0))):
                    dve.wait_ge(w_high, n + 1)
                    nc.vector.scalar_tensor_tensor(w[1][:, first:end], staged[:, first:end], float(scale),
                                                   w[0][:, first:end].bitcast(F32), ALU.mult, ALU.subtract).then_inc(w_low, 1)
                for par in range(2):
                    ins = nc.vector.memset(values[par][:, :, :, D:D + 1], 1.0)
                ins.then_inc(consts_step, 1)
                dve.wait_ge(consts_loaded, 16 * len(consts))
                if causal:
                    nc.vector.memset(ones_row[:], 1.0)
                    nc.vector.tensor_copy(mask_bf[:], mask[:]).then_inc(consts_ready, 1)
                else:
                    nc.vector.tensor_reduce(neg_bias[:], table[:], AX.X, ALU.add, negate=True).then_inc(consts_step, 1)
                    dve.wait_ge(consts_step, 2)
                    nc.vector.tensor_scalar(neg_bias[:], neg_bias[:], 1.0 / D, None, ALU.mult).then_inc(consts_ready, 1)
                    dve.wait_ge(consts_ready, 1)

                def step(u, n):
                    kind, i = cfg.steps[n]
                    dve.wait_ge(step_done, u.b * NSTEP + n + 1)
                    p = p_bank[n % 2]
                    if kind in ("q", "k"):
                        dve.wait_ge(step_high, u.b * 2 + n + 1)
                        nc.vector.tensor_tensor(qk[n][1][:], p[:].rearrange("p (k t) -> p k t", k=KT),
                                                qk[n][0][:].bitcast(F32), ALU.subtract).then_inc(step_read, 1)
                    elif kind == "v":
                        need(dve, o_done, (u.b - 1) * H)
                        nc.vector.tensor_copy(values[u.parity][:, :, :, 0:D],
                                              p[:].rearrange("p (t h d) -> p t h d", t=QT, h=H)).then_inc(step_read, 1)
                    else:
                        need(dve, scores_done, (u.b - 1) * H)
                        target = stack[0 if kind == "q_stack" else 1][u.parity]
                        nc.vector.tensor_copy(target[:, 2 * i:2 * i + 2, :], p[:].rearrange("p (k t) -> p k t", k=2))\
                            .then_inc(step_read, 1)

                def score(u, h):
                    m = u.slot(h)
                    dve.wait_ge(scores_done, m + 1)
                    need(dve, probs_ready, m - 1)
                    if not causal:
                        nc.vector.memset(carrier[h % 2][:], 0.0)
                    for t in range(QT):
                        width = P if causal and t == 0 else S
                        s = s_bank[h % 2][:, t * S:t * S + width]
                        if causal:
                            ins = nc.vector.tensor_reduce(bound[h % 2][:, t:t + 1], s, AX.X, ALU.max, negate=True)
                        else:
                            at = P * (1 - t)
                            ins = nc.vector.tensor_tensor_reduce(
                                out=neg_scores[h % 2][:, t, :], in0=s, in1=neg_bias[:, at:at + S], scale=1.0, scalar=BIG,
                                op0=ALU.add, op1=ALU.min, accum_out=bound[h % 2][:, t:t + 1])
                    ins.then_inc(bound_ready, 1)

                def transposed(u, h):
                    if not by_act[h]:
                        dve.wait_ge(t_done, u.slot(h) + 1)
                        need(dve, o_done, u.slot(h) - 1)
                        nc.vector.tensor_copy(probs_t[h % 2][:], t_bank[h % 2][:, 0:NB]).then_inc(t_by_dve, 1)

                def finish(u):
                    dve.wait_ge(o_done, (u.b + 1) * H)
                    need(dve, out_ready, u.b)
                    for t in range(QT):
                        o = o_bank[t][:, 0:H * (D + 1)].rearrange("p (h d) -> p h d", h=H)
                        ins = nc.vector.reciprocal(inv[:, t, :], o[:, :, D])
                    ins.then_inc(inv_ready, 1)
                    dve.wait_ge(inv_ready, u.b + 1)
                    need(dve, out_t_done, u.b)
                    for t in range(QT):
                        o = o_bank[t][:, 0:H * (D + 1)].rearrange("p (h d) -> p h d", h=H)
                        ins = nc.vector.tensor_tensor(out[:, t, :].rearrange("p (h d) -> p h d", h=H), o[:, :, 0:D],
                                                      inv[:, t, :].rearrange("p (h a) -> p h a", a=1).to_broadcast([P, H, D]),
                                                      ALU.mult)
                    ins.then_inc(out_ready, 1)

                def transpose_out(u):
                    dve.wait_ge(out_t_high, u.b + 1)
                    nc.vector.tensor_tensor(out_t[1][:], p_bank[0][:].rearrange("p (k t) -> p k t", k=KT),
                                            out_t[0][:].bitcast(F32), ALU.subtract).then_inc(out_t_low, 1)

                def project_out(u):
                    dve.wait_ge(y_done, u.b + 1)
                    tiles = x[:, bass.ds(u.b * QT, QT), :]
                    nc.vector.tensor_tensor(tiles, p_bank[1][:].rearrange("p (t c) -> p t c", t=QT), tiles, ALU.add)\
                        .then_inc(y_added, 1)

                over_slots(dve, step, transposed, score, lambda u, h: None, finish, transpose_out, project_out)


class Experts:

    def __init__(self, experts, top, groups, gated, act, router, capacity=None):
        self.E, self.top, self.NG, self.gated, self.act = experts, top, groups, gated, act
        self.router, self.capacity = router, capacity
        self.up = (2 if gated else 1) * KT * P
        self.down_at = self.up
        self.pick_at = self.up + C
        self.width = self.pick_at + P


def route_stage(core, cfg, w_in, gates_t, consts_in):
    nc, bank, E = core.nc, core.bank, cfg.E
    FILL = 8 - cfg.top
    CHUNK = 512
    NC_ = TILES * P // CHUNK
    TC = CHUNK // P
    GROUPS_OF = 4 if cfg.router == "limited" else 0
    with Stage(core) as st:
        staged = st.sb("staged", [P, KT, E])
        w = [st.sb("w", [P, KT, E], F32R) for _ in range(2)]
        logits_t = [st.sb("logits_t", [E, CHUNK]) for _ in range(2)]
        logits = st.sb("logits", [P, TILES, E])
        scored = st.sb("scored", [P, TILES, E])
        padded = st.sb("padded", [P, TILES, E + FILL])
        replaced = st.sb("replaced", [P, TILES, E + FILL])
        best = st.sb("best", [P, TILES, 8])
        chosen = st.sb("chosen", [P, TILES, E])
        total, inv, tile_max = (st.sb(n, [P, TILES]) for n in ("total", "inv", "tile_max"))
        gates = st.sb("gates", [P, TILES, P])
        w_loaded, w_high, w_low = st.sem("w_loaded"), st.sem("w_high"), st.sem("w_low")
        t_done, t_copied = st.sem("t_done"), st.sem("t_copied")
        logits_done, logits_ready = st.sem("logits_done"), st.sem("logits_ready")
        scored_ready, chain, gates_ready = st.sem("scored_ready"), st.sem("chain"), st.sem("gates_ready")
        g_done, g_high, g_low = st.sem("g_done"), st.sem("g_high"), st.sem("g_low")
        shifted_ready = st.sem("shifted_ready")
        if cfg.capacity:
            before = st.sb("before", [P, P])
            before_bf, ones_bf = st.sb("before_bf", [P, P], BF16), st.sb("ones_bf", [P, P], BF16)
            chosen_bf, earlier_bf = st.sb("chosen_bf", [P, TILES, E], BF16), st.sb("earlier_bf", [P, TILES, E], BF16)
            chosen_ready, position_done = st.sem("chosen_ready"), st.sem("position_done")
        if GROUPS_OF:
            group_values = st.sb("group_values", [P, TILES, 8 + 6])
            group_replaced = st.sb("group_replaced", [P, TILES, 8 + 6])
            group_chosen = st.sb("group_chosen", [P, TILES, GROUPS_OF])

        with nc.Block() as block:

            @block.sync
            def _(sp):
                sp.dma_start(staged[:], w_in).then_inc(w_loaded, 16)
                if cfg.capacity:
                    sp.dma_start(before[:], consts_in[0]).then_inc(w_loaded, 16)

            @block.tensor
            def _(pe):
                pe.wait_ge(w_low, 1)

                def project(c, par):
                    need(pe, t_copied, c - 1)
                    n = 0
                    for kt in range(KT):
                        for a, m in ((0, 0), (0, 1), (1, 0)):
                            zz = (core.norm_t_high, core.norm_t_low)[m]
                            ins = nc.tensor.matmul(bank[par][0:E, :], w[a][:, kt, :], zz[:, kt, bass.ds(c * CHUNK, CHUNK)],
                                                   start=(n == 0), stop=(n == 5))
                            n += 1
                    ins.then_inc(t_done, 1)

                def back(c, par):
                    pe.wait_ge(t_copied, c + 1)
                    need(pe, logits_ready, c - 1)
                    for t in range(TC):
                        ins = nc.tensor.transpose(bank[2 + par][:, t * E:(t + 1) * E], logits_t[par][:, t * P:(t + 1) * P],
                                                  core.ident[0:E, 0:E])
                    ins.then_inc(logits_done, 1)

                for c in range(NC_):
                    project(c, c % 2)
                    back(c, c % 2)
                if cfg.capacity:
                    pe.wait_ge(chosen_ready, 1)
                    for t in range(TILES):
                        to = bank[4 + t // 8][:, (t % 8) * E:(t % 8 + 1) * E]
                        nc.tensor.matmul(to, before_bf[:], chosen_bf[:, t, :], start=True, stop=False)
                        ins = nc.tensor.matmul(to, ones_bf[:], earlier_bf[:, t, :], start=False, stop=True)
                    ins.then_inc(position_done, 1)
                pe.wait_ge(gates_ready, 1)
                for t in range(TILES):
                    b = t // 4
                    need(pe, g_low, b - 1)
                    ins = nc.tensor.transpose(bank[b % 2][:, (t % 4) * P:(t % 4 + 1) * P], gates[:, t, :], core.ident[:])
                    if t % 4 == 3:
                        ins.then_inc(g_done, 1)

            @block.scalar
            def _(act):
                act.wait_ge(w_loaded, 16 * (2 if cfg.capacity else 1))
                nc.scalar.activation(w[0][:], staged[:], ACT.Copy).then_inc(w_high, 1)
                for c in range(NC_):
                    act.wait_ge(t_done, c + 1)
                    need(act, logits_done, c - 1)
                    nc.scalar.activation(logits_t[c % 2][:], bank[c % 2][0:E, :], ACT.Copy).then_inc(t_copied, 1)
                if cfg.router == "softmax":
                    act.wait_ge(shifted_ready, 1)
                    nc.scalar.activation(scored[:], scored[:], ACT.Exp).then_inc(scored_ready, 1)
                else:
                    act.wait_ge(logits_ready, NC_)
                    nc.scalar.activation(scored[:], logits[:], ACT.Sigmoid).then_inc(scored_ready, 1)
                for b in range(TILES // 4):
                    act.wait_ge(g_done, b + 1)
                    nc.scalar.activation(gates_t[0][:, b * 512:(b + 1) * 512], bank[b % 2][:], ACT.Copy).then_inc(g_high, 1)

            @block.vector
            def _(dve):
                steps = [0]

                def after(ins):
                    steps[0] += 1
                    ins.then_inc(chain, 1)
                    dve.wait_ge(chain, steps[0])

                def spread(t, n):
                    return t.rearrange("p (t a) -> p t a", a=1).to_broadcast([P, TILES, n])

                def choose(values, without, chosen_of, n, k):
                    low = max(n, 8)
                    for t in range(TILES):
                        ins = nc.vector.max(best[:, t, :], values[:, t, 0:low])
                    after(ins)
                    after(nc.vector.tensor_copy(best[:, :, k:8], values[:, :, low:low + 8 - k]))
                    for t in range(TILES):
                        ins = nc.vector.match_replace(without[:, t, :], best[:, t, :], values[:, t, :], -BIG)
                    after(ins)
                    after(nc.vector.tensor_tensor(chosen_of[:], without[:, :, 0:n], values[:, :, 0:n], ALU.not_equal))

                dve.wait_ge(w_high, 1)
                nc.vector.tensor_tensor(w[1][:], staged[:], w[0][:].bitcast(F32), ALU.subtract).then_inc(w_low, 1)
                after(nc.vector.memset(gates[:], 0.0))
                nc.vector.memset(padded[:], BIG)
                if GROUPS_OF:
                    after(nc.vector.memset(group_values[:], BIG))
                    nc.vector.memset(group_values[:, :, GROUPS_OF:8], -BIG)
                after(nc.vector.memset(gates[:, :, E:E + 1], 1.0))
                for c in range(NC_):
                    dve.wait_ge(logits_done, c + 1)
                    nc.vector.tensor_copy(logits[:, c * TC:(c + 1) * TC, :],
                                          bank[2 + c % 2][:, 0:TC * E].rearrange("p (t e) -> p t e", t=TC)).then_inc(logits_ready, 1)
                dve.wait_ge(logits_ready, NC_)
                if cfg.router == "softmax":
                    after(nc.vector.tensor_reduce(tile_max[:], logits[:], AX.X, ALU.max))
                    nc.vector.tensor_tensor(scored[:], logits[:], spread(tile_max[:], E), ALU.subtract).then_inc(shifted_ready, 1)
                if GROUPS_OF:
                    after(nc.vector.tensor_reduce(group_values[:, :, 0:GROUPS_OF],
                                                  logits[:].rearrange("p t (g n) -> p t g n", g=GROUPS_OF), AX.X, ALU.max))
                    choose(group_values, group_replaced, group_chosen, GROUPS_OF, 2)
                    after(nc.vector.tensor_scalar(group_chosen[:], group_chosen[:], -MASKED, MASKED, ALU.mult, ALU.add))
                    after(nc.vector.tensor_tensor(
                        padded[:, :, 0:E].rearrange("p t (g n) -> p t g n", g=GROUPS_OF),
                        logits[:].rearrange("p t (g n) -> p t g n", g=GROUPS_OF),
                        group_chosen[:].rearrange("p t (g a) -> p t g a", a=1).to_broadcast([P, TILES, GROUPS_OF, E // GROUPS_OF]),
                        ALU.add))
                else:
                    after(nc.vector.tensor_copy(padded[:, :, 0:E], logits[:]))
                choose(padded, replaced, chosen, E, cfg.top)
                if cfg.capacity:
                    nc.vector.tensor_copy(before_bf[:], before[:])
                    nc.vector.memset(ones_bf[:], 1.0)
                    after(nc.vector.memset(earlier_bf[:, 0, :], 0.0))
                    after(nc.vector.tensor_copy(chosen_bf[:], chosen[:]))
                    for t in range(1, TILES):
                        ins = nc.vector.tensor_tensor(earlier_bf[:, t, :], earlier_bf[:, t - 1, :], chosen_bf[:, t - 1, :], ALU.add)
                        if t < TILES - 1:
                            after(ins)
                    ins.then_inc(chosen_ready, 1)
                dve.wait_ge(scored_ready, 1)
                if cfg.router == "softmax":
                    after(nc.vector.tensor_reduce(total[:], scored[:], AX.X, ALU.add))
                    after(nc.vector.tensor_tensor(chosen[:], chosen[:], scored[:], ALU.mult))
                else:
                    after(nc.vector.tensor_tensor(chosen[:], chosen[:], scored[:], ALU.mult))
                    after(nc.vector.tensor_reduce(total[:], chosen[:], AX.X, ALU.add))
                after(nc.vector.reciprocal(inv[:], total[:]))
                if cfg.capacity:
                    after(nc.vector.tensor_tensor(chosen[:], chosen[:], spread(inv[:], E), ALU.mult))
                    dve.wait_ge(position_done, 1)
                    for half in range(2):
                        rows = slice(8 * half, 8 * half + 8)
                        ins = nc.vector.scalar_tensor_tensor(
                            gates[:, rows, 0:E], bank[4 + half][:].rearrange("p (t e) -> p t e", e=E), float(cfg.capacity),
                            chosen[:, rows, :], ALU.is_lt, ALU.mult)
                    ins.then_inc(gates_ready, 1)
                else:
                    nc.vector.tensor_tensor(gates[:, :, 0:E], chosen[:], spread(inv[:], E), ALU.mult).then_inc(gates_ready, 1)
                for b in range(TILES // 4):
                    dve.wait_ge(g_high, b + 1)
                    at = slice(b * 512, (b + 1) * 512)
                    nc.vector.tensor_tensor(gates_t[1][:, at], bank[b % 2][:], gates_t[0][:, at].bitcast(F32), ALU.subtract)\
                        .then_inc(g_low, 1)


def experts_stage(core, cfg, w_in, gates_t):
    nc, x, bank, NG = core.nc, core.x, core.bank, cfg.NG
    HALF, STEP = TILES * P // 2, 512
    a_bank, up_bank, pick_bank, y_bank = bank[0:2], bank[2], bank[3], bank[4:8]
    with Stage(core) as st:
        staged = [st.sb("staged", [P, cfg.width]) for _ in range(2)]
        w_high = [st.sb("w_high", [P, cfg.width], F32R) for _ in range(2)]
        w_low = [st.sb("w_low", [P, cfg.pick_at], F32R) for _ in range(2)]
        acted, hidden = ([st.sb(name, [P, STEP]) for _ in range(2)] for name in ("acted", "hidden"))
        hidden_parts = [[st.sb("hidden_parts", [P, STEP], F32R) for _ in range(2)] for _ in range(2)]
        zeros = st.sb("zeros", [P, STEP], BF16)
        w_loaded = [st.sem("w_loaded") for _ in range(2)]
        high_ready, low_ready, zeros_ready = st.sem("high_ready"), st.sem("low_ready"), st.sem("zeros_ready")
        a_done, up_done, pick_done = st.sem("a_done"), st.sem("up_done"), st.sem("pick_done")
        acted_ready, gated_ready, hidden_ready = st.sem("acted_ready"), st.sem("gated_ready"), st.sem("hidden_ready")
        hidden_high, hidden_low = st.sem("hidden_high"), st.sem("hidden_low")
        down_done, y_done, y_read = st.sem("down_done"), st.sem("y_done"), st.sem("y_read")

        class Group:

            def __init__(self, c, i, k):
                self.c, self.i, self.k = c, i, k
                self.j = 2 * i + k
                self.u = c * NG + self.j
                self.parity = (c * NG + k) % 2
                self.turn = i + (c * NG + k) // 2
                known = isinstance(i, int)
                self.first, self.last = known and self.j == 0, known and self.j == NG - 1
                self.very_last = self.last and c == 1

            def next(self):
                return Group(self.c + 1, 0, 0) if self.last else Group(self.c, self.i, self.k + 1)

            def before(self):
                return Group(self.c - 1, 0, NG - 1) if self.first else Group(self.c, self.i, self.k - 1)

            def step(self, s):
                return 2 * self.u + s

        def over_groups(eng, work):
            for c in range(2):
                work(Group(c, 0, 0))
                pairs = (NG - 2) // 2
                with eng.Fori(0, pairs) as i:
                    work(Group(c, i, 1))
                    work(Group(c, i, 2))
                for k in range(2 * pairs + 1, NG):
                    work(Group(c, 0, k))

        with nc.Block() as block:

            @block.sync
            def _(sp):
                sp.dma_start(staged[0][:], w_in[0]).then_inc(w_loaded[0], 16)

                def work(g):
                    if not g.very_last:
                        need(sp, low_ready, g.u)
                        source = w_in[0] if g.last else w_in[bass.ds(g.j + 1, 1)].rearrange("a p n -> p (a n)")
                        sp.dma_start(staged[1 - g.parity][:], source).then_inc(w_loaded[1 - g.parity], 16)

                over_groups(sp, work)

            @block.tensor
            def _(pe):
                def passes(out, operands, start=True, stop=True):
                    n = len(operands)
                    for i, (a, c) in enumerate(operands):
                        ins = nc.tensor.matmul(out, a, c, start=(start and i == 0), stop=(stop and i == n - 1))
                    return ins

                z = (core.norm_t_high, core.norm_t_low)

                def up(g, s):
                    r = g.step(s)
                    if s == 0:
                        pe.wait_ge(low_ready, g.u + 1)
                    tokens = slice(g.c * HALF + s * STEP, g.c * HALF + (s + 1) * STEP)
                    w = (w_high[g.parity], w_low[g.parity])

                    def product(out, at):
                        return passes(out, [(w[a][:, at + kt * P:at + (kt + 1) * P], z[b][:, kt, tokens])
                                            for kt in range(KT) for a, b in ((0, 0), (0, 1), (1, 0))])

                    need(pe, acted_ready, r - 1)
                    product(a_bank[s][:], 0).then_inc(a_done, 1)
                    if cfg.gated:
                        need(pe, gated_ready, r)
                        product(up_bank[:], KT * P).then_inc(up_done, 1)
                    need(pe, hidden_ready, r)
                    passes(pick_bank[:], [(w[0][:, cfg.pick_at:cfg.pick_at + P], gates_t[b][:, tokens]) for b in (0, 1)])\
                        .then_inc(pick_done, 1)

                def down(g, s):
                    r = g.step(s)
                    pe.wait_ge(hidden_low, r + 1)
                    if g.first and s == 0:
                        need(pe, y_read, g.c)
                        for y in y_bank:
                            nc.tensor.matmul(y[:], zeros[:, 0:P], zeros[:], start=True, stop=False)
                    for t in range(STEP // P):
                        y = y_bank[2 * s + t // 2][:, (t % 2) * C:(t % 2 + 1) * C]
                        tokens = slice(t * P, (t + 1) * P)
                        ins = passes(y, [(hidden_parts[s][a][:, tokens],
                                          (w_high, w_low)[b][g.parity][:, cfg.down_at:cfg.down_at + C])
                                         for a, b in ((0, 0), (0, 1), (1, 0))], start=False, stop=False)
                    ins.then_inc(down_done, 1)
                    if g.last and s == 1:
                        for y in y_bank:
                            ins = nc.tensor.matmul(y[:], zeros[:, 0:P], zeros[:], start=False, stop=True)
                        ins.then_inc(y_done, 1)

                pe.wait_ge(zeros_ready, 1)

                def work(g):
                    up(g, 0)
                    if not (g.first and g.c == 0):
                        down(g.before(), 1)
                    up(g, 1)
                    down(g, 0)

                over_groups(pe, work)
                down(Group(1, 0, NG - 1), 1)

            @block.scalar
            def _(act):
                def split(g):
                    act.wait_ge(w_loaded[g.parity], (g.turn + 1) * 16)
                    need(act, down_done, 2 * (g.u - 1))
                    nc.scalar.activation(w_high[g.parity][:], staged[g.parity][:], ACT.Copy).then_inc(high_ready, 1)

                split(Group(0, 0, 0))

                def work(g):
                    for s in range(2):
                        r = g.step(s)
                        act.wait_ge(a_done, r + 1)
                        need(act, hidden_ready, r - 1)
                        nc.scalar.activation(acted[s][:], a_bank[s][:], cfg.act).then_inc(acted_ready, 1)
                        act.wait_ge(hidden_ready, r + 1)
                        need(act, down_done, r - 1)
                        nc.scalar.activation(hidden_parts[s][0][:], hidden[s][:], ACT.Copy).then_inc(hidden_high, 1)
                        if s == 0 and not g.very_last:
                            split(g.next())

                over_groups(act, work)

            @block.vector
            def _(dve):
                nc.vector.memset(zeros[:], 0.0).then_inc(zeros_ready, 1)

                def split(g):
                    dve.wait_ge(high_ready, g.u + 1)
                    nc.vector.tensor_tensor(w_low[g.parity][:], staged[g.parity][:, 0:cfg.pick_at],
                                            w_high[g.parity][:, 0:cfg.pick_at].bitcast(F32), ALU.subtract).then_inc(low_ready, 1)

                split(Group(0, 0, 0))

                def add_to_x(c):
                    dve.wait_ge(y_done, c + 1)
                    for i, y in enumerate(y_bank):
                        tile = c * TILES // 2 + 2 * i
                        tiles = x[:, tile:tile + 2, :]
                        ins = nc.vector.tensor_tensor(tiles, y[:].rearrange("p (t c) -> p t c", t=2), tiles, ALU.add)
                    ins.then_inc(y_read, 1)

                def work(g):
                    for s in range(2):
                        r = g.step(s)
                        dve.wait_ge(acted_ready, r + 1)
                        source = acted[s]
                        need(dve, hidden_high, r - 1)
                        need(dve, hidden_low, r - 1)
                        if cfg.gated:
                            dve.wait_ge(up_done, r + 1)
                            nc.vector.tensor_tensor(hidden[s][:], acted[s][:], up_bank[:], ALU.mult).then_inc(gated_ready, 1)
                            dve.wait_ge(gated_ready, r + 1)
                            source = hidden[s]
                        dve.wait_ge(pick_done, r + 1)
                        nc.vector.tensor_tensor(hidden[s][:], source[:], pick_bank[:], ALU.mult).then_inc(hidden_ready, 1)
                        if s == 1 and g.first and g.c == 1:
                            add_to_x(0)
                        dve.wait_ge(hidden_high, r + 1)
                        dve.wait_ge(hidden_ready, r + 1)
                        nc.vector.tensor_tensor(hidden_parts[s][1][:], hidden[s][:], hidden_parts[s][0][:].bitcast(F32),
                                                ALU.subtract).then_inc(hidden_low, 1)
                        if s == 0 and not g.very_last:
                            split(g.next())

                over_groups(dve, work)
                add_to_x(1)


def thought_stage(core, w_in, gate_w_in, rows_in, columns_in, wide_rows_in, steps=4, hidden=1024, eps=1e-6):
    nc, x, bank = core.nc, core.x, core.bank
    HB = hidden // P
    AGG, BC, D1, D2 = 0, KT * C, 2 * KT * C, 2 * KT * C + KT * hidden
    with Stage(core) as st:
        w = st.sb("w", [P, D2 + HB * C])
        gate_staged = st.sb("gate_staged", [P, KT, C])
        gate_w = [st.sb("gate_w", [P, KT, C], F32R) for _ in range(2)]
        rows = st.sb("rows", [B, 6, C])
        columns = st.sb("columns", [P, HB + 2 * KT])
        wide_rows = st.sb("wide_rows", [P, 2, C])
        gate = st.sb("gate", [P, KT, TILES * P])
        last, current, thought, thought_bias = (st.sb(n, [B, C]) for n in ("last", "current", "thought", "thought_bias"))
        stats8, meanvar8, rstd8 = st.sb("stats8", [B, 6]), st.sb("meanvar8", [B, 2]), st.sb("rstd8", [B, 1])
        half8, half = st.sb("half8", [B, 1]), st.sb("half", [P, QT])
        var8, eps_tile = st.sb("var8", [B, 1]), st.sb("eps_tile", [P, QT])
        carrier = [st.sb("carrier", [1, 1]) for _ in range(2)]
        current_t, act_in, acted = st.sb("current_t", [P, KT, B]), st.sb("act_in", [P, HB, B]), st.sb("acted", [P, HB, B])
        message_t = st.sb("message_t", [P, KT, B])
        sent = [st.sb("sent", [P, KT, S]) for _ in range(2)]
        mixed = [st.sb("mixed", [P, QT, C]) for _ in range(2)]
        stats = [st.sb("stats", [P, QT, 6]) for _ in range(2)]
        meanvar = [st.sb("meanvar", [P, QT, 2]) for _ in range(2)]
        var_eps, rstd, shift = ([st.sb(n, [P, QT]) for _ in range(2)] for n in ("var_eps", "rstd", "shift"))

        loaded, last_loaded = st.sem("loaded"), st.sem("last_loaded")
        gate_high, gate_low, gate_done, gate_ready = st.sem("gate_high"), st.sem("gate_low"), st.sem("gate_done"), st.sem("gate_ready")
        chain, var8_ready, rstd8_ready, pool_chain = st.sem("chain"), st.sem("var8_ready"), st.sem("rstd8_ready"), st.sem("pool_chain")
        current_ready, current_t_done, current_t_ready = st.sem("current_ready"), st.sem("current_t_done"), st.sem("current_t_ready")
        product_done, act_in_ready, acted_ready = st.sem("product_done"), st.sem("act_in_ready"), st.sem("acted_ready")
        message_ready, sent_ready, sent_t_done, mixed_ready = st.sem("message_ready"), st.sem("sent_ready"), st.sem("sent_t_done"), st.sem("mixed_ready")
        var_ready, rstd_ready, half_ready, tail = st.sem("var_ready"), st.sem("rstd_ready"), st.sem("half_ready"), st.sem("tail")
        ROUNDS = 3 + steps
        t_bank, wide_bank, row_bank = bank[4], bank[5], bank[6]

        with nc.Block() as block:

            @block.sync
            def _(sp):
                sp.dma_start(last[:], x[P - 1:P, QT - 1::QT, :]).then_inc(last_loaded, 16)
                sp.dma_start(gate_staged[:], gate_w_in).then_inc(last_loaded, 16)
                for t, source in ((rows, rows_in), (columns, columns_in), (w, w_in), (wide_rows, wide_rows_in)):
                    sp.dma_start(t[:], source).then_inc(loaded, 16)

            @block.gpsimd
            def _(pool):
                nc.gpsimd.memset(half8[:], -0.5)
                nc.gpsimd.memset(eps_tile[:], eps)
                nc.gpsimd.memset(half[:], -0.5).then_inc(half_ready, 1)
                pool.wait_ge(half_ready, 1)
                for n in range(2 + steps):
                    pool.wait_ge(var8_ready, n + 1)
                    nc.gpsimd.tensor_scalar(var8[:], meanvar8[:, 1:2], 1.0, 1e-5 if n == 0 else eps, ALU.mult, ALU.add)\
                        .then_inc(pool_chain, 1)
                    pool.wait_ge(pool_chain, n + 1)
                    nc.gpsimd.tensor_tensor(rstd8[:], var8[:], half8[:], ALU.pow).then_inc(rstd8_ready, 1)

                with pool.Fori(0, PAIRS) as i:
                    for par in range(2):
                        b = 2 * i + par
                        pool.wait_ge(var_ready, b + 1)
                        nc.gpsimd.tensor_tensor(var_eps[par][:], meanvar[par][:, :, 1], eps_tile[:], ALU.add)\
                            .then_inc(pool_chain, 1)
                        pool.wait_ge(pool_chain, 2 + steps + b + 1)
                        nc.gpsimd.tensor_tensor(rstd[par][:], var_eps[par][:], half[:], ALU.pow).then_inc(rstd_ready, 1)

            @block.tensor
            def _(pe):
                pe.wait_ge(gate_low, 1)

                def gates(i):
                    for par in range(2):
                        b = 2 * i + par
                        need(pe, gate_ready, b - 1)
                        for c in range(KT):
                            n = 0
                            for kt in range(KT):
                                for a, m in ((0, 0), (0, 1), (1, 0)):
                                    z = (core.norm_t_high, core.norm_t_low)[m]
                                    ins = nc.tensor.matmul(bank[par][:, c * S:(c + 1) * S], gate_w[a][:, kt, c * P:(c + 1) * P],
                                                           z[:, kt, bass.ds(b * S, S)], start=(n == 0), stop=(n == 5))
                                    n += 1
                        ins.then_inc(gate_done, 1)

                gates(0)
                with pe.Fori(1, PAIRS) as i:
                    gates(i)

                pe.wait_ge(loaded, 64)

                def transpose_current(n):
                    pe.wait_ge(current_ready, n + 1)
                    for kt in range(KT):
                        ins = nc.tensor.transpose(t_bank[:, kt * B:(kt + 1) * B], current[:, kt * P:(kt + 1) * P],
                                                  core.ident[0:B, 0:B])
                    ins.then_inc(current_t_done, 1)
                    pe.wait_ge(current_t_ready, n + 1)

                def by_rows(at, operands, count):
                    for kt in range(count):
                        ins = nc.tensor.matmul(row_bank[0:B, 0:C], operands[:, kt, :], w[:, at + kt * C:at + (kt + 1) * C],
                                               start=(kt == 0), stop=(kt == count - 1))
                    ins.then_inc(product_done, 1)

                def by_columns(at, width):
                    for c in range(width // P):
                        for kt in range(KT):
                            ins = nc.tensor.matmul(wide_bank[:, c * B:(c + 1) * B],
                                                   w[:, at + kt * width + c * P:at + kt * width + (c + 1) * P],
                                                   current_t[:, kt, :], start=(kt == 0), stop=(kt == KT - 1))
                    ins.then_inc(product_done, 1)

                transpose_current(0)
                by_rows(AGG, current_t, KT)
                for n in range(steps):
                    transpose_current(1 + n)
                    by_columns(D1, hidden)
                    pe.wait_ge(acted_ready, n + 1)
                    by_rows(D2, acted, HB)
                transpose_current(1 + steps)
                by_columns(BC, C)

                def back(i):
                    for par in range(2):
                        b = 2 * i + par
                        pe.wait_ge(sent_ready, b + 1)
                        need(pe, mixed_ready, b - 1)
                        for t in range(QT):
                            for kt in range(KT):
                                ins = nc.tensor.transpose(bank[2 + par][:, t * C + kt * P:t * C + (kt + 1) * P],
                                                          sent[par][:, kt, t * P:(t + 1) * P], core.ident[:])
                        ins.then_inc(sent_t_done, 1)

                back(0)
                with pe.Fori(1, PAIRS) as i:
                    back(i)

            @block.scalar
            def _(act):
                act.wait_ge(last_loaded, 32)
                nc.scalar.activation(gate_w[0][:], gate_staged[:], ACT.Copy).then_inc(gate_high, 1)
                act.wait_ge(loaded, 64)
                with act.Fori(0, PAIRS) as i:
                    for par in range(2):
                        b = 2 * i + par
                        act.wait_ge(gate_done, b + 1)
                        for c in range(KT):
                            ins = nc.scalar.activation(gate[:, c, bass.ds(b * S, S)], bank[par][:, c * S:(c + 1) * S],
                                                       ACT.Sigmoid, bias=columns[:, HB + c:HB + c + 1])
                        ins.then_inc(gate_ready, 1)
                for n in range(steps):
                    act.wait_ge(act_in_ready, n + 1)
                    nc.scalar.activation(acted[:], act_in[:], ACT.Gelu).then_inc(acted_ready, 1)

            @block.vector
            def _(dve):
                count = [0]

                def after(ins):
                    count[0] += 1
                    ins.then_inc(chain, 1)
                    dve.wait_ge(chain, count[0])

                dve.wait_ge(gate_high, 1)
                nc.vector.tensor_tensor(gate_w[1][:], gate_staged[:], gate_w[0][:].bitcast(F32), ALU.subtract).then_inc(gate_low, 1)
                dve.wait_ge(last_loaded, 32)
                dve.wait_ge(loaded, 64)

                def norm8(source, target, n, gamma=None, beta=None):
                    after(nc.vector.bn_stats(stats8[:], source[:]))
                    nc.vector.bn_aggr(meanvar8[:], stats8[:]).then_inc(var8_ready, 1)
                    dve.wait_ge(var8_ready, n + 1)
                    dve.wait_ge(rstd8_ready, n + 1)
                    ins = nc.vector.tensor_scalar(target[:], source[:], meanvar8[:, 0:1], rstd8[:, 0:1], ALU.subtract, ALU.mult)
                    if gamma is None:
                        after(ins)
                        return
                    after(ins)
                    after(nc.vector.tensor_tensor(target[:], target[:], rows[:, gamma, :], ALU.mult))
                    nc.vector.tensor_tensor(target[:], target[:], rows[:, beta, :], ALU.add).then_inc(current_ready, 1)

                def copy_transposed(n):
                    dve.wait_ge(current_t_done, n + 1)
                    nc.vector.tensor_copy(current_t[:], t_bank[:, 0:KT * B].rearrange("p (k b) -> p k b", k=KT)).then_inc(current_t_ready, 1)

                norm8(last, last, 0)
                norm8(last, current, 1, 0, 1)
                copy_transposed(0)
                dve.wait_ge(product_done, 1)
                after(nc.vector.tensor_tensor(thought[:], row_bank[0:B, 0:C], rows[:, 2, :], ALU.add))
                for n in range(steps):
                    norm8(thought, current, 2 + n, 3, 4)
                    copy_transposed(1 + n)
                    after(nc.vector.tensor_tensor(thought_bias[:], thought[:], rows[:, 5, :], ALU.add))
                    dve.wait_ge(product_done, 2 + 2 * n)
                    nc.vector.tensor_tensor(act_in[:], wide_bank[:, 0:HB * B].rearrange("p (h b) -> p h b", h=HB),
                                            columns[:, 0:HB].rearrange("p (h a) -> p h a", a=1).to_broadcast([P, HB, B]),
                                            ALU.add).then_inc(act_in_ready, 1)
                    dve.wait_ge(product_done, 3 + 2 * n)
                    after(nc.vector.tensor_tensor(thought[:], row_bank[0:B, 0:C], thought_bias[:], ALU.add))
                nc.vector.tensor_copy(current[:], thought[:]).then_inc(current_ready, 1)
                copy_transposed(1 + steps)
                dve.wait_ge(product_done, 2 + 2 * steps)
                nc.vector.tensor_tensor(message_t[:], wide_bank[:, 0:KT * B].rearrange("p (k b) -> p k b", k=KT),
                                        columns[:, HB + KT:HB + 2 * KT].rearrange("p (k a) -> p k a", a=1).to_broadcast([P, KT, B]),
                                        ALU.add).then_inc(message_ready, 1)
                dve.wait_ge(message_ready, 1)
                dve.wait_ge(gate_ready, B)

                TAIL = 8

                def send(b, par):
                    need(dve, sent_t_done, b - 1)
                    for kt in range(KT):
                        ins = nc.vector.tensor_scalar(sent[par][:, kt, :], gate[:, kt, bass.ds(b * S, S)],
                                                      message_t[:, kt, bass.ds(b, 1)], None, ALU.mult)
                    ins.then_inc(sent_ready, 1)

                def mix(b, par, base):
                    for t in range(QT):
                        tile = b * QT + t
                        ins = nc.vector.tensor_scalar(mixed[par][:, t, :], x[:, bass.ds(tile, 1), :].rearrange("p a c -> p (a c)"),
                                                      core.rstd[:, bass.ds(tile, 1)], core.shift[:, bass.ds(tile, 1)],
                                                      ALU.mult, ALU.add)
                    ins.then_inc(tail, 1)
                    dve.wait_ge(tail, base + 1)
                    dve.wait_ge(sent_t_done, b + 1)
                    nc.vector.tensor_tensor(mixed[par][:], mixed[par][:], bank[2 + par][:].rearrange("p (t c) -> p t c", t=QT),
                                            ALU.add).then_inc(mixed_ready, 1)
                    dve.wait_ge(mixed_ready, b + 1)
                    for t in range(QT):
                        ins = nc.vector.bn_stats(stats[par][:, t, :], mixed[par][:, t, :])
                    ins.then_inc(tail, 1)
                    dve.wait_ge(tail, base + 2)
                    nc.vector.memset(carrier[par][:], 0.0)
                    for t in range(QT):
                        ins = nc.vector.bn_aggr(meanvar[par][:, t, :], stats[par][:, t, :])
                    ins.then_inc(var_ready, 1)

                def add(b, par, base):
                    dve.wait_ge(rstd_ready, b + 1)
                    dve.wait_ge(var_ready, b + 1)
                    nc.vector.scalar_tensor_tensor(shift[par][:], meanvar[par][:, :, 0], -1.0, rstd[par][:], ALU.mult, ALU.mult)\
                        .then_inc(tail, 1)
                    dve.wait_ge(tail, base + 1)
                    for t in range(QT):
                        ins = nc.vector.tensor_scalar(mixed[par][:, t, :], mixed[par][:, t, :], rstd[par][:, t:t + 1],
                                                      shift[par][:, t:t + 1], ALU.mult, ALU.add)
                    ins.then_inc(tail, 1)
                    dve.wait_ge(tail, base + 2)
                    tiles = x[:, bass.ds(b * QT, QT), :]
                    gamma, beta = (wide_rows[:, n:n + 1, :].to_broadcast([P, QT, C]) for n in range(2))
                    nc.vector.tensor_tensor(mixed[par][:], mixed[par][:], gamma, ALU.mult).then_inc(tail, 1)
                    nc.vector.tensor_tensor(tiles, tiles, beta, ALU.add).then_inc(tail, 1)
                    dve.wait_ge(tail, base + 4)
                    nc.vector.tensor_tensor(tiles, tiles, mixed[par][:], ALU.add).then_inc(tail, 1)

                PER = 7

                def pair(i):
                    send(2 * i, 0)
                    send(2 * i + 1, 1)
                    base = 2 * PER * i
                    mix(2 * i, 0, base)
                    mix(2 * i + 1, 1, base + 2)
                    add(2 * i, 0, base + 4)
                    add(2 * i + 1, 1, base + 9)

                pair(0)
                with dve.Fori(1, PAIRS) as i:
                    pair(i)


def four_layers_kernel(nc, d, out):
    narrow = (NarrowAttention(16, causal=True), NarrowAttention(32, causal=False))
    wide = {2: WideAttention(4, 4, shared_kv=True, rope=False, causal=True, scale=1 / math.sqrt(P)),
            3: WideAttention(2, 8, shared_kv=False, rope=True, causal=False, scale=1 / math.sqrt(P))}
    experts = {0: Experts(64, 6, d["experts_0"].shape[0], True, ACT.Silu, "sigmoid", capacity=128),
               2: Experts(16, 2, d["experts_2"].shape[0], False, ACT.Gelu, "softmax"),
               3: Experts(32, 6, d["experts_3"].shape[0], True, ACT.Silu, "limited")}

    with ExitStack() as stack:
        core = Core(nc, stack)
        load_stage(core, d["x"], d["ident"])

        def feed_forward(layer):
            norm_stage(core)
            with ExitStack() as held:
                gates_t = [held.enter_context(nc.sbuf_tensor(core.unique("gates_t"), [P, TILES * P], F32R)) for _ in range(2)]
                route_stage(core, experts[layer], d[f"router_{layer}"], gates_t, [d["earlier"]])
                experts_stage(core, experts[layer], d[f"experts_{layer}"], gates_t)

        norm_stage(core)
        narrow_attention_stage(core, narrow[0], d["attention_0"], d["select_0"], [d["mask"], d["out_bias_0"]])
        feed_forward(0)
        norm_stage(core)
        narrow_attention_stage(core, narrow[1], d["attention_1"], d["select_1"], [d["relative_1"]])
        norm_stage(core)
        thought_stage(core, d["thought_w"], d["thought_gate_w"], d["thought_rows"], d["thought_columns"], d["thought_wide_rows"])
        norm_stage(core)
        wide_attention_stage(core, wide[2], d["attention_2"], [d["position"], d["bias_2"], d["value_bias_2"], d["mask"]])
        feed_forward(2)
        norm_stage(core)
        wide_attention_stage(core, wide[3], d["attention_3"], [d["rotation"]])
        feed_forward(3)
        store_stage(core, out)



def by_contraction(w):
    return np.concatenate([w[at:at + P] for at in range(0, w.shape[0], P)], axis=1)


def narrow_weights(i, layer):
    return np.concatenate([by_contraction(i[f"{layer}_attn_{n}"].T) for n in ("wq", "wk", "wv", "wo")], axis=1)


def stack_selection(heads):
    dim = C // heads
    rows = 4 * dim
    per = P // rows
    s = np.zeros((P, 2, 4, 2, P), np.float32)
    for which, blocks in enumerate(((0, 1, 0, 1), (0, 0, 1, 1))):
        for tile in range(4):
            for head in range(per):
                for block, part in enumerate(blocks):
                    n = np.arange(dim)
                    s[(tile * per + head) * dim + n, which, tile, part, head * rows + block * dim + n] = 1
    return s


def relative_table(rel_pos):
    relative = np.arange(S + P)[None] - np.arange(P)[:, None] - P
    return rel_pos[np.clip(relative + 63, 0, 126)]


def position_encoding():
    ang = np.arange(S, dtype=np.float32)[:, None] * np.exp(-(np.log(np.float32(10000.0)) * np.arange(0, P, 2, dtype=np.float32) / np.float32(P)))
    pe = np.zeros((S, P), np.float32)
    pe[:, 0::2], pe[:, 1::2] = np.sin(ang), np.cos(ang)
    return pe.T


def rotation_table():
    inv = 1.0 / np.float32(10000.0) ** (np.arange(0, 64, 2, dtype=np.float32) / np.float32(64))
    angle = np.arange(S, dtype=np.float32)[:, None] * inv[None]
    c, s = np.cos(angle).T.astype(np.float32), np.sin(angle).T.astype(np.float32)
    table = np.stack([np.concatenate([c, -s], axis=1), np.concatenate([s, c], axis=1)], axis=1)
    scale = np.float32(1 / 8)
    return np.concatenate([table * scale, table * scale, table, table])


def wide_weights_2(i):
    wq, wkv, wo = (i[f"L2_attn_{n}"] for n in ("wq", "wkv", "wo"))
    return np.stack([np.concatenate([
        by_contraction(wq[:, g * 512:(g + 1) * 512]), by_contraction(wkv[:, g * 256:g * 256 + P]),
        by_contraction(wkv[:, g * 256 + P:(g + 1) * 256]), by_contraction(wo[g * 512:(g + 1) * 512])], axis=1) for g in range(4)])


def wide_biases_2(i):
    kv = i["L2_attn_bkv"].reshape(4, 2, P)
    columns = np.concatenate([i["L2_attn_bq"].reshape(4, 4, P), kv[:, :1]], axis=1).transpose(2, 0, 1)
    return columns, np.broadcast_to(kv[:, 1], (P, 4, P))


def wide_weights_3(i):
    wq, wk, wv, wo = (i[f"L3_attn_{n}"] for n in ("Wq", "Wk", "Wv", "Wo"))
    blocks = []
    for g in range(8):
        turned = np.stack([w[2048 + g * P:2048 + (g + 1) * P] for w in (wq, wk)]).reshape(4, 2, 32, C)
        parts = [by_contraction(turned.transpose(1, 0, 2, 3).reshape(2 * P, C).T)]
        parts += [by_contraction(w[g * 256:(g + 1) * 256].T) for w in (wq, wk)]
        parts += [by_contraction(wv[g * 256:(g + 1) * 256].T), by_contraction(wo.T[g * 256:(g + 1) * 256])]
        blocks.append(np.concatenate(parts, axis=1))
    return np.stack(blocks)


def hidden_groups(ups, down, owner):
    rows = down.shape[0]
    whole = -(-rows // P) * P
    ups = [np.concatenate([u, np.zeros((C, whole - rows), u.dtype)], axis=1) for u in ups]
    down = np.concatenate([down, np.zeros((whole - rows, C), down.dtype)])
    owner = np.concatenate([owner, np.full(whole - rows, owner[-1])])
    groups = []
    for at in range(0, whole, P):
        pick = np.zeros((P, P), np.float32)
        pick[owner[at:at + P], np.arange(P)] = 1
        groups.append(np.concatenate([by_contraction(u[:, at:at + P]) for u in ups] + [down[at:at + P], pick], axis=1))
    return groups


def flat(w):
    return w.transpose(1, 0, 2).reshape(C, -1)


def expert_weights(i):
    def get(layer, *names):
        return (i[f"L{layer}_ffn_{n}"] for n in names)
    up, down, shared_up, shared_down = get(0, "w_up", "w_down", "w_shared_up", "w_shared_down")
    first = hidden_groups([flat(up[:, :, :32]), flat(up[:, :, 32:])], down.reshape(-1, C), np.repeat(np.arange(64), 32))
    first += hidden_groups([shared_up[:, 64:], shared_up[:, :64]], shared_down, np.full(64, 64))
    up, down, shared_up, shared_down = get(2, "Wrt_up", "Wrt_down", "Wsh_up", "Wsh_down")
    second = hidden_groups([flat(up)], down.reshape(-1, C), np.repeat(np.arange(16), 128))
    second += hidden_groups([flat(shared_up)], shared_down.reshape(-1, C), np.full(256, 16))
    gate, up, down, shared_gate, shared_up, shared_down = get(3, "w_gate", "w_up", "w_down", "sw_gate", "sw_up", "sw_down")
    third = hidden_groups([flat(gate), flat(up)], down.reshape(-1, C), np.repeat(np.arange(32), 176))
    third += hidden_groups([shared_gate, shared_up], shared_down, np.full(352, 32))
    return {"experts_0": np.stack(first), "experts_2": np.stack(second), "experts_3": np.stack(third)}


def layouts(i):
    def thought(n):
        return i[f"L1_ffn_{n}"]

    def by_tile(w):
        return w.reshape(KT, P, -1).transpose(1, 0, 2)

    n = np.arange(P)
    bias_2, value_bias_2 = wide_biases_2(i)
    return {
        "x": i["L0_attn_x"].reshape(TILES, P, C).transpose(1, 0, 2),
        "ident": np.eye(P, dtype=np.float32),
        "mask": np.where(n[None] > n[:, None], np.float32(MASKED), np.float32(0)),
        "earlier": np.where(n[:, None] < n[None], np.float32(1), np.float32(0)),
        "attention_0": narrow_weights(i, "L0"), "select_0": stack_selection(16), "out_bias_0": i["L0_attn_bo"][None],
        "attention_1": narrow_weights(i, "L1"), "select_1": stack_selection(32),
        "relative_1": relative_table(i["L1_attn_rel_pos"]),
        "attention_2": wide_weights_2(i), "bias_2": bias_2, "value_bias_2": value_bias_2, "position": position_encoding(),
        "attention_3": wide_weights_3(i), "rotation": rotation_table(),
        "router_0": by_tile(i["L0_ffn_w_gate"]), "router_2": by_tile(i["L2_ffn_W_router"]), "router_3": by_tile(i["L3_ffn_gate_w"]),
        **expert_weights(i),
        "thought_w": np.concatenate([by_contraction(thought(w)) for w in ("agg_w", "bc_w", "d1_w", "d2_w")], axis=1),
        "thought_gate_w": by_tile(thought("gate_w")),
        "thought_rows": np.broadcast_to(np.stack([thought(w) for w in ("in_gamma", "in_beta", "agg_b", "pn_gamma", "pn_beta", "d2_b")]), (B, 6, C)),
        "thought_columns": np.concatenate([thought(w).reshape(-1, P) for w in ("d1_b", "gate_b", "bc_b")]).T,
        "thought_wide_rows": np.broadcast_to(np.stack([thought(w) for w in ("out_gamma", "out_beta")]), (P, 2, C)),
    }


def kernel(**inputs):
    import concourse.bacc as bacc
    from concourse.bass_utils import run_bass_kernel_spmd

    arrays = {f"in_{name}": np.ascontiguousarray(a) for name, a in layouts({k: np.asarray(v) for k, v in inputs.items()}).items()}
    nc = bacc.Bacc("TRN2", target_bir_lowering=False, num_devices=1)
    d = {name[3:]: nc.dram_tensor(name, a.shape, mybir.dt.from_np(a.dtype), kind="ExternalInput").ap() for name, a in arrays.items()}
    out = nc.dram_tensor("out", (P, TILES, C), F32, kind="ExternalOutput").ap()
    four_layers_kernel(nc, d, out)
    result = run_bass_kernel_spmd(nc, [arrays], core_ids=[0])
    return result.results[0]["out"].transpose(1, 0, 2).reshape(B, S, C)
```

```python
import math
from contextlib import ExitStack

import numpy as np

import concourse.bass as bass
from concourse import mybir

F32 = mybir.dt.float32
F32R = mybir.dt.float32r
BF16 = mybir.dt.bfloat16
ALU = mybir.AluOpType
ACT = mybir.ActivationFunctionType
AX = mybir.AxisListType

P = 128
B, S, C = 8, 256, 256
TILES = B * S // P
KT = C // P
QT = S // P
BIG = 3.0e38
MASKED = -1.0e30
PAIRS = B // 2


def need(eng, sem, value):
    if isinstance(value, int) and value <= 0:
        return
    eng.wait_ge(sem, value)


class Stage:

    def __init__(self, core):
        self.nc, self.core, self.stack, self.sems = core.nc, core, ExitStack(), []

    def __enter__(self):
        self.stack.__enter__()
        return self

    def __exit__(self, *error):
        self.stack.__exit__(*error)
        if not error[0]:
            self.nc.clear_and_free_semaphores(self.sems)
            self.nc.all_engine_barrier()

    def sb(self, name, shape, dtype=F32):
        return self.stack.enter_context(self.nc.sbuf_tensor(self.core.unique(name), shape, dtype))

    def sem(self, name):
        s = self.nc.alloc_semaphore(self.core.unique(name))
        self.sems.append(s)
        return s


class Core:

    def __init__(self, nc, stack):
        self.nc, self.count = nc, 0

        def sb(name, shape, dtype=F32):
            return stack.enter_context(nc.sbuf_tensor(name, shape, dtype))

        self.x = sb("x_sb", [P, TILES, C])
        self.norm_t_high = sb("norm_t_high", [P, KT, TILES * P], F32R)
        self.norm_t_low = sb("norm_t_low", [P, KT, TILES * P], F32R)
        self.rstd = sb("rstd", [P, TILES])
        self.shift = sb("shift", [P, TILES])
        self.ident = sb("ident_sb", [P, P])
        self.ident_bf = sb("ident_bf", [P, P], BF16)
        self.bank = [stack.enter_context(nc.psum_tensor(f"bank{i}", [P, 512], F32)) for i in range(8)]

    def unique(self, name):
        self.count += 1
        return f"{name}_{self.count}"


def load_stage(core, x_in, ident_in):
    nc = core.nc
    with Stage(core) as st:
        loaded = st.sem("loaded")
        with nc.Block() as block:

            @block.sync
            def _(sp):
                sp.dma_start(core.x[:], x_in).then_inc(loaded, 16)
                sp.dma_start(core.ident[:], ident_in).then_inc(loaded, 16)
                sp.wait_ge(loaded, 32)

            @block.vector
            def _(dve):
                dve.wait_ge(loaded, 32)
                nc.vector.tensor_copy(core.ident_bf[:], core.ident[:])


def store_stage(core, out):
    nc = core.nc
    with Stage(core) as st:
        stored = st.sem("stored")
        with nc.Block() as block:

            @block.sync
            def _(sp):
                sp.dma_start(out, core.x[:]).then_inc(stored, 16)
                sp.wait_ge(stored, 16)


def norm_stage(core, early_loads=(), eps=1e-5):
    nc, x = core.nc, core.x
    with Stage(core) as st:
        stats = st.sb("stats", [P, TILES, 6])
        meanvar = st.sb("meanvar", [P, TILES, 2])
        var_eps = st.sb("var_eps", [P, TILES])
        minus_half = st.sb("minus_half", [P, TILES])
        normed = [[st.sb("normed", [P, C]) for _ in range(QT)] for _ in range(2)]
        stats_ready, meanvar_ready = st.sem("stats_ready"), st.sem("meanvar_ready")
        pool_step, rstd_ready, shift_ready = st.sem("pool_step"), st.sem("rstd_ready"), st.sem("shift_ready")
        normed_ready, normed_by_act, transposed = st.sem("normed_ready"), st.sem("normed_by_act"), st.sem("transposed")
        high_ready, low_ready = st.sem("high_ready"), st.sem("low_ready")
        bank = core.bank

        def columns(t, b):
            return t[:, :, bass.ds(b * S, S)]

        parts = (0, 2 * QT, TILES)

        with nc.Block() as block:

            @block.sync
            def _(sp):
                for target, source, semaphore in early_loads:
                    sp.dma_start(target, source).then_inc(semaphore, 16)

            @block.gpsimd
            def _(pool):
                nc.gpsimd.memset(minus_half[:], -0.5).then_inc(pool_step, 1)
                for n, (first, end) in enumerate(zip(parts, parts[1:])):
                    pool.wait_ge(meanvar_ready, end)
                    nc.gpsimd.tensor_scalar(var_eps[:, first:end], meanvar[:, first:end, 1], 1.0, float(eps), ALU.mult, ALU.add)\
                        .then_inc(pool_step, 1)
                    pool.wait_ge(pool_step, n + 2)
                    nc.gpsimd.tensor_tensor(core.rstd[:, first:end], var_eps[:, first:end], minus_half[:, first:end], ALU.pow)\
                        .then_inc(rstd_ready, 1)

            @block.vector
            def _(dve):
                for first, end in zip(parts, parts[1:]):
                    for t in range(first, end):
                        nc.vector.bn_stats(stats[:, t, :], x[:, t, :]).then_inc(stats_ready, 1)
                    for t in range(first, end):
                        dve.wait_ge(stats_ready, t + 1)
                        nc.vector.bn_aggr(meanvar[:, t, :], stats[:, t, :]).then_inc(meanvar_ready, 1)

                def shift(n):
                    first, end = parts[n:n + 2]
                    dve.wait_ge(rstd_ready, n + 1)
                    dve.wait_ge(meanvar_ready, end)
                    nc.vector.scalar_tensor_tensor(core.shift[:, first:end], meanvar[:, first:end, 0], -1.0,
                                                   core.rstd[:, first:end], ALU.mult, ALU.mult).then_inc(shift_ready, 1)
                    dve.wait_ge(shift_ready, n + 1)

                def apply(b, par):
                    need(dve, transposed, b - 1)
                    tile = b * QT
                    nc.vector.tensor_scalar(
                        normed[par][0][:], x[:, bass.ds(tile, 1), :].rearrange("p a c -> p (a c)"),
                        core.rstd[:, bass.ds(tile, 1)], core.shift[:, bass.ds(tile, 1)], ALU.mult, ALU.add)\
                        .then_inc(normed_ready, 1)

                def low(b, par):
                    dve.wait_ge(high_ready, b + 1)
                    nc.vector.tensor_tensor(columns(core.norm_t_low, b), bank[par][:].rearrange("p (k t) -> p k t", k=KT),
                                            columns(core.norm_t_high, b).bitcast(F32), ALU.subtract).then_inc(low_ready, 1)

                shift(0)
                apply(0, 0)

                def pair(i, last=False):
                    apply(2 * i + 1, 1)
                    low(2 * i, 0)
                    if not last:
                        apply(2 * i + 2, 0)
                    low(2 * i + 1, 1)

                apply(1, 1)
                shift(1)
                low(0, 0)
                apply(2, 0)
                low(1, 1)
                with dve.Fori(1, PAIRS - 1) as i:
                    pair(i)
                pair(PAIRS - 1, last=True)

            @block.tensor
            def _(pe):
                def pair(i):
                    for par in range(2):
                        b = 2 * i + par
                        pe.wait_ge(normed_ready, b + 1)
                        pe.wait_ge(normed_by_act, b + 1)
                        need(pe, low_ready, b - 1)
                        for t in range(QT):
                            for k in range(KT):
                                ins = nc.tensor.transpose(bank[par][:, k * S + t * P:k * S + (t + 1) * P],
                                                          normed[par][t][:, k * P:(k + 1) * P], core.ident[:])
                        ins.then_inc(transposed, 1)

                pair(0)
                with pe.Fori(1, PAIRS) as i:
                    pair(i)

            @block.scalar
            def _(act):
                def apply(b):
                    act.wait_ge(shift_ready, 1 if b < 2 else 2)
                    need(act, transposed, b - 1)
                    tile = b * QT + 1
                    nc.scalar.activation(normed[b % 2][1][:], x[:, tile, :], ACT.Identity, bias=core.shift[:, tile:tile + 1],
                                         scale=core.rstd[:, tile:tile + 1]).then_inc(normed_by_act, 1)

                apply(0)
                for b in range(B):
                    if b < B - 1:
                        apply(b + 1)
                    act.wait_ge(transposed, b + 1)
                    nc.scalar.activation(columns(core.norm_t_high, b), bank[b % 2][:].rearrange("p (k t) -> p k t", k=KT),
                                         ACT.Copy).then_inc(high_ready, 1)


class WideAttention:

    def __init__(self, heads, groups, shared_kv, rope, causal, scale):
        self.HG, self.G, self.rope, self.causal, self.scale = heads, groups, rope, causal, scale
        self.shared_kv, self.KV = shared_kv, 1 if shared_kv else heads
        widths = [2 * P, heads * P, self.KV * P, self.KV * P] if rope else [heads * P, P, P]
        scales = [1.0, scale, 1.0, 1.0] if rope else [scale, 1.0, 1.0]
        names = ["rope", "q", "k", "v"] if rope else ["q", "k", "v"]
        at, self.segment, self.parts = 0, {}, []
        for name, width, s in zip(names, widths, scales):
            self.segment[name] = (len(self.parts), at, width)
            self.parts.append((at, at + KT * width, s))
            at += KT * width
        self.wo_at, self.width = at, at + heads * C
        self.parts.append((at, self.width, 1.0))
        if rope:
            self.pieces = [("q", False, ["q"]), ("k", False, ["k"]), ("v", False, ["v"]), ("rope", True, ["rope"])]
            self.before = {0: [0], 1: [2]}
            self.after = {0: [1], 1: [3]}
        else:
            self.pieces = [("q", True, ["q"]), ("q2", True, ["q"]), ("kv", True, ["k", "v"])]
            self.before = {}
            self.after = {0: [0], 1: [1], 2: [2]}
        self.ahead = 1 if rope else 0
        self.sums = [i for i, p in enumerate(self.pieces) if p[1]]


def wide_attention_stage(core, cfg, w_in, consts_in):
    nc, x, bank = core.nc, core.x, core.bank
    norm_t = (core.norm_t_high, core.norm_t_low)
    HG, G, KV, rope, causal = cfg.HG, cfg.G, cfg.KV, cfg.rope, cfg.causal
    NP, NS, NW, AHEAD = len(cfg.pieces), len(cfg.sums), len(cfg.parts), cfg.ahead
    assert B % 2 == 0 and HG % 2 == 0
    p_bank, s_bank, t_bank, o_bank, y_bank = bank[0:2], bank[2:4], bank[4], bank[5], bank[6:8]
    NB = S + P if causal else QT * S

    with Stage(core) as st:
        staged = st.sb("staged", [P, cfg.width])
        w = [st.sb("w", [P, cfg.width], F32R) for _ in range(2)]
        z, q, k, v = (
            [[st.sb(name, shape, F32R) for _ in range(2)] for _ in range(2)]
            for name, shape in (("z", [P, KT, S]), ("q", [P, HG, S]), ("k", [P, KV, S]), ("v", [P, QT, KV * P])))
        if rope:
            tables = st.sb("tables", [P, 2, 2 * S])
            consts = [tables]
            turned = st.sb("turned", [P, 2, 2 * S])
            summed = [st.sb("summed", [P, 2 * S]) for _ in range(2)]
            halves = st.sb("halves", [P, 2, 2, S], F32R)
            rotated = [st.sb("rotated", [P, 2, 2, S], F32R) for _ in range(2)]
            moved = [st.sem("moved") for _ in range(2)]
            halves_high, halves_low = st.sem("halves_high"), st.sem("halves_low")
            MOVES = 8
        else:
            position = st.sb("position", [P, S])
            bias = st.sb("bias", [P, G, HG + 1])
            v_bias = st.sb("v_bias", [P, G, P])
            mask = st.sb("mask", [P, P])
            consts = [position, bias, v_bias, mask]
            scaled_position = st.sb("scaled_position", [P, S])
            scaled_bias = st.sb("scaled_bias", [P, G, HG])
            mask_bf = st.sb("mask_bf", [P, P], BF16)
            summed = [st.sb("summed", [P, 2 * S]) for _ in range(2)]
        probs = [st.sb("probs", [P, QT, S]) for _ in range(2)]
        probs_t = [[st.sb("probs_t", [P, NB], F32R) for _ in range(2)] for _ in range(2)]
        out_t = [[st.sb("out_t", [P, S], F32R) for _ in range(2)] for _ in range(2)]
        neg_max = [st.sb("neg_max", [P, QT]) for _ in range(2)]
        sums = [st.sb("sums", [P, QT]) for _ in range(2)]
        inv = [st.sb("inv", [P, QT]) for _ in range(2)]

        consts_loaded, consts_ready = st.sem("consts_loaded"), st.sem("consts_ready")
        w_loaded, w_high, w_low = st.sem("w_loaded"), st.sem("w_high"), st.sem("w_low")
        z_loaded = [st.sem("z_loaded") for _ in range(2)]
        piece_done, piece_read, piece_high = st.sem("piece_done"), st.sem("piece_read"), st.sem("piece_high")
        sum_ready, sum_low = st.sem("sum_ready"), st.sem("sum_low")
        scores_done, max_ready, probs_ready = st.sem("scores_done"), st.sem("max_ready"), st.sem("probs_ready")
        t_done, t_high, t_low = st.sem("t_done"), st.sem("t_high"), st.sem("t_low")
        o_done, o_high, o_low = st.sem("o_done"), st.sem("o_high"), st.sem("o_low")
        y_done, y_added, inv_ready = st.sem("y_done"), st.sem("y_added"), st.sem("inv_ready")

        class Unit:

            def __init__(self, g, i, parity, first=False, last=False):
                self.g, self.i, self.parity, self.first, self.last = g, i, parity, first, last
                self.b = 2 * i + parity
                self.n = g * B + self.b
                self.opens = isinstance(i, int) and i == 0 and parity == 0
                self.closes = isinstance(i, int) and i == PAIRS - 1 and parity == 1
                self.in_last_group = isinstance(g, int) and g == G - 1

            def next(self):
                if self.closes:
                    return Unit(self.g + 1, 0, 0)
                return Unit(self.g, self.i, 1) if self.parity == 0 else Unit(self.g, self.i + 1, 0)

            def before(self):
                if self.opens:
                    return Unit(self.g - 1, PAIRS - 1, 1)
                return Unit(self.g, self.i, 0) if self.parity == 1 else Unit(self.g, self.i - 1, 1)

            def slot(self, j):
                return self.n * HG + j

        def over_units(eng, work):
            def group(g, first=False, last=False):
                work(Unit(g, 0, 0, first=first))
                work(Unit(g, 0, 1))
                with eng.Fori(1, PAIRS - 1) as i:
                    work(Unit(g, i, 0))
                    work(Unit(g, i, 1))
                work(Unit(g, PAIRS - 1, 0))
                work(Unit(g, PAIRS - 1, 1, last=last))
            group(0, first=True)
            with eng.Fori(1, G - 1) as g:
                group(g)
            group(G - 1, last=True)

        def next_slot(u, j):
            return (u, j + 1) if j + 1 < HG else (u.next(), 0)

        def slot_before(u, j):
            return (u, j - 1) if j else (u.before(), HG - 1)

        def over_slots(eng, piece, value, transposed, score, output, slot_start=None, later_pieces_last=False,
                       finish=None):
            if rope:
                piece(Unit(-1, PAIRS - 1, 1), NP - 1)
                if finish:
                    finish(Unit(0, 0, 0))
            for i in range(NP):
                piece(Unit(0, 0, 0), i)
            score(Unit(0, 0, 0), 0)

            def work(u):
                for j in range(HG):
                    if slot_start:
                        slot_start(u, j)
                    if finish and j == 0 and not u.last:
                        finish(u.next())
                    if not u.last:
                        for i in cfg.before.get(j, []):
                            piece(u.next(), i)
                    if not (u.first and j == 0):
                        value(*slot_before(u, j))
                    if later_pieces_last:
                        transposed(u, j)
                    if not u.last:
                        for i in cfg.after.get(j, []):
                            if not (cfg.pieces[i][0] == "rope" and u.next().closes and u.in_last_group):
                                piece(u.next(), i)
                    if not later_pieces_last:
                        transposed(u, j)
                    if not (u.last and j == HG - 1):
                        score(*next_slot(u, j))
                    if not (u.first and j == 0):
                        output(*slot_before(u, j))

            over_units(eng, work)
            end = Unit(G - 1, PAIRS - 1, 1)
            value(end, HG - 1)
            output(end, HG - 1)

        def piece_number(u, i):
            return u.n * NP + i + 1 + AHEAD

        def piece_bank(u, i):
            return p_bank[(u.parity * NP + i) % 2]

        def sum_number(u, i):
            s = cfg.sums.index(i)
            if rope:
                u = u.next()
            return u.n * NS + s, summed[(u.parity * NS + s) % 2]

        def destination(u, i, part):
            name = cfg.pieces[i][0]
            if name == "q":
                return [(q[u.parity][part][:, 0:2, :], slice(0, 2 * S))]
            if name == "q2":
                return [(q[u.parity][part][:, 2:4, :], slice(0, 2 * S))]
            if name == "k":
                return [(k[u.parity][part][:, 0:2, :], slice(0, 2 * S))]
            if name == "v":
                return [(v[u.parity][part][:], slice(0, 2 * S))]
            return [(k[u.parity][part][:, 0, :], slice(0, S)), (v[u.parity][part][:], slice(S, 2 * S))]

        def shaped(source, target):
            return source.rearrange("p (a c) -> p a c", a=target.shape[1]) if len(target.shape) == 3 else source

        def wait_destination_free(eng, u, i):
            need(eng, scores_done, (u.n - 1) * HG)
            if "v" in cfg.pieces[i][2]:
                need(eng, o_done, (u.n - 1) * HG)

        def wait_moved(eng, u):
            if isinstance(u.n, int) and u.n < 0:
                return
            eng.wait_ge(moved[u.parity], (u.g * PAIRS + u.i + 1) * MOVES * 16)

        def wait_weights_free(eng, g, part):
            if rope and part == 0:
                need(eng, piece_done, (g * B - 1) * NP + AHEAD)
            elif part < NW - 1:
                need(eng, piece_done, g * B * NP)
            else:
                need(eng, y_done, g * B * HG)

        def split_parts_at(u, j):
            if rope and u.next().closes and not u.in_last_group and j == 0:
                return u.g + 1, [0]
            if u.closes and not u.last and j == 0:
                return u.g + 1, range(1 if rope else 0, NW - 1)
            if u.opens and not u.first and j == 1:
                return u.g, [NW - 1]
            return None, []

        norm_stage(core, [(t[:], source, consts_loaded) for t, source in zip(consts, consts_in)]
                   + [(staged[:], w_in[0], w_loaded)])

        with nc.Block() as block:

            @block.sync
            def _(sp):
                def load_z(u):
                    need(sp, piece_done, (u.n - 1) * NP)
                    for part, source in enumerate((core.norm_t_high, core.norm_t_low)):
                        sp.dma_start(z[u.parity][part][:].bitcast(F32), source[:, :, bass.ds(u.b * S, S)].bitcast(F32))\
                            .then_inc(z_loaded[u.parity], 16)

                def move(u):
                    sp.wait_ge(halves_low, u.n + 1)
                    for half in range(2):
                        for side in range(2):
                            for head in range(2):
                                at, to = (side * 2 + head) * 32, (head * 2 + half) * 32
                                sp.dma_start(rotated[u.parity][to:to + 32, side, :, :].bitcast(F32),
                                             halves[at:at + 32, half, :, :].bitcast(F32)).then_inc(moved[u.parity], 16)

                load_z(Unit(0, 0, 0))
                if rope:
                    move(Unit(0, 0, 0))

                def work(u):
                    if not u.last:
                        load_z(u.next())
                        if rope:
                            move(u.next())
                    if u.opens and not (isinstance(u.g, int) and u.g == G - 1):
                        sp.wait_ge(w_low, (u.g + 1) * NW)
                        sp.dma_start(staged[:], w_in[bass.ds(u.g + 1, 1)].rearrange("a p n -> p (a n)"))\
                            .then_inc(w_loaded, 16)

                over_units(sp, work)

            @block.tensor
            def _(pe):
                pe.wait_ge(consts_ready, 1)

                def weights(part, name, kt, first, width):
                    _, at, whole = cfg.segment[name]
                    at += kt * whole + first
                    return w[part][:, at:at + width]

                def group_of_passes(out, operands):
                    n = len(operands)
                    for kt, (stationary, moving) in enumerate(operands):
                        for m, (a, c) in enumerate(((0, 0), (0, 1), (1, 0))):
                            ins = nc.tensor.matmul(out, stationary(a), moving(c), start=(kt == 0 and m == 0),
                                                   stop=(kt == n - 1 and m == 2))
                    return ins

                def piece(u, i):
                    name, _, segments = cfg.pieces[i]
                    p = piece_bank(u, i)
                    need(pe, piece_read, piece_number(u, i) - 2)
                    if name == "rope":
                        u = u.next()
                    if "v" in segments:
                        pe.wait_ge(z_loaded[u.parity], (u.g * PAIRS + u.i + 1) * 32)
                    if u.opens:
                        for s in segments:
                            pe.wait_ge(w_low, u.g * NW + cfg.segment[s][0] + 1)
                    zz = z[u.parity]
                    if name != "v":
                        s = segments[0]
                        for c in range(1 if name == "kv" else 2):
                            first = (c + (2 if name == "q2" else 0)) * P
                            ins = group_of_passes(p[:, c * S:(c + 1) * S], [
                                (lambda a, kt=kt: weights(a, s, kt, first, P), lambda c_, kt=kt: norm_t[c_][:, kt, bass.ds(u.b * S, S)])
                                for kt in range(KT)])
                    if "v" in segments:
                        at = S if name == "kv" else 0
                        for t in range(QT):
                            ins = group_of_passes(p[:, at + t * KV * P:at + (t + 1) * KV * P], [
                                (lambda a, kt=kt: zz[a][:, kt, t * P:(t + 1) * P],
                                 lambda c_, kt=kt: weights(c_, "v", kt, 0, KV * P)) for kt in range(KT)])
                    ins.then_inc(piece_done, 1)

                def score(u, j):
                    if j == 0:
                        if rope:
                            pe.wait_ge(piece_read, piece_number(u, 1))
                            wait_moved(pe, u)
                        else:
                            pe.wait_ge(sum_low, (u.n + 1) * NS)
                    need(pe, probs_ready, u.slot(j) - 1)
                    s = s_bank[j % 2]
                    qq, kk, kj = q[u.parity], k[u.parity], 0 if cfg.shared_kv else j
                    for t in range(QT):
                        width = P if causal and t == 0 else S
                        operands = [(qq[a][:, j, t * P:(t + 1) * P], kk[c][:, kj, 0:width])
                                    for a, c in ((0, 0), (0, 1), (1, 0))]
                        if rope:
                            rows = slice(64 * j, 64 * j + 64)
                            r = rotated[u.parity]
                            operands += [(r[rows, 0, a, t * P:(t + 1) * P], r[rows, 1, c, 0:width])
                                         for a, c in ((0, 0), (0, 1), (1, 0))]
                        for n, (a, c) in enumerate(operands):
                            ins = nc.tensor.matmul(s[:, t * S:t * S + width], a, c, start=(n == 0),
                                                   stop=(n == len(operands) - 1 and not causal))
                        if causal:
                            at = t * (S + P)
                            ins = nc.tensor.matmul(s[:, at:at + P], core.ident_bf[:], mask_bf[:], start=False, stop=True)
                    ins.then_inc(scores_done, 1)

                def transposed(u, j):
                    pe.wait_ge(probs_ready, u.slot(j) + 1)
                    need(pe, t_low, u.slot(j))
                    for kt in range(QT):
                        for t in range(kt if causal else 0, QT):
                            at = kt * S + t * P - (P if causal and kt else 0)
                            ins = nc.tensor.transpose(t_bank[:, at:at + P], probs[j % 2][:, t, kt * P:(kt + 1) * P],
                                                      core.ident[:])
                    ins.then_inc(t_done, 1)

                def value(u, j):
                    m = u.slot(j)
                    pe.wait_ge(t_low, m + 1)
                    need(pe, o_low, m)
                    if j == 0 and rope:
                        pe.wait_ge(piece_read, piece_number(u, 2))
                    jv, vv, pp = 0 if cfg.shared_kv else j, v[u.parity], probs_t[j % 2]
                    for kt in range(QT):
                        to = slice(P, S) if causal and kt else slice(0, S)
                        of = slice(kt * S, NB if kt else S)
                        for n, (a, c) in enumerate(((0, 0), (0, 1), (1, 0))):
                            ins = nc.tensor.matmul(o_bank[:, to], vv[a][:, kt, jv * P:(jv + 1) * P], pp[c][:, of],
                                                   start=(kt == 0 and n == 0), stop=(kt == QT - 1 and n == 2))
                    ins.then_inc(o_done, 1)

                def output(u, j):
                    m = u.slot(j)
                    pe.wait_ge(o_low, m + 1)
                    need(pe, y_added, m - 1)
                    if u.opens:
                        pe.wait_ge(w_low, (u.g + 1) * NW)
                    for t in range(QT):
                        ins = group_of_passes(y_bank[j % 2][:, t * C:(t + 1) * C], [
                            (lambda a: out_t[j % 2][a][:, t * P:(t + 1) * P],
                             lambda c: w[c][:, cfg.wo_at + j * C:cfg.wo_at + (j + 1) * C])])
                    ins.then_inc(y_done, 1)

                over_slots(pe, piece, value, transposed, score, output)

            @block.scalar
            def _(act):
                def split_high(g, parts):
                    for part in parts:
                        first, end, scale = cfg.parts[part]
                        act.wait_ge(w_loaded, (g + 1) * 16)
                        wait_weights_free(act, g, part)
                        nc.scalar.activation(w[0][:, first:end], staged[:, first:end], ACT.Copy, scale=float(scale))\
                            .then_inc(w_high, 1)

                split_high(0, range(NW))

                def slot_start(u, j):
                    split_high(*split_parts_at(u, j))

                def piece(u, i):
                    if cfg.pieces[i][0] == "rope":
                        return
                    wait_destination_free(act, u, i)
                    if cfg.pieces[i][1]:
                        number, source = sum_number(u, i)
                        act.wait_ge(piece_read, piece_number(u, i))
                    else:
                        source = piece_bank(u, i)
                        act.wait_ge(piece_done, piece_number(u, i))
                    for target, columns in destination(u, i, 0):
                        ins = nc.scalar.activation(target, shaped(source[:, columns], target), ACT.Copy)
                    ins.then_inc(piece_high, 1)

                def finish(u):
                    wait_moved(act, u.before())
                    act.wait_ge(sum_ready, u.n + 1)
                    nc.scalar.activation(halves[:, :, 0, :], summed[u.parity][:].rearrange("p (h c) -> p h c", h=2), ACT.Copy)\
                        .then_inc(halves_high, 1)

                def score(u, j):
                    m = u.slot(j)
                    act.wait_ge(max_ready, m + 1)
                    need(act, t_done, m - 1)
                    need(act, inv_ready, m - 1)
                    for t in range(QT):
                        width = P if causal and t == 0 else S
                        ins = nc.scalar.activation(probs[j % 2][:, t, 0:width], s_bank[j % 2][:, t * S:t * S + width],
                                                   ACT.Exp, bias=neg_max[j % 2][:, t:t + 1],
                                                   accum_out=sums[j % 2][:, t:t + 1])
                    ins.then_inc(probs_ready, 1)

                def transposed(u, j):
                    act.wait_ge(t_done, u.slot(j) + 1)
                    need(act, o_done, u.slot(j) - 1)
                    nc.scalar.activation(probs_t[j % 2][0][:], t_bank[:, 0:NB], ACT.Copy).then_inc(t_high, 1)

                def value(u, j):
                    act.wait_ge(o_done, u.slot(j) + 1)
                    need(act, y_done, u.slot(j) - 1)
                    nc.scalar.activation(out_t[j % 2][0][:], o_bank[:, 0:S], ACT.Copy).then_inc(o_high, 1)

                over_slots(act, piece, value, transposed, score, lambda u, j: None, slot_start=slot_start,
                           later_pieces_last=True, finish=finish if rope else None)

            @block.vector
            def _(dve):
                dve.wait_ge(consts_loaded, 16 * len(consts))
                if rope:
                    nc.vector.memset(sums[0][:], 0.0).then_inc(consts_ready, 1)
                else:
                    nc.vector.tensor_copy(mask_bf[:], mask[:])
                    nc.vector.tensor_scalar(scaled_position[:], position[:], float(cfg.scale), None, ALU.mult)
                    nc.vector.tensor_scalar(scaled_bias[:], bias[:, :, 0:HG], float(cfg.scale), None, ALU.mult)\
                        .then_inc(consts_ready, 1)
                dve.wait_ge(consts_ready, 1)

                def split_low(g, parts):
                    for part in parts:
                        first, end, scale = cfg.parts[part]
                        dve.wait_ge(w_high, g * NW + part + 1)
                        nc.vector.scalar_tensor_tensor(w[1][:, first:end], staged[:, first:end], float(scale),
                                                       w[0][:, first:end].bitcast(F32), ALU.mult, ALU.subtract)\
                            .then_inc(w_low, 1)

                split_low(0, range(NW))

                def slot_start(u, j):
                    split_low(*split_parts_at(u, j))

                def piece(u, i):
                    name, through_sum, _ = cfg.pieces[i]
                    p = piece_bank(u, i)
                    if not through_sum:
                        dve.wait_ge(piece_high, u.n * (NP - AHEAD) + i + 1)
                        (target, columns), (high, _) = destination(u, i, 1)[0], destination(u, i, 0)[0]
                        nc.vector.tensor_tensor(target, shaped(p[:, columns], target), high.bitcast(F32), ALU.subtract)\
                            .then_inc(piece_read, 1)
                        return
                    dve.wait_ge(piece_done, piece_number(u, i))
                    number, target = sum_number(u, i)
                    if rope:
                        need(dve, sum_ready, number)
                        for half in range(2):
                            ins = nc.vector.tensor_tensor(turned[:, half, :], p[:], tables[:, half, :], ALU.mult)
                        ins.then_inc(piece_read, 1)
                        return
                    need(dve, sum_low, number - 1)
                    for c in range(1 if name == "kv" else 2):
                        head = c + (2 if name == "q2" else 0)
                        b_ap = bias[:, bass.ds(u.g, 1), HG:HG + 1] if name == "kv" else scaled_bias[:, bass.ds(u.g, 1), head:head + 1]
                        ins = nc.vector.scalar_tensor_tensor(
                            target[:, c * S:(c + 1) * S], p[:, c * S:(c + 1) * S], b_ap.rearrange("p a c -> p (a c)"),
                            (position if name == "kv" else scaled_position)[:], ALU.add, ALU.add)
                    if name == "kv":
                        b_ap = v_bias[:, bass.ds(u.g, 1), :].to_broadcast([P, QT, P])
                        ins = nc.vector.tensor_tensor(target[:, S:2 * S].rearrange("p (a c) -> p a c", a=QT),
                                                      p[:, S:2 * S].rearrange("p (a c) -> p a c", a=QT), b_ap, ALU.add)
                    ins.then_inc(piece_read, 1)

                def score(u, j):
                    m = u.slot(j)
                    dve.wait_ge(scores_done, m + 1)
                    need(dve, probs_ready, m - 1)
                    s = s_bank[j % 2][:].rearrange("p (a c) -> p a c", a=QT)
                    if causal:
                        nc.vector.tensor_reduce(neg_max[j % 2][:, 0:1], s[:, 0, 0:P], AX.X, ALU.max, negate=True)
                        ins = nc.vector.tensor_reduce(neg_max[j % 2][:, 1:2], s[:, 1, :], AX.X, ALU.max, negate=True)
                    else:
                        ins = nc.vector.tensor_reduce(neg_max[j % 2][:], s, AX.X, ALU.max, negate=True)
                    ins.then_inc(max_ready, 1)

                def transposed(u, j):
                    dve.wait_ge(t_high, u.slot(j) + 1)
                    nc.vector.tensor_tensor(probs_t[j % 2][1][:], t_bank[:, 0:NB], probs_t[j % 2][0][:].bitcast(F32),
                                            ALU.subtract).then_inc(t_low, 1)

                def value(u, j):
                    dve.wait_ge(o_high, u.slot(j) + 1)
                    nc.vector.tensor_tensor(out_t[j % 2][1][:], o_bank[:, 0:S], out_t[j % 2][0][:].bitcast(F32),
                                            ALU.subtract).then_inc(o_low, 1)

                def output(u, j):
                    m = u.slot(j)
                    dve.wait_ge(probs_ready, m + 1)
                    need(dve, y_added, m - 1)
                    nc.vector.reciprocal(inv[j % 2][:], sums[j % 2][:]).then_inc(inv_ready, 1)
                    dve.wait_ge(inv_ready, m + 1)
                    dve.wait_ge(y_done, m + 1)
                    need(dve, y_added, m)
                    for t in range(QT):
                        tile = x[:, bass.ds(u.b * QT + t, 1), :].rearrange("p a c -> p (a c)")
                        ins = nc.vector.scalar_tensor_tensor(tile, y_bank[j % 2][:, t * C:(t + 1) * C],
                                                             inv[j % 2][:, t:t + 1], tile, ALU.mult, ALU.add)
                    ins.then_inc(y_added, 1)

                def finish(u):
                    dve.wait_ge(halves_high, u.n + 1)
                    nc.vector.tensor_tensor(halves[:, :, 1, :], summed[u.parity][:].rearrange("p (h c) -> p h c", h=2),
                                            halves[:, :, 0, :].bitcast(F32), ALU.subtract).then_inc(halves_low, 1)

                over_slots(dve, piece, value, transposed, score, output, slot_start=slot_start,
                           finish=finish if rope else None)

            @block.gpsimd
            def _(pool):
                def piece(u, i):
                    if not cfg.pieces[i][1]:
                        return
                    number, total = sum_number(u, i)
                    if rope:
                        pool.wait_ge(piece_read, piece_number(u, i))
                        need(pool, halves_low, number - 1)
                        nc.gpsimd.tensor_tensor(total[:].rearrange("p (h c) -> p h c", h=2), turned[:, :, 0:S],
                                                turned[:, :, S:2 * S], ALU.add).then_inc(sum_ready, 1)
                        return
                    pool.wait_ge(piece_high, u.n * NP + i + 1)
                    wait_destination_free(pool, u, i)
                    for (target, columns), (high, _) in zip(destination(u, i, 1), destination(u, i, 0)):
                        ins = nc.gpsimd.tensor_tensor(target, shaped(total[:, columns], target), high.bitcast(F32), ALU.subtract)
                    ins.then_inc(sum_low, 1)

                none = lambda *a: None
                over_slots(pool, piece, none, none, none, none)


class NarrowAttention:

    def __init__(self, heads, causal):
        self.H, self.causal = heads, causal
        self.D = C // heads
        self.rows = 4 * self.D
        self.per_tile = P // self.rows
        self.stacks = heads // self.per_tile
        self.block = 32 // self.D
        self.pair = 2 * self.block
        self.banks = heads // self.pair
        self.scale = (1 if causal else -1) / math.sqrt(self.D)
        pairs = [(kind, i) for i in range(self.stacks // 2) for kind in ("q_stack", "k_stack")]
        self.steps = [("q", 0), ("k", 0), ("v", 0)] + pairs
        self.output_slot = 7
        spaces = list(range(8, heads - 3))
        self.at = {6: [0]}
        for n in range(1, len(self.steps)):
            self.at.setdefault(spaces[(n - 1) * len(spaces) // (len(self.steps) - 1)], []).append(n)


def narrow_attention_stage(core, cfg, w_in, select_in, consts_in):
    nc, x, bank = core.nc, core.x, core.bank
    H, D, causal, NSTEP = cfg.H, cfg.D, cfg.causal, len(cfg.steps)
    p_bank, s_bank, t_bank, o_bank = bank[0:2], bank[2:4], bank[4:6], bank[6:8]
    NB = S + P if causal else QT * S
    W = KT * C
    RELATIVE = S + P

    WINDOW, AT, ONES_AT = 64, 32 - D, 64 - D
    FULL = QT * H * WINDOW
    BANKS, PAIR, ROWS = cfg.banks, cfg.pair, 32

    with Stage(core) as st:
        w = [st.sb("w", [P, 4 * W], F32R) for _ in range(2)]
        select = st.sb("select", [P, 2, 4, 2, P], F32R)
        z = [st.sb("z", [P, KT, S], F32R) for _ in range(2)]
        qk = [[st.sb("qk", [P, KT, S], F32R) for _ in range(2)] for _ in range(2)]
        stack = [[st.sb("stack", [P, cfg.stacks, S], F32R) for _ in range(2)] for _ in range(2)]
        values = [[st.sb("values", [P, QT, H, D], F32R) for _ in range(2)] for _ in range(2)]
        unit = st.sb("unit", [P, QT, PAIR, D])
        windows = [st.sb("windows", [P, FULL + WINDOW], F32R) for _ in range(2)]
        scores_space, sums_space = st.sb("scores_space", [P, 4, QT * S]), st.sb("sums_space", [P, 4, KT * S])
        staged = sums_space[:].rearrange("p a n -> p (a n)")
        select_staged = scores_space[:].rearrange("p a n -> p (a n)")
        probs = [scores_space[:, par, :].rearrange("p (t k) -> p t k", t=QT) for par in range(2)]
        probs_t = [[st.sb("probs_t", [P, NB], F32R) for _ in range(2)] for _ in range(2)]
        bound = [st.sb("bound", [P, QT]) for _ in range(2)]
        weighted = [sums_space[:, par, :] for par in range(2)]
        totals = [sums_space[:, 2 + par, :] for par in range(2)]
        inv = st.sb("inv", [P, KT * S])
        out_t = [st.sb("out_t", [P, KT, S], F32R) for _ in range(2)]
        if causal:
            mask, bias_row = st.sb("mask", [P, P]), st.sb("bias_row", [1, C])
            mask_bf, ones_row = st.sb("mask_bf", [P, P], BF16), st.sb("ones_row", [1, P])
            consts = [mask, bias_row]
        else:
            table = st.sb("table", [P, RELATIVE, D])
            neg_bias = st.sb("neg_bias", [P, RELATIVE])
            neg_scores = [scores_space[:, 2 + par, :].rearrange("p (t k) -> p t k", t=QT) for par in range(2)]
            carrier = [st.sb("carrier", [1, 1]) for _ in range(2)]
            consts = [table]

        consts_loaded, w_loaded, z_loaded = st.sem("consts_loaded"), st.sem("w_loaded"), st.sem("z_loaded")
        w_high, w_low = st.sem("w_high"), st.sem("w_low")
        select_loaded, select_ready = st.sem("select_loaded"), st.sem("select_ready")
        consts_step, consts_ready = st.sem("consts_step"), st.sem("consts_ready")
        step_done, step_high, step_read = st.sem("step_done"), st.sem("step_high"), st.sem("step_read")
        scores_done, bound_ready, probs_ready = st.sem("scores_done"), st.sem("bound_ready"), st.sem("probs_ready")
        t_done, t_high, t_low = st.sem("t_done"), st.sem("t_high"), st.sem("t_low")
        spread, windows_ready = st.sem("spread"), st.sem("windows_ready")
        o_done, o_copied, inv_ready, out_ready = st.sem("o_done"), st.sem("o_copied"), st.sem("inv_ready"), st.sem("out_ready")
        out_t_high, out_t_low = st.sem("out_t_high"), st.sem("out_t_low")
        y_done, y_added = st.sem("y_done"), st.sem("y_added")

        CHUNKS = 4
        SPLIT_SLOT, Y_SLOT = 4, cfg.output_slot

        class Batch:

            def __init__(self, i, parity, first=False, last=False):
                self.i, self.parity, self.first, self.last = i, parity, first, last
                self.b = 2 * i + parity

            def next(self):
                return Batch(self.i, 1) if self.parity == 0 else Batch(self.i + 1, 0)

            def before(self):
                return Batch(self.i, 0) if self.parity == 1 else Batch(self.i - 1, 1)

            def slot(self, h):
                return self.b * H + h

        def over_batches(eng, work):
            work(Batch(0, 0, first=True))
            work(Batch(0, 1))
            with eng.Fori(1, PAIRS - 1) as i:
                work(Batch(i, 0))
                work(Batch(i, 1))
            work(Batch(PAIRS - 1, 0))
            work(Batch(PAIRS - 1, 1, last=True))

        def over_slots(eng, step, transposed, score, value, finish, split_out, project_out,
                       invert=lambda u, n: None, score_first=False):
            start = Batch(0, 0)
            for n in range(NSTEP):
                step(start, n)
            score(start, 0)
            score(start, 1)

            def work(u):
                for h in range(H):
                    if not score_first:
                        transposed(u, h)
                    if not (u.last and h >= H - 2):
                        score(*((u, h + 2) if h < H - 2 else (u.next(), h + 2 - H)))
                    if score_first:
                        transposed(u, h)
                    if not u.last:
                        for n in cfg.at.get(h, []):
                            step(u.next(), n)
                    if h or not u.first:
                        value(*((u, h - 1) if h else (u.before(), H - 1)))
                        if h % PAIR == 0:
                            finish(*((u, h // PAIR - 1) if h else (u.before(), BANKS - 1)))
                    if not u.first:
                        if h < CHUNKS:
                            invert(u.before(), h)
                        if h == SPLIT_SLOT:
                            split_out(u.before())
                        if h == Y_SLOT:
                            project_out(u.before())

            over_batches(eng, work)
            end = Batch(PAIRS - 1, 1)
            value(end, H - 1)
            finish(end, BANKS - 1)
            for n in range(CHUNKS):
                invert(end, n)
            split_out(end)
            project_out(end)

        def as_tiles(t):
            return t.rearrange("p (k t) -> p k t", k=KT)

        def over_pairs(u, h):
            return u.b * BANKS + h // PAIR

        norm_stage(core, [(staged, w_in, w_loaded), (select_staged, select_in.rearrange("p a b c d -> p (a b c d)"), select_loaded)]
                   + [(t[:], source, consts_loaded) for t, source in zip(consts, consts_in)])

        with nc.Block() as block:

            @block.sync
            def _(sp):
                def load_z(u):
                    need(sp, step_done, (u.b - 1) * NSTEP + 3)
                    for part, source in enumerate((core.norm_t_high, core.norm_t_low)):
                        sp.dma_start(z[part][:].bitcast(F32), source[:, :, bass.ds(u.b * S, S)].bitcast(F32))\
                            .then_inc(z_loaded, 16)

                load_z(Batch(0, 0))
                over_batches(sp, lambda u: None if u.last else load_z(u.next()))

            @block.tensor
            def _(pe):
                def three_passes(out, operands, close=True):
                    n = len(operands)
                    for kt, (stationary, moving) in enumerate(operands):
                        for m, (a, c) in enumerate(((0, 0), (0, 1), (1, 0))):
                            ins = nc.tensor.matmul(out, stationary(a), moving(c), start=(kt == 0 and m == 0),
                                                   stop=(close and kt == n - 1 and m == 2))
                    return ins

                pe.wait_ge(w_low, 2)
                pe.wait_ge(select_ready, 1)
                pe.wait_ge(windows_ready, 2)
                pe.wait_ge(consts_ready, 1)

                def step(u, n):
                    kind, i = cfg.steps[n]
                    need(pe, step_read, u.b * NSTEP + max(n - 1, 0))
                    if n == 1:
                        need(pe, y_added, u.b - 1)
                    p = p_bank[n % 2]
                    norm_t = (core.norm_t_high, core.norm_t_low)
                    if kind == "v":
                        pe.wait_ge(z_loaded, (u.b + 1) * 32)
                    if kind in ("q", "k"):
                        at = 0 if kind == "q" else W
                        for c in range(KT):
                            ins = three_passes(p[:, c * S:(c + 1) * S], [
                                (lambda a, kt=kt: w[a][:, at + kt * C + c * P:at + kt * C + (c + 1) * P],
                                 lambda c_, kt=kt: norm_t[c_][:, kt, bass.ds(u.b * S, S)]) for kt in range(KT)])
                    elif kind == "v":
                        for t in range(QT):
                            ins = three_passes(p[:, t * C:(t + 1) * C], [
                                (lambda a, kt=kt: z[a][:, kt, t * P:(t + 1) * P],
                                 lambda c_, kt=kt: w[c_][:, 2 * W + kt * C:2 * W + (kt + 1) * C]) for kt in range(KT)])
                    else:
                        which = 0 if kind == "q_stack" else 1
                        pe.wait_ge(step_read, u.b * NSTEP + which + 1)
                        for c in range(2):
                            tile = 2 * i + c
                            for part in range(2):
                                ins = nc.tensor.matmul(p[:, c * S:(c + 1) * S], select[:, which, tile % 4, part, :],
                                                       qk[which][part][:, tile // 4, :], start=(part == 0), stop=(part == 1))
                    ins.then_inc(step_done, 1)

                def score(u, h):
                    m = u.slot(h)
                    tile, row = h // cfg.per_tile, (h % cfg.per_tile) * cfg.rows
                    if tile % 2 == 0 and row == 0:
                        pe.wait_ge(step_read, u.b * NSTEP + cfg.steps.index(("k_stack", tile // 2)) + 1)
                    need(pe, probs_ready, m - 1)
                    rows = slice(row, row + cfg.rows)
                    qs, ks = stack[0][u.parity], stack[1][u.parity]
                    for t in range(QT):
                        width = P if causal and t == 0 else S
                        ins = nc.tensor.matmul(s_bank[h % 2][:, t * S:t * S + width], qs[rows, tile, t * P:(t + 1) * P],
                                               ks[rows, tile, 0:width], start=True, stop=not causal)
                        if causal:
                            at = t * (S + P)
                            ins = nc.tensor.matmul(s_bank[h % 2][:, at:at + P], core.ident_bf[:], mask_bf[:],
                                                   start=False, stop=True)
                    ins.then_inc(scores_done, 1)

                def transposed(u, h):
                    pe.wait_ge(probs_ready, u.slot(h) + 1)
                    need(pe, t_low, u.slot(h) - 1)
                    for kt in range(QT):
                        for t in range(kt if causal else 0, QT):
                            at = kt * S + t * P - (P if causal and kt else 0)
                            ins = nc.tensor.transpose(t_bank[h % 2][:, at:at + P], probs[h % 2][:, t, kt * P:(kt + 1) * P],
                                                      core.ident[:])
                    ins.then_inc(t_done, 1)

                def value(u, h):
                    pe.wait_ge(t_low, u.slot(h) + 1)
                    if h % PAIR == 0:
                        need(pe, o_copied, over_pairs(u, h) - 1)
                        pe.wait_ge(spread, over_pairs(u, h) + 1)
                    block, inner = h // cfg.block, h % cfg.block
                    at_bank = (block % 2) * S
                    for kt in range(QT):
                        to = slice(at_bank + (P if causal and kt else 0), at_bank + S)
                        of = slice(kt * S, NB if kt else S)
                        at = (kt * H + h) * WINDOW + AT - inner * D
                        for n, (a, c) in enumerate(((0, 0), (0, 1), (1, 0))):
                            ins = nc.tensor.matmul(
                                o_bank[(block // 2) % 2][0:WINDOW, to], windows[a][:, at:at + WINDOW], probs_t[h % 2][c][:, of],
                                start=(inner == 0 and kt == 0 and n == 0),
                                stop=(inner == cfg.block - 1 and kt == QT - 1 and n == 2))
                    ins.then_inc(o_done, 1)

                def project_out(u):
                    pe.wait_ge(out_t_low, u.b + 1)
                    ends = isinstance(u.i, int) and u.b == B - 1
                    pe.wait_ge(step_read, (u.b + (1 if ends else 2)) * NSTEP)
                    for t in range(QT):
                        to = p_bank[1][:, t * C:(t + 1) * C]
                        ins = three_passes(to, [
                            (lambda a, kt=kt: out_t[a][:, kt, t * P:(t + 1) * P],
                             lambda c_, kt=kt: w[c_][:, 3 * W + kt * C:3 * W + (kt + 1) * C]) for kt in range(KT)],
                            close=not causal)
                        if causal:
                            ins = nc.tensor.matmul(to, ones_row[:], bias_row[:], start=False, stop=True)
                    ins.then_inc(y_done, 1)

                over_slots(pe, step, transposed, score, value, lambda u, bp: None, lambda u: None, project_out)

            @block.scalar
            def _(act):
                act.wait_ge(w_loaded, 16)
                nc.scalar.activation(w[0][:, 0:W], staged[:, 0:W], ACT.Copy, scale=float(cfg.scale)).then_inc(w_high, 1)
                nc.scalar.activation(w[0][:, W:4 * W], staged[:, W:4 * W], ACT.Copy).then_inc(w_high, 1)
                act.wait_ge(select_loaded, 16)
                nc.scalar.activation(select[:].rearrange("p a b c d -> p (a b c d)"), select_staged, ACT.Copy).then_inc(select_ready, 1)

                def step(u, n):
                    kind, i = cfg.steps[n]
                    if kind == "v":
                        act.wait_ge(step_done, u.b * NSTEP + n + 1)
                        need(act, spread, (u.b - 1) * BANKS)
                        nc.scalar.activation(values[u.parity][0][:], p_bank[n % 2][:].rearrange("p (t h d) -> p t h d", t=QT, h=H),
                                             ACT.Copy).then_inc(step_high, 1)
                    elif n < 2:
                        act.wait_ge(step_done, u.b * NSTEP + n + 1)
                        need(act, step_done, u.b * NSTEP)
                        nc.scalar.activation(qk[n][0][:], p_bank[n][:].rearrange("p (k t) -> p k t", k=KT), ACT.Copy)\
                            .then_inc(step_high, 1)

                def score(u, h):
                    m = u.slot(h)
                    act.wait_ge(bound_ready, m + 1)
                    need(act, t_done, m - 1)
                    for t in range(QT):
                        width = P if causal and t == 0 else S
                        source = s_bank[h % 2][:, t * S:t * S + width] if causal else neg_scores[h % 2][:, t, :]
                        ins = nc.scalar.activation(probs[h % 2][:, t, 0:width], source, ACT.Exp,
                                                   bias=bound[h % 2][:, t:t + 1], scale=1.0 if causal else -1.0)
                    ins.then_inc(probs_ready, 1)

                def transposed(u, h):
                    act.wait_ge(t_done, u.slot(h) + 1)
                    need(act, o_done, u.slot(h) - 1)
                    nc.scalar.activation(probs_t[h % 2][0][:], t_bank[h % 2][:, 0:NB], ACT.Copy).then_inc(t_high, 1)

                def finish(u, bp):
                    act.wait_ge(o_done, u.b * H + (bp + 1) * PAIR)
                    if bp == 0:
                        need(act, out_t_low, u.b - 1)
                    rows = slice(bp * ROWS, (bp + 1) * ROWS)
                    nc.scalar.activation(weighted[u.parity][rows, :], o_bank[bp % 2][0:ROWS, :], ACT.Copy)
                    nc.scalar.activation(totals[u.parity][rows, :], o_bank[bp % 2][ROWS:2 * ROWS, :], ACT.Copy)\
                        .then_inc(o_copied, 1)

                def split_out(u):
                    act.wait_ge(out_ready, u.b + 1)
                    need(act, y_done, u.b)
                    nc.scalar.activation(out_t[0][:], as_tiles(weighted[u.parity]), ACT.Copy).then_inc(out_t_high, 1)

                none = lambda *a: None
                over_slots(act, step, transposed, score, none, finish, split_out, none)

            @block.vector
            def _(dve):
                for n, (first, end, scale) in enumerate(((0, W, cfg.scale), (W, 4 * W, 1.0))):
                    dve.wait_ge(w_high, n + 1)
                    nc.vector.scalar_tensor_tensor(w[1][:, first:end], staged[:, first:end], float(scale),
                                                   w[0][:, first:end].bitcast(F32), ALU.mult, ALU.subtract).then_inc(w_low, 1)
                dve.wait_ge(consts_loaded, 16 * len(consts))
                if causal:
                    nc.vector.memset(ones_row[:], 1.0)
                    nc.vector.tensor_copy(mask_bf[:], mask[:]).then_inc(consts_ready, 1)
                else:
                    nc.vector.tensor_reduce(neg_bias[:], table[:], AX.X, ALU.add, negate=True).then_inc(consts_step, 1)
                    dve.wait_ge(consts_step, 1)
                    nc.vector.tensor_scalar(neg_bias[:], neg_bias[:], 1.0 / D, None, ALU.mult).then_inc(consts_ready, 1)
                    dve.wait_ge(consts_ready, 1)

                def step(u, n):
                    kind, i = cfg.steps[n]
                    dve.wait_ge(step_done, u.b * NSTEP + n + 1)
                    p = p_bank[n % 2]
                    if kind in ("q", "k"):
                        dve.wait_ge(step_high, u.b * 3 + n + 1)
                        nc.vector.tensor_tensor(qk[n][1][:], p[:].rearrange("p (k t) -> p k t", k=KT),
                                                qk[n][0][:].bitcast(F32), ALU.subtract).then_inc(step_read, 1)
                    elif kind == "v":
                        dve.wait_ge(step_high, u.b * 3 + n + 1)
                        high, low = values[u.parity]
                        nc.vector.tensor_tensor(low[:], p[:].rearrange("p (t h d) -> p t h d", t=QT, h=H),
                                                high[:].bitcast(F32), ALU.subtract).then_inc(step_read, 1)
                    else:
                        need(dve, scores_done, (u.b - 1) * H)
                        target = stack[0 if kind == "q_stack" else 1][u.parity]
                        nc.vector.tensor_copy(target[:, 2 * i:2 * i + 2, :], p[:].rearrange("p (k t) -> p k t", k=2))\
                            .then_inc(step_read, 1)

                def score(u, h):
                    m = u.slot(h)
                    dve.wait_ge(scores_done, m + 1)
                    need(dve, probs_ready, m - 1)
                    if not causal:
                        nc.vector.memset(carrier[h % 2][:], 0.0)
                    for t in range(QT):
                        width = P if causal and t == 0 else S
                        s = s_bank[h % 2][:, t * S:t * S + width]
                        if causal:
                            ins = nc.vector.tensor_reduce(bound[h % 2][:, t:t + 1], s, AX.X, ALU.max, negate=True)
                        else:
                            at = P * (1 - t)
                            ins = nc.vector.tensor_tensor_reduce(
                                out=neg_scores[h % 2][:, t, :], in0=s, in1=neg_bias[:, at:at + S], scale=1.0, scalar=BIG,
                                op0=ALU.add, op1=ALU.min, accum_out=bound[h % 2][:, t:t + 1])
                    ins.then_inc(bound_ready, 1)

                def transposed(u, h):
                    dve.wait_ge(t_high, u.slot(h) + 1)
                    nc.vector.tensor_tensor(probs_t[h % 2][1][:], t_bank[h % 2][:, 0:NB], probs_t[h % 2][0][:].bitcast(F32),
                                            ALU.subtract).then_inc(t_low, 1)

                def invert(u, n):
                    dve.wait_ge(o_copied, (u.b + 1) * BANKS)
                    if n == 0:
                        need(dve, out_ready, u.b)
                    at = slice(n * KT * S // CHUNKS, (n + 1) * KT * S // CHUNKS)
                    nc.vector.reciprocal(inv[:, at], totals[u.parity][:, at]).then_inc(inv_ready, 1)
                    if n == CHUNKS - 1:
                        dve.wait_ge(inv_ready, (u.b + 1) * CHUNKS)
                        nc.vector.tensor_tensor(weighted[u.parity][:], weighted[u.parity][:], inv[:], ALU.mult).then_inc(out_ready, 1)

                def split_out(u):
                    dve.wait_ge(out_t_high, u.b + 1)
                    nc.vector.tensor_tensor(out_t[1][:], as_tiles(weighted[u.parity]), out_t[0][:].bitcast(F32), ALU.subtract).then_inc(out_t_low, 1)

                def project_out(u):
                    dve.wait_ge(y_done, u.b + 1)
                    tiles = x[:, bass.ds(u.b * QT, QT), :]
                    nc.vector.tensor_tensor(tiles, p_bank[1][:].rearrange("p (t c) -> p t c", t=QT), tiles, ALU.add)\
                        .then_inc(y_added, 1)

                over_slots(dve, step, transposed, score, lambda u, h: None, lambda u, bp: None, split_out, project_out,
                           invert=invert, score_first=True)

            @block.gpsimd
            def _(pool):
                def of_heads(t, first, columns):
                    return t[:, 0:FULL].rearrange("p (t h w) -> p t h w", t=QT, w=WINDOW)[:, :, first[0]:first[1], columns:columns + D]

                nc.gpsimd.memset(unit[:], 1.0)
                for part in range(2):
                    ins = nc.gpsimd.memset(windows[part][:].bitcast(F32), 0.0)
                ins.then_inc(windows_ready, 1)
                pool.wait_ge(windows_ready, 1)
                nc.gpsimd.memset(of_heads(windows[0], (0, H), ONES_AT).bitcast(F32), 1.0).then_inc(windows_ready, 1)
                pool.wait_ge(windows_ready, 2)

                def work(u):
                    for bp in range(BANKS):
                        heads = (bp * PAIR, (bp + 1) * PAIR)
                        if bp == 0:
                            pool.wait_ge(step_read, u.b * NSTEP + 3)
                        need(pool, o_done, (u.b - 1) * H + heads[1])
                        for part in range(2):
                            source = values[u.parity][part][:, :, heads[0]:heads[1], :].bitcast(F32)
                            ins = nc.gpsimd.tensor_tensor(of_heads(windows[part], heads, AT), source, unit[:], ALU.mult)
                        ins.then_inc(spread, 1)

                over_batches(pool, work)


HALF_ROWS = P // 2


class Experts:

    def __init__(self, experts, top, groups, gated, act, router, capacity=None):
        self.E, self.top, self.NG, self.gated, self.act = experts, top, groups, gated, act
        self.router, self.capacity = router, capacity
        self.up = (2 if gated else 1) * KT * P
        self.down_at = self.up
        self.pick_at = self.up + C
        self.ones_row = experts < HALF_ROWS
        self.width = self.pick_at + P


def route_stage(core, cfg, w_in, gates_t, consts_in, early_loads):
    nc, bank, E = core.nc, core.bank, cfg.E
    FILL = 8 - cfg.top
    CHUNK = 512
    NC_ = TILES * P // CHUNK
    TC = CHUNK // P
    GROUPS_OF = 4 if cfg.router == "limited" else 0
    with Stage(core) as st:
        staged = st.sb("staged", [P, KT, E])
        w = [st.sb("w", [P, KT, E], F32R) for _ in range(2)]
        logits_t = [st.sb("logits_t", [E, CHUNK]) for _ in range(2)]
        logits = st.sb("logits", [P, TILES, E])
        scored = st.sb("scored", [P, TILES, E])
        padded = st.sb("padded", [P, TILES, E + FILL])
        replaced = st.sb("replaced", [P, TILES, E + FILL])
        best = st.sb("best", [P, TILES, 8])
        chosen = st.sb("chosen", [P, TILES, E])
        total, inv, tile_max = (st.sb(n, [P, TILES]) for n in ("total", "inv", "tile_max"))
        gates = st.sb("gates", [P, TILES, P])
        w_loaded, w_high, w_low = st.sem("w_loaded"), st.sem("w_high"), st.sem("w_low")
        t_done, t_copied = st.sem("t_done"), st.sem("t_copied")
        logits_done, logits_ready = st.sem("logits_done"), st.sem("logits_ready")
        scored_ready, chain, gates_ready = st.sem("scored_ready"), st.sem("chain"), st.sem("gates_ready")
        g_done, g_high, g_low = st.sem("g_done"), st.sem("g_high"), st.sem("g_low")
        shifted_ready = st.sem("shifted_ready")
        if cfg.capacity:
            before = st.sb("before", [P, P])
            before_bf, ones_bf = st.sb("before_bf", [P, P], BF16), st.sb("ones_bf", [P, P], BF16)
            chosen_bf, earlier_bf = st.sb("chosen_bf", [P, TILES, E], BF16), st.sb("earlier_bf", [P, TILES, E], BF16)
            chosen_ready, position_done = st.sem("chosen_ready"), st.sem("position_done")
        if GROUPS_OF:
            group_values = st.sb("group_values", [P, TILES, 8 + 6])
            group_replaced = st.sb("group_replaced", [P, TILES, 8 + 6])
            group_chosen = st.sb("group_chosen", [P, TILES, GROUPS_OF])

        norm_stage(core, [(staged[:], w_in, w_loaded)] + ([(before[:], consts_in[0], w_loaded)] if cfg.capacity else [])
                   + early_loads)

        with nc.Block() as block:

            @block.tensor
            def _(pe):
                pe.wait_ge(w_low, 1)

                def project(c, par):
                    need(pe, t_copied, c - 1)
                    n = 0
                    for kt in range(KT):
                        for a, m in ((0, 0), (0, 1), (1, 0)):
                            zz = (core.norm_t_high, core.norm_t_low)[m]
                            ins = nc.tensor.matmul(bank[par][0:E, :], w[a][:, kt, :], zz[:, kt, bass.ds(c * CHUNK, CHUNK)],
                                                   start=(n == 0), stop=(n == 5))
                            n += 1
                    ins.then_inc(t_done, 1)

                def back(c, par):
                    pe.wait_ge(t_copied, c + 1)
                    need(pe, logits_ready, c - 1)
                    for t in range(TC):
                        ins = nc.tensor.transpose(bank[2 + par][:, t * E:(t + 1) * E], logits_t[par][:, t * P:(t + 1) * P],
                                                  core.ident[0:E, 0:E])
                    ins.then_inc(logits_done, 1)

                for c in range(NC_):
                    project(c, c % 2)
                    back(c, c % 2)
                if cfg.capacity:
                    pe.wait_ge(chosen_ready, 1)
                    for t in range(TILES):
                        to = bank[4 + t // 8][:, (t % 8) * E:(t % 8 + 1) * E]
                        nc.tensor.matmul(to, before_bf[:], chosen_bf[:, t, :], start=True, stop=False)
                        ins = nc.tensor.matmul(to, ones_bf[:], earlier_bf[:, t, :], start=False, stop=True)
                    ins.then_inc(position_done, 1)
                pe.wait_ge(gates_ready, 1)
                for t in range(TILES):
                    b = t // 4
                    need(pe, g_low, b - 1)
                    ins = nc.tensor.transpose(bank[b % 2][:, (t % 4) * P:(t % 4 + 1) * P], gates[:, t, :], core.ident[:])
                    if t % 4 == 3:
                        ins.then_inc(g_done, 1)

            @block.scalar
            def _(act):
                act.wait_ge(w_loaded, 16 * (2 if cfg.capacity else 1))
                nc.scalar.activation(w[0][:], staged[:], ACT.Copy).then_inc(w_high, 1)
                for c in range(NC_):
                    act.wait_ge(t_done, c + 1)
                    need(act, logits_done, c - 1)
                    nc.scalar.activation(logits_t[c % 2][:], bank[c % 2][0:E, :], ACT.Copy).then_inc(t_copied, 1)
                if cfg.router == "softmax":
                    act.wait_ge(shifted_ready, 1)
                    nc.scalar.activation(scored[:], scored[:], ACT.Exp).then_inc(scored_ready, 1)
                else:
                    act.wait_ge(logits_ready, NC_)
                    nc.scalar.activation(scored[:], logits[:], ACT.Sigmoid).then_inc(scored_ready, 1)
                for b in range(TILES // 4):
                    act.wait_ge(g_done, b + 1)
                    nc.scalar.activation(gates_t[:, b * 512:(b + 1) * 512], bank[b % 2][:], ACT.Copy).then_inc(g_high, 1)

            @block.vector
            def _(dve):
                steps = [0]

                def after(ins):
                    steps[0] += 1
                    ins.then_inc(chain, 1)
                    dve.wait_ge(chain, steps[0])

                def spread(t, n):
                    return t.rearrange("p (t a) -> p t a", a=1).to_broadcast([P, TILES, n])

                def choose(values, without, chosen_of, n, k):
                    low = max(n, 8)
                    for t in range(TILES):
                        ins = nc.vector.max(best[:, t, :], values[:, t, 0:low])
                    after(ins)
                    after(nc.vector.tensor_copy(best[:, :, k:8], values[:, :, low:low + 8 - k]))
                    for t in range(TILES):
                        ins = nc.vector.match_replace(without[:, t, :], best[:, t, :], values[:, t, :], -BIG)
                    after(ins)
                    after(nc.vector.tensor_tensor(chosen_of[:], without[:, :, 0:n], values[:, :, 0:n], ALU.not_equal))

                dve.wait_ge(w_high, 1)
                nc.vector.tensor_tensor(w[1][:], staged[:], w[0][:].bitcast(F32), ALU.subtract).then_inc(w_low, 1)
                after(nc.vector.memset(gates[:], 0.0))
                nc.vector.memset(padded[:], BIG)
                if GROUPS_OF:
                    after(nc.vector.memset(group_values[:], BIG))
                    nc.vector.memset(group_values[:, :, GROUPS_OF:8], -BIG)
                if cfg.ones_row:
                    nc.vector.memset(gates[:, :, E:E + 1], 1.0)
                for c in range(NC_):
                    dve.wait_ge(logits_done, c + 1)
                    nc.vector.tensor_copy(logits[:, c * TC:(c + 1) * TC, :],
                                          bank[2 + c % 2][:, 0:TC * E].rearrange("p (t e) -> p t e", t=TC)).then_inc(logits_ready, 1)
                dve.wait_ge(logits_ready, NC_)
                if cfg.router == "softmax":
                    after(nc.vector.tensor_reduce(tile_max[:], logits[:], AX.X, ALU.max))
                    nc.vector.tensor_tensor(scored[:], logits[:], spread(tile_max[:], E), ALU.subtract).then_inc(shifted_ready, 1)
                if GROUPS_OF:
                    after(nc.vector.tensor_reduce(group_values[:, :, 0:GROUPS_OF],
                                                  logits[:].rearrange("p t (g n) -> p t g n", g=GROUPS_OF), AX.X, ALU.max))
                    choose(group_values, group_replaced, group_chosen, GROUPS_OF, 2)
                    after(nc.vector.tensor_scalar(group_chosen[:], group_chosen[:], -MASKED, MASKED, ALU.mult, ALU.add))
                    after(nc.vector.tensor_tensor(
                        padded[:, :, 0:E].rearrange("p t (g n) -> p t g n", g=GROUPS_OF),
                        logits[:].rearrange("p t (g n) -> p t g n", g=GROUPS_OF),
                        group_chosen[:].rearrange("p t (g a) -> p t g a", a=1).to_broadcast([P, TILES, GROUPS_OF, E // GROUPS_OF]),
                        ALU.add))
                else:
                    after(nc.vector.tensor_copy(padded[:, :, 0:E], logits[:]))
                choose(padded, replaced, chosen, E, cfg.top)
                if cfg.capacity:
                    nc.vector.tensor_copy(before_bf[:], before[:])
                    nc.vector.memset(ones_bf[:], 1.0)
                    after(nc.vector.memset(earlier_bf[:, 0, :], 0.0))
                    after(nc.vector.tensor_copy(chosen_bf[:], chosen[:]))
                    for t in range(1, TILES):
                        ins = nc.vector.tensor_tensor(earlier_bf[:, t, :], earlier_bf[:, t - 1, :], chosen_bf[:, t - 1, :], ALU.add)
                        if t < TILES - 1:
                            after(ins)
                    ins.then_inc(chosen_ready, 1)
                dve.wait_ge(scored_ready, 1)
                if cfg.router == "softmax":
                    after(nc.vector.tensor_reduce(total[:], scored[:], AX.X, ALU.add))
                    after(nc.vector.tensor_tensor(chosen[:], chosen[:], scored[:], ALU.mult))
                else:
                    after(nc.vector.tensor_tensor(chosen[:], chosen[:], scored[:], ALU.mult))
                    after(nc.vector.tensor_reduce(total[:], chosen[:], AX.X, ALU.add))
                after(nc.vector.reciprocal(inv[:], total[:]))
                if cfg.capacity:
                    after(nc.vector.tensor_tensor(chosen[:], chosen[:], spread(inv[:], E), ALU.mult))
                    dve.wait_ge(position_done, 1)
                    for half, at in ((0, 0), (1, 0), (0, HALF_ROWS), (1, HALF_ROWS)):
                        rows = slice(8 * half, 8 * half + 8)
                        ins = nc.vector.scalar_tensor_tensor(
                            gates[:, rows, at:at + E], bank[4 + half][:].rearrange("p (t e) -> p t e", e=E), float(cfg.capacity),
                            chosen[:, rows, :], ALU.is_lt, ALU.mult)
                    ins.then_inc(gates_ready, 1)
                else:
                    for at in (0, HALF_ROWS):
                        ins = nc.vector.tensor_tensor(gates[:, :, at:at + E], chosen[:], spread(inv[:], E), ALU.mult)
                    ins.then_inc(gates_ready, 1)
                for b in range(TILES // 4):
                    dve.wait_ge(g_high, b + 1)
                    at = slice(b * 512, (b + 1) * 512)
                    low = gates_t[HALF_ROWS:P, at]
                    nc.vector.tensor_tensor(low, bank[b % 2][HALF_ROWS:P, :], low.bitcast(F32), ALU.subtract).then_inc(g_low, 1)


def experts_stage(core, cfg, w_in, gates_t, staged, w_loaded):
    nc, x, bank, NG = core.nc, core.x, core.bank, cfg.NG
    HALF, STEP = TILES * P // 2, 512
    a_bank, up_bank, pick_bank, y_bank = bank[0:2], bank[2], bank[3], bank[4:8]
    with Stage(core) as st:
        w_high = [st.sb("w_high", [P, cfg.width], F32R) for _ in range(2)]
        w_low = [st.sb("w_low", [P, cfg.pick_at], F32R) for _ in range(2)]
        acted, hidden = ([st.sb(name, [P, STEP]) for _ in range(2)] for name in ("acted", "hidden"))
        hidden_parts = [[st.sb("hidden_parts", [P, STEP], F32R) for _ in range(2)] for _ in range(2)]
        zeros = st.sb("zeros", [P, STEP], BF16)
        ones = st.sb("ones", [1, STEP], BF16)
        high_ready, low_ready, zeros_ready = st.sem("high_ready"), st.sem("low_ready"), st.sem("zeros_ready")
        a_done, up_done, pick_done = st.sem("a_done"), st.sem("up_done"), st.sem("pick_done")
        acted_ready, gated_ready, hidden_ready = st.sem("acted_ready"), st.sem("gated_ready"), st.sem("hidden_ready")
        hidden_high, hidden_low = st.sem("hidden_high"), st.sem("hidden_low")
        down_done, y_done, y_read = st.sem("down_done"), st.sem("y_done"), st.sem("y_read")

        class Group:

            def __init__(self, c, i, k):
                self.c, self.i, self.k = c, i, k
                self.j = 2 * i + k
                self.u = c * NG + self.j
                self.parity = (c * NG + k) % 2
                self.turn = i + (c * NG + k) // 2
                known = isinstance(i, int)
                self.first, self.last = known and self.j == 0, known and self.j == NG - 1
                self.very_last = self.last and c == 1

            def next(self):
                return Group(self.c + 1, 0, 0) if self.last else Group(self.c, self.i, self.k + 1)

            def before(self):
                return Group(self.c - 1, 0, NG - 1) if self.first else Group(self.c, self.i, self.k - 1)

            def step(self, s):
                return 2 * self.u + s

        def over_groups(eng, work):
            for c in range(2):
                work(Group(c, 0, 0))
                pairs = (NG - 2) // 2
                with eng.Fori(0, pairs) as i:
                    work(Group(c, i, 1))
                    work(Group(c, i, 2))
                for k in range(2 * pairs + 1, NG):
                    work(Group(c, 0, k))

        with nc.Block() as block:

            @block.sync
            def _(sp):
                def work(g):
                    if not g.very_last:
                        need(sp, low_ready, g.u)
                        source = w_in[0] if g.last else w_in[bass.ds(g.j + 1, 1)].rearrange("a p n -> p (a n)")
                        sp.dma_start(staged[1 - g.parity][:], source).then_inc(w_loaded[1 - g.parity], 16)

                over_groups(sp, work)

            @block.tensor
            def _(pe):
                def passes(out, operands, start=True, stop=True):
                    n = len(operands)
                    for i, (a, c) in enumerate(operands):
                        ins = nc.tensor.matmul(out, a, c, start=(start and i == 0), stop=(stop and i == n - 1))
                    return ins

                z = (core.norm_t_high, core.norm_t_low)

                def up(g, s):
                    r = g.step(s)
                    if s == 0:
                        pe.wait_ge(low_ready, g.u + 1)
                    tokens = slice(g.c * HALF + s * STEP, g.c * HALF + (s + 1) * STEP)
                    w = (w_high[g.parity], w_low[g.parity])

                    def product(out, at):
                        return passes(out, [(w[a][:, at + kt * P:at + (kt + 1) * P], z[b][:, kt, tokens])
                                            for kt in range(KT) for a, b in ((0, 0), (0, 1), (1, 0))])

                    need(pe, acted_ready, r - 1)
                    product(a_bank[s][:], 0).then_inc(a_done, 1)
                    if cfg.gated:
                        need(pe, gated_ready, r)
                        product(up_bank[:], KT * P).then_inc(up_done, 1)
                    need(pe, hidden_ready, r)
                    if g.last and not cfg.ones_row:
                        pick = (ones[:, 0:P], ones[:])
                    else:
                        pick = (w[0][:, cfg.pick_at:cfg.pick_at + P], gates_t[:, tokens])
                    passes(pick_bank[:], [pick]).then_inc(pick_done, 1)

                def down(g, s):
                    r = g.step(s)
                    pe.wait_ge(hidden_low, r + 1)
                    if g.first and s == 0:
                        need(pe, y_read, g.c)
                        for y in y_bank:
                            nc.tensor.matmul(y[:], zeros[:, 0:P], zeros[:], start=True, stop=False)
                    for t in range(STEP // P):
                        y = y_bank[2 * s + t // 2][:, (t % 2) * C:(t % 2 + 1) * C]
                        tokens = slice(t * P, (t + 1) * P)
                        ins = passes(y, [(hidden_parts[s][a][:, tokens],
                                          (w_high, w_low)[b][g.parity][:, cfg.down_at:cfg.down_at + C])
                                         for a, b in ((0, 0), (0, 1), (1, 0))], start=False, stop=False)
                    ins.then_inc(down_done, 1)
                    if g.last and s == 1:
                        for y in y_bank:
                            ins = nc.tensor.matmul(y[:], zeros[:, 0:P], zeros[:], start=False, stop=True)
                        ins.then_inc(y_done, 1)

                pe.wait_ge(zeros_ready, 1)

                def work(g):
                    up(g, 0)
                    if not (g.first and g.c == 0):
                        down(g.before(), 1)
                    up(g, 1)
                    down(g, 0)

                over_groups(pe, work)
                down(Group(1, 0, NG - 1), 1)

            @block.scalar
            def _(act):
                def split(g):
                    act.wait_ge(w_loaded[g.parity], (g.turn + 1) * 16)
                    need(act, down_done, 2 * (g.u - 1))
                    nc.scalar.activation(w_high[g.parity][:], staged[g.parity][:], ACT.Copy).then_inc(high_ready, 1)

                split(Group(0, 0, 0))

                def work(g):
                    for s in range(2):
                        r = g.step(s)
                        act.wait_ge(a_done, r + 1)
                        need(act, hidden_ready, r - 1)
                        nc.scalar.activation(acted[s][:], a_bank[s][:], cfg.act).then_inc(acted_ready, 1)
                        act.wait_ge(hidden_ready, r + 1)
                        need(act, down_done, r - 1)
                        nc.scalar.activation(hidden_parts[s][0][:], hidden[s][:], ACT.Copy).then_inc(hidden_high, 1)
                        if s == 0 and not g.very_last:
                            split(g.next())

                over_groups(act, work)

            @block.vector
            def _(dve):
                nc.vector.memset(ones[:], 1.0)
                nc.vector.memset(zeros[:], 0.0).then_inc(zeros_ready, 1)

                def split(g):
                    dve.wait_ge(high_ready, g.u + 1)
                    nc.vector.tensor_tensor(w_low[g.parity][:], staged[g.parity][:, 0:cfg.pick_at],
                                            w_high[g.parity][:, 0:cfg.pick_at].bitcast(F32), ALU.subtract).then_inc(low_ready, 1)

                split(Group(0, 0, 0))

                def add_to_x(c):
                    dve.wait_ge(y_done, c + 1)
                    for i, y in enumerate(y_bank):
                        tile = c * TILES // 2 + 2 * i
                        tiles = x[:, tile:tile + 2, :]
                        ins = nc.vector.tensor_tensor(tiles, y[:].rearrange("p (t c) -> p t c", t=2), tiles, ALU.add)
                    ins.then_inc(y_read, 1)

                def work(g):
                    for s in range(2):
                        r = g.step(s)
                        dve.wait_ge(acted_ready, r + 1)
                        source = acted[s]
                        need(dve, hidden_high, r - 1)
                        need(dve, hidden_low, r - 1)
                        if cfg.gated:
                            dve.wait_ge(up_done, r + 1)
                            nc.vector.tensor_tensor(hidden[s][:], acted[s][:], up_bank[:], ALU.mult).then_inc(gated_ready, 1)
                            dve.wait_ge(gated_ready, r + 1)
                            source = hidden[s]
                        dve.wait_ge(pick_done, r + 1)
                        nc.vector.tensor_tensor(hidden[s][:], source[:], pick_bank[:], ALU.mult).then_inc(hidden_ready, 1)
                        if s == 1 and g.first and g.c == 1:
                            add_to_x(0)
                        dve.wait_ge(hidden_high, r + 1)
                        dve.wait_ge(hidden_ready, r + 1)
                        nc.vector.tensor_tensor(hidden_parts[s][1][:], hidden[s][:], hidden_parts[s][0][:].bitcast(F32),
                                                ALU.subtract).then_inc(hidden_low, 1)
                        if s == 0 and not g.very_last:
                            split(g.next())

                over_groups(dve, work)
                add_to_x(1)


def thought_stage(core, w_in, gate_w_in, rows_in, columns_in, wide_rows_in, steps=4, hidden=1024, eps=1e-6):
    nc, x, bank = core.nc, core.x, core.bank
    HB = hidden // P
    AGG, BC, D1, D2 = 0, KT * C, 2 * KT * C, 2 * KT * C + KT * hidden
    with Stage(core) as st:
        w = st.sb("w", [P, D2 + HB * C])
        gate_staged = st.sb("gate_staged", [P, KT, C])
        gate_w = [st.sb("gate_w", [P, KT, C], F32R) for _ in range(2)]
        rows = st.sb("rows", [B, 6, C])
        columns = st.sb("columns", [P, HB + 2 * KT])
        wide_rows = st.sb("wide_rows", [P, 2, C])
        gate = st.sb("gate", [P, KT, TILES * P])
        last, current, thought, thought_bias = (st.sb(n, [B, C]) for n in ("last", "current", "thought", "thought_bias"))
        stats8, meanvar8, rstd8 = st.sb("stats8", [B, 6]), st.sb("meanvar8", [B, 2]), st.sb("rstd8", [B, 1])
        half8, half = st.sb("half8", [B, 1]), st.sb("half", [P, QT])
        var8, eps_tile = st.sb("var8", [B, 1]), st.sb("eps_tile", [P, QT])
        carrier = [st.sb("carrier", [1, 1]) for _ in range(2)]
        current_t, act_in, acted = st.sb("current_t", [P, KT, B]), st.sb("act_in", [P, HB, B]), st.sb("acted", [P, HB, B])
        message_t = st.sb("message_t", [P, KT, B])
        sent = [st.sb("sent", [P, KT, S]) for _ in range(2)]
        mixed = [st.sb("mixed", [P, QT, C]) for _ in range(2)]
        stats = [st.sb("stats", [P, QT, 6]) for _ in range(2)]
        meanvar = [st.sb("meanvar", [P, QT, 2]) for _ in range(2)]
        var_eps, rstd, shift = ([st.sb(n, [P, QT]) for _ in range(2)] for n in ("var_eps", "rstd", "shift"))

        loaded, last_loaded = st.sem("loaded"), st.sem("last_loaded")
        gate_high, gate_low, gate_done, gate_ready = st.sem("gate_high"), st.sem("gate_low"), st.sem("gate_done"), st.sem("gate_ready")
        chain, var8_ready, rstd8_ready, pool_chain = st.sem("chain"), st.sem("var8_ready"), st.sem("rstd8_ready"), st.sem("pool_chain")
        current_ready, current_t_done, current_t_ready = st.sem("current_ready"), st.sem("current_t_done"), st.sem("current_t_ready")
        product_done, act_in_ready, acted_ready = st.sem("product_done"), st.sem("act_in_ready"), st.sem("acted_ready")
        message_ready, sent_ready, sent_t_done, mixed_ready = st.sem("message_ready"), st.sem("sent_ready"), st.sem("sent_t_done"), st.sem("mixed_ready")
        var_ready, rstd_ready, half_ready, tail = st.sem("var_ready"), st.sem("rstd_ready"), st.sem("half_ready"), st.sem("tail")
        ROUNDS = 3 + steps
        t_bank, wide_bank, row_bank = bank[4], bank[5], bank[6]

        norm_stage(core, [(last[:], x[P - 1:P, QT - 1::QT, :], last_loaded), (gate_staged[:], gate_w_in, last_loaded)] + [
            (t[:], source, loaded) for t, source in ((rows, rows_in), (columns, columns_in), (w, w_in), (wide_rows, wide_rows_in))])

        with nc.Block() as block:

            @block.gpsimd
            def _(pool):
                nc.gpsimd.memset(half8[:], -0.5)
                nc.gpsimd.memset(eps_tile[:], eps)
                nc.gpsimd.memset(half[:], -0.5).then_inc(half_ready, 1)
                pool.wait_ge(half_ready, 1)
                for n in range(2 + steps):
                    pool.wait_ge(var8_ready, n + 1)
                    nc.gpsimd.tensor_scalar(var8[:], meanvar8[:, 1:2], 1.0, 1e-5 if n == 0 else eps, ALU.mult, ALU.add)\
                        .then_inc(pool_chain, 1)
                    pool.wait_ge(pool_chain, n + 1)
                    nc.gpsimd.tensor_tensor(rstd8[:], var8[:], half8[:], ALU.pow).then_inc(rstd8_ready, 1)

                with pool.Fori(0, PAIRS) as i:
                    for par in range(2):
                        b = 2 * i + par
                        pool.wait_ge(var_ready, b + 1)
                        nc.gpsimd.tensor_tensor(var_eps[par][:], meanvar[par][:, :, 1], eps_tile[:], ALU.add)\
                            .then_inc(pool_chain, 1)
                        pool.wait_ge(pool_chain, 2 + steps + b + 1)
                        nc.gpsimd.tensor_tensor(rstd[par][:], var_eps[par][:], half[:], ALU.pow).then_inc(rstd_ready, 1)

            @block.tensor
            def _(pe):
                pe.wait_ge(gate_low, 1)

                def gates(i):
                    for par in range(2):
                        b = 2 * i + par
                        need(pe, gate_ready, b - 1)
                        for c in range(KT):
                            n = 0
                            for kt in range(KT):
                                for a, m in ((0, 0), (0, 1), (1, 0)):
                                    z = (core.norm_t_high, core.norm_t_low)[m]
                                    ins = nc.tensor.matmul(bank[par][:, c * S:(c + 1) * S], gate_w[a][:, kt, c * P:(c + 1) * P],
                                                           z[:, kt, bass.ds(b * S, S)], start=(n == 0), stop=(n == 5))
                                    n += 1
                        ins.then_inc(gate_done, 1)

                gates(0)
                with pe.Fori(1, PAIRS) as i:
                    gates(i)

                pe.wait_ge(loaded, 64)

                def transpose_current(n):
                    pe.wait_ge(current_ready, n + 1)
                    for kt in range(KT):
                        ins = nc.tensor.transpose(t_bank[:, kt * B:(kt + 1) * B], current[:, kt * P:(kt + 1) * P],
                                                  core.ident[0:B, 0:B])
                    ins.then_inc(current_t_done, 1)
                    pe.wait_ge(current_t_ready, n + 1)

                def by_rows(at, operands, count):
                    for kt in range(count):
                        ins = nc.tensor.matmul(row_bank[0:B, 0:C], operands[:, kt, :], w[:, at + kt * C:at + (kt + 1) * C],
                                               start=(kt == 0), stop=(kt == count - 1))
                    ins.then_inc(product_done, 1)

                def by_columns(at, width):
                    for c in range(width // P):
                        for kt in range(KT):
                            ins = nc.tensor.matmul(wide_bank[:, c * B:(c + 1) * B],
                                                   w[:, at + kt * width + c * P:at + kt * width + (c + 1) * P],
                                                   current_t[:, kt, :], start=(kt == 0), stop=(kt == KT - 1))
                    ins.then_inc(product_done, 1)

                transpose_current(0)
                by_rows(AGG, current_t, KT)
                for n in range(steps):
                    transpose_current(1 + n)
                    by_columns(D1, hidden)
                    pe.wait_ge(acted_ready, n + 1)
                    by_rows(D2, acted, HB)
                transpose_current(1 + steps)
                by_columns(BC, C)

                def back(i):
                    for par in range(2):
                        b = 2 * i + par
                        pe.wait_ge(sent_ready, b + 1)
                        need(pe, mixed_ready, b - 1)
                        for t in range(QT):
                            for kt in range(KT):
                                ins = nc.tensor.transpose(bank[2 + par][:, t * C + kt * P:t * C + (kt + 1) * P],
                                                          sent[par][:, kt, t * P:(t + 1) * P], core.ident[:])
                        ins.then_inc(sent_t_done, 1)

                back(0)
                with pe.Fori(1, PAIRS) as i:
                    back(i)

            @block.scalar
            def _(act):
                act.wait_ge(last_loaded, 32)
                nc.scalar.activation(gate_w[0][:], gate_staged[:], ACT.Copy).then_inc(gate_high, 1)
                act.wait_ge(loaded, 64)
                with act.Fori(0, PAIRS) as i:
                    for par in range(2):
                        b = 2 * i + par
                        act.wait_ge(gate_done, b + 1)
                        for c in range(KT):
                            ins = nc.scalar.activation(gate[:, c, bass.ds(b * S, S)], bank[par][:, c * S:(c + 1) * S],
                                                       ACT.Sigmoid, bias=columns[:, HB + c:HB + c + 1])
                        ins.then_inc(gate_ready, 1)
                for n in range(steps):
                    act.wait_ge(act_in_ready, n + 1)
                    nc.scalar.activation(acted[:], act_in[:], ACT.Gelu).then_inc(acted_ready, 1)

            @block.vector
            def _(dve):
                count = [0]

                def after(ins):
                    count[0] += 1
                    ins.then_inc(chain, 1)
                    dve.wait_ge(chain, count[0])

                dve.wait_ge(gate_high, 1)
                nc.vector.tensor_tensor(gate_w[1][:], gate_staged[:], gate_w[0][:].bitcast(F32), ALU.subtract).then_inc(gate_low, 1)
                dve.wait_ge(last_loaded, 32)
                dve.wait_ge(loaded, 64)

                def norm8(source, target, n, gamma=None, beta=None):
                    after(nc.vector.bn_stats(stats8[:], source[:]))
                    nc.vector.bn_aggr(meanvar8[:], stats8[:]).then_inc(var8_ready, 1)
                    dve.wait_ge(var8_ready, n + 1)
                    dve.wait_ge(rstd8_ready, n + 1)
                    ins = nc.vector.tensor_scalar(target[:], source[:], meanvar8[:, 0:1], rstd8[:, 0:1], ALU.subtract, ALU.mult)
                    if gamma is None:
                        after(ins)
                        return
                    after(ins)
                    after(nc.vector.tensor_tensor(target[:], target[:], rows[:, gamma, :], ALU.mult))
                    nc.vector.tensor_tensor(target[:], target[:], rows[:, beta, :], ALU.add).then_inc(current_ready, 1)

                def copy_transposed(n):
                    dve.wait_ge(current_t_done, n + 1)
                    nc.vector.tensor_copy(current_t[:], t_bank[:, 0:KT * B].rearrange("p (k b) -> p k b", k=KT)).then_inc(current_t_ready, 1)

                norm8(last, last, 0)
                norm8(last, current, 1, 0, 1)
                copy_transposed(0)
                dve.wait_ge(product_done, 1)
                after(nc.vector.tensor_tensor(thought[:], row_bank[0:B, 0:C], rows[:, 2, :], ALU.add))
                for n in range(steps):
                    norm8(thought, current, 2 + n, 3, 4)
                    copy_transposed(1 + n)
                    after(nc.vector.tensor_tensor(thought_bias[:], thought[:], rows[:, 5, :], ALU.add))
                    dve.wait_ge(product_done, 2 + 2 * n)
                    nc.vector.tensor_tensor(act_in[:], wide_bank[:, 0:HB * B].rearrange("p (h b) -> p h b", h=HB),
                                            columns[:, 0:HB].rearrange("p (h a) -> p h a", a=1).to_broadcast([P, HB, B]),
                                            ALU.add).then_inc(act_in_ready, 1)
                    dve.wait_ge(product_done, 3 + 2 * n)
                    after(nc.vector.tensor_tensor(thought[:], row_bank[0:B, 0:C], thought_bias[:], ALU.add))
                nc.vector.tensor_copy(current[:], thought[:]).then_inc(current_ready, 1)
                copy_transposed(1 + steps)
                dve.wait_ge(product_done, 2 + 2 * steps)
                nc.vector.tensor_tensor(message_t[:], wide_bank[:, 0:KT * B].rearrange("p (k b) -> p k b", k=KT),
                                        columns[:, HB + KT:HB + 2 * KT].rearrange("p (k a) -> p k a", a=1).to_broadcast([P, KT, B]),
                                        ALU.add).then_inc(message_ready, 1)
                dve.wait_ge(message_ready, 1)
                dve.wait_ge(gate_ready, B)

                TAIL = 8

                def send(b, par):
                    need(dve, sent_t_done, b - 1)
                    for kt in range(KT):
                        ins = nc.vector.tensor_scalar(sent[par][:, kt, :], gate[:, kt, bass.ds(b * S, S)],
                                                      message_t[:, kt, bass.ds(b, 1)], None, ALU.mult)
                    ins.then_inc(sent_ready, 1)

                def mix(b, par, base):
                    for t in range(QT):
                        tile = b * QT + t
                        ins = nc.vector.tensor_scalar(mixed[par][:, t, :], x[:, bass.ds(tile, 1), :].rearrange("p a c -> p (a c)"),
                                                      core.rstd[:, bass.ds(tile, 1)], core.shift[:, bass.ds(tile, 1)],
                                                      ALU.mult, ALU.add)
                    ins.then_inc(tail, 1)
                    dve.wait_ge(tail, base + 1)
                    dve.wait_ge(sent_t_done, b + 1)
                    nc.vector.tensor_tensor(mixed[par][:], mixed[par][:], bank[2 + par][:].rearrange("p (t c) -> p t c", t=QT),
                                            ALU.add).then_inc(mixed_ready, 1)
                    dve.wait_ge(mixed_ready, b + 1)
                    for t in range(QT):
                        ins = nc.vector.bn_stats(stats[par][:, t, :], mixed[par][:, t, :])
                    ins.then_inc(tail, 1)
                    dve.wait_ge(tail, base + 2)
                    nc.vector.memset(carrier[par][:], 0.0)
                    for t in range(QT):
                        ins = nc.vector.bn_aggr(meanvar[par][:, t, :], stats[par][:, t, :])
                    ins.then_inc(var_ready, 1)

                def add(b, par, base):
                    dve.wait_ge(rstd_ready, b + 1)
                    dve.wait_ge(var_ready, b + 1)
                    nc.vector.scalar_tensor_tensor(shift[par][:], meanvar[par][:, :, 0], -1.0, rstd[par][:], ALU.mult, ALU.mult)\
                        .then_inc(tail, 1)
                    dve.wait_ge(tail, base + 1)
                    for t in range(QT):
                        ins = nc.vector.tensor_scalar(mixed[par][:, t, :], mixed[par][:, t, :], rstd[par][:, t:t + 1],
                                                      shift[par][:, t:t + 1], ALU.mult, ALU.add)
                    ins.then_inc(tail, 1)
                    dve.wait_ge(tail, base + 2)
                    tiles = x[:, bass.ds(b * QT, QT), :]
                    gamma, beta = (wide_rows[:, n:n + 1, :].to_broadcast([P, QT, C]) for n in range(2))
                    nc.vector.tensor_tensor(mixed[par][:], mixed[par][:], gamma, ALU.mult).then_inc(tail, 1)
                    nc.vector.tensor_tensor(tiles, tiles, beta, ALU.add).then_inc(tail, 1)
                    dve.wait_ge(tail, base + 4)
                    nc.vector.tensor_tensor(tiles, tiles, mixed[par][:], ALU.add).then_inc(tail, 1)

                PER = 7

                def pair(i):
                    send(2 * i, 0)
                    send(2 * i + 1, 1)
                    base = 2 * PER * i
                    mix(2 * i, 0, base)
                    mix(2 * i + 1, 1, base + 2)
                    add(2 * i, 0, base + 4)
                    add(2 * i + 1, 1, base + 9)

                pair(0)
                with dve.Fori(1, PAIRS) as i:
                    pair(i)


def four_layers_kernel(nc, d, out):
    narrow = (NarrowAttention(16, causal=True), NarrowAttention(32, causal=False))
    wide = {2: WideAttention(4, 4, shared_kv=True, rope=False, causal=True, scale=1 / math.sqrt(P)),
            3: WideAttention(2, 8, shared_kv=False, rope=True, causal=False, scale=1 / math.sqrt(P))}
    experts = {0: Experts(64, 6, d["experts_0"].shape[0], True, ACT.Silu, "sigmoid", capacity=128),
               2: Experts(16, 2, d["experts_2"].shape[0], False, ACT.Gelu, "softmax"),
               3: Experts(32, 6, d["experts_3"].shape[0], True, ACT.Silu, "limited")}

    with ExitStack() as stack:
        core = Core(nc, stack)
        load_stage(core, d["x"], d["ident"])

        def feed_forward(layer):
            cfg, weights = experts[layer], d[f"experts_{layer}"]
            with Stage(core) as held:
                gates_t = held.sb("gates_t", [P, TILES * P], F32R)
                staged = [held.sb("staged", [P, cfg.width]) for _ in range(2)]
                w_loaded = [held.sem("w_loaded") for _ in range(2)]
                route_stage(core, cfg, d[f"router_{layer}"], gates_t, [d["earlier"]], [(staged[0][:], weights[0], w_loaded[0])])
                experts_stage(core, cfg, weights, gates_t, staged, w_loaded)

        narrow_attention_stage(core, narrow[0], d["attention_0"], d["select_0"], [d["mask"], d["out_bias_0"]])
        feed_forward(0)
        narrow_attention_stage(core, narrow[1], d["attention_1"], d["select_1"], [d["relative_1"]])
        thought_stage(core, d["thought_w"], d["thought_gate_w"], d["thought_rows"], d["thought_columns"], d["thought_wide_rows"])
        wide_attention_stage(core, wide[2], d["attention_2"], [d["position"], d["bias_2"], d["value_bias_2"], d["mask"]])
        feed_forward(2)
        wide_attention_stage(core, wide[3], d["attention_3"], [d["rotation"]])
        feed_forward(3)
        store_stage(core, out)



def by_contraction(w):
    return np.concatenate([w[at:at + P] for at in range(0, w.shape[0], P)], axis=1)


def narrow_weights(i, layer):
    wq, wk, wv, wo = (i[f"{layer}_attn_{n}"].T for n in ("wq", "wk", "wv", "wo"))
    wo = wo.reshape(4, 2, 32, C).transpose(1, 0, 2, 3).reshape(C, C)
    return np.concatenate([by_contraction(w) for w in (wq, wk, wv, wo)], axis=1)


def stack_selection(heads):
    dim = C // heads
    rows = 4 * dim
    per = P // rows
    s = np.zeros((P, 2, 4, 2, P), np.float32)
    for which, blocks in enumerate(((0, 1, 0, 1), (0, 0, 1, 1))):
        for tile in range(4):
            for head in range(per):
                for block, part in enumerate(blocks):
                    n = np.arange(dim)
                    s[(tile * per + head) * dim + n, which, tile, part, head * rows + block * dim + n] = 1
    return s


def relative_table(rel_pos):
    relative = np.arange(S + P)[None] - np.arange(P)[:, None] - P
    return rel_pos[np.clip(relative + 63, 0, 126)]


def position_encoding():
    ang = np.arange(S, dtype=np.float32)[:, None] * np.exp(-(np.log(np.float32(10000.0)) * np.arange(0, P, 2, dtype=np.float32) / np.float32(P)))
    pe = np.zeros((S, P), np.float32)
    pe[:, 0::2], pe[:, 1::2] = np.sin(ang), np.cos(ang)
    return pe.T


def rotation_table():
    inv = 1.0 / np.float32(10000.0) ** (np.arange(0, 64, 2, dtype=np.float32) / np.float32(64))
    angle = np.arange(S, dtype=np.float32)[:, None] * inv[None]
    c, s = np.cos(angle).T.astype(np.float32), np.sin(angle).T.astype(np.float32)
    table = np.stack([np.concatenate([c, -s], axis=1), np.concatenate([s, c], axis=1)], axis=1)
    scale = np.float32(1 / 8)
    return np.concatenate([table * scale, table * scale, table, table])


def wide_weights_2(i):
    wq, wkv, wo = (i[f"L2_attn_{n}"] for n in ("wq", "wkv", "wo"))
    return np.stack([np.concatenate([
        by_contraction(wq[:, g * 512:(g + 1) * 512]), by_contraction(wkv[:, g * 256:g * 256 + P]),
        by_contraction(wkv[:, g * 256 + P:(g + 1) * 256]), by_contraction(wo[g * 512:(g + 1) * 512])], axis=1) for g in range(4)])


def wide_biases_2(i):
    kv = i["L2_attn_bkv"].reshape(4, 2, P)
    columns = np.concatenate([i["L2_attn_bq"].reshape(4, 4, P), kv[:, :1]], axis=1).transpose(2, 0, 1)
    return columns, np.broadcast_to(kv[:, 1], (P, 4, P))


def wide_weights_3(i):
    wq, wk, wv, wo = (i[f"L3_attn_{n}"] for n in ("Wq", "Wk", "Wv", "Wo"))
    blocks = []
    for g in range(8):
        turned = np.stack([w[2048 + g * P:2048 + (g + 1) * P] for w in (wq, wk)]).reshape(4, 2, 32, C)
        parts = [by_contraction(turned.transpose(1, 0, 2, 3).reshape(2 * P, C).T)]
        parts += [by_contraction(w[g * 256:(g + 1) * 256].T) for w in (wq, wk)]
        parts += [by_contraction(wv[g * 256:(g + 1) * 256].T), by_contraction(wo.T[g * 256:(g + 1) * 256])]
        blocks.append(np.concatenate(parts, axis=1))
    return np.stack(blocks)


def hidden_groups(ups, down, owner):
    rows = down.shape[0]
    whole = -(-rows // P) * P
    ups = [np.concatenate([u, np.zeros((C, whole - rows), u.dtype)], axis=1) for u in ups]
    down = np.concatenate([down, np.zeros((whole - rows, C), down.dtype)])
    owner = np.concatenate([owner, np.full(whole - rows, owner[-1])])
    groups = []
    for at in range(0, whole, P):
        pick = np.zeros((P, P), np.float32)
        for half in (0, 64):
            pick[owner[at:at + P] % 64 + half, np.arange(P)] = 1
        groups.append(np.concatenate([by_contraction(u[:, at:at + P]) for u in ups] + [down[at:at + P], pick], axis=1))
    return groups


def flat(w):
    return w.transpose(1, 0, 2).reshape(C, -1)


def expert_weights(i):
    def get(layer, *names):
        return (i[f"L{layer}_ffn_{n}"] for n in names)
    up, down, shared_up, shared_down = get(0, "w_up", "w_down", "w_shared_up", "w_shared_down")
    first = hidden_groups([flat(up[:, :, :32]), flat(up[:, :, 32:])], down.reshape(-1, C), np.repeat(np.arange(64), 32))
    first += hidden_groups([shared_up[:, 64:], shared_up[:, :64]], shared_down, np.full(64, 64))
    up, down, shared_up, shared_down = get(2, "Wrt_up", "Wrt_down", "Wsh_up", "Wsh_down")
    second = hidden_groups([flat(up)], down.reshape(-1, C), np.repeat(np.arange(16), 128))
    second += hidden_groups([flat(shared_up)], shared_down.reshape(-1, C), np.full(256, 16))
    gate, up, down, shared_gate, shared_up, shared_down = get(3, "w_gate", "w_up", "w_down", "sw_gate", "sw_up", "sw_down")
    third = hidden_groups([flat(gate), flat(up)], down.reshape(-1, C), np.repeat(np.arange(32), 176))
    third += hidden_groups([shared_gate, shared_up], shared_down, np.full(352, 32))
    return {"experts_0": np.stack(first), "experts_2": np.stack(second), "experts_3": np.stack(third)}


def layouts(i):
    def thought(n):
        return i[f"L1_ffn_{n}"]

    def by_tile(w):
        return w.reshape(KT, P, -1).transpose(1, 0, 2)

    n = np.arange(P)
    bias_2, value_bias_2 = wide_biases_2(i)
    return {
        "x": i["L0_attn_x"].reshape(TILES, P, C).transpose(1, 0, 2),
        "ident": np.eye(P, dtype=np.float32),
        "mask": np.where(n[None] > n[:, None], np.float32(MASKED), np.float32(0)),
        "earlier": np.where(n[:, None] < n[None], np.float32(1), np.float32(0)),
        "attention_0": narrow_weights(i, "L0"), "select_0": stack_selection(16), "out_bias_0": i["L0_attn_bo"][None],
        "attention_1": narrow_weights(i, "L1"), "select_1": stack_selection(32),
        "relative_1": relative_table(i["L1_attn_rel_pos"]),
        "attention_2": wide_weights_2(i), "bias_2": bias_2, "value_bias_2": value_bias_2, "position": position_encoding(),
        "attention_3": wide_weights_3(i), "rotation": rotation_table(),
        "router_0": by_tile(i["L0_ffn_w_gate"]), "router_2": by_tile(i["L2_ffn_W_router"]), "router_3": by_tile(i["L3_ffn_gate_w"]),
        **expert_weights(i),
        "thought_w": np.concatenate([by_contraction(thought(w)) for w in ("agg_w", "bc_w", "d1_w", "d2_w")], axis=1),
        "thought_gate_w": by_tile(thought("gate_w")),
        "thought_rows": np.broadcast_to(np.stack([thought(w) for w in ("in_gamma", "in_beta", "agg_b", "pn_gamma", "pn_beta", "d2_b")]), (B, 6, C)),
        "thought_columns": np.concatenate([thought(w).reshape(-1, P) for w in ("d1_b", "gate_b", "bc_b")]).T,
        "thought_wide_rows": np.broadcast_to(np.stack([thought(w) for w in ("out_gamma", "out_beta")]), (P, 2, C)),
    }


def kernel(**inputs):
    import concourse.bacc as bacc
    from concourse.bass_utils import run_bass_kernel_spmd

    arrays = {f"in_{name}": np.ascontiguousarray(a) for name, a in layouts({k: np.asarray(v) for k, v in inputs.items()}).items()}
    nc = bacc.Bacc("TRN2", target_bir_lowering=False, num_devices=1)
    d = {name[3:]: nc.dram_tensor(name, a.shape, mybir.dt.from_np(a.dtype), kind="ExternalInput").ap() for name, a in arrays.items()}
    out = nc.dram_tensor("out", (P, TILES, C), F32, kind="ExternalOutput").ap()
    four_layers_kernel(nc, d, out)
    result = run_bass_kernel_spmd(nc, [arrays], core_ids=[0])
    return result.results[0]["out"].transpose(1, 0, 2).reshape(B, S, C)
```

```python
import math
from contextlib import ExitStack

import numpy as np

import concourse.bass as bass
from concourse import mybir

F32 = mybir.dt.float32
F32R = mybir.dt.float32r
BF16 = mybir.dt.bfloat16
ALU = mybir.AluOpType
ACT = mybir.ActivationFunctionType
AX = mybir.AxisListType

P = 128
B, S, C = 8, 256, 256
TILES = B * S // P
KT = C // P
QT = S // P
BIG = 3.0e38
MASKED = -1.0e30
PAIRS = B // 2


def need(eng, sem, value):
    if isinstance(value, int) and value <= 0:
        return
    eng.wait_ge(sem, value)


class Stage:

    def __init__(self, core):
        self.nc, self.core, self.stack, self.sems = core.nc, core, ExitStack(), []

    def __enter__(self):
        self.stack.__enter__()
        return self

    def __exit__(self, *error):
        self.stack.__exit__(*error)
        if not error[0]:
            self.nc.clear_and_free_semaphores(self.sems)
            self.nc.all_engine_barrier()

    def sb(self, name, shape, dtype=F32):
        return self.stack.enter_context(self.nc.sbuf_tensor(self.core.unique(name), shape, dtype))

    def sem(self, name):
        s = self.nc.alloc_semaphore(self.core.unique(name))
        self.sems.append(s)
        return s


class Core:

    def __init__(self, nc, stack):
        self.nc, self.count = nc, 0

        def sb(name, shape, dtype=F32):
            return stack.enter_context(nc.sbuf_tensor(name, shape, dtype))

        self.x = sb("x_sb", [P, TILES, C])
        self.norm_t_high = sb("norm_t_high", [P, KT, TILES * P], F32R)
        self.norm_t_low = sb("norm_t_low", [P, KT, TILES * P], F32R)
        self.rstd = sb("rstd", [P, TILES])
        self.shift = sb("shift", [P, TILES])
        self.ident = sb("ident_sb", [P, P])
        self.ident_bf = sb("ident_bf", [P, P], BF16)
        self.bank = [stack.enter_context(nc.psum_tensor(f"bank{i}", [P, 512], F32)) for i in range(8)]

    def unique(self, name):
        self.count += 1
        return f"{name}_{self.count}"


def load_stage(core, x_in, ident_in):
    nc = core.nc
    with Stage(core) as st:
        loaded = st.sem("loaded")
        with nc.Block() as block:

            @block.sync
            def _(sp):
                sp.dma_start(core.x[:], x_in).then_inc(loaded, 16)
                sp.dma_start(core.ident[:], ident_in).then_inc(loaded, 16)
                sp.wait_ge(loaded, 32)

            @block.vector
            def _(dve):
                dve.wait_ge(loaded, 32)
                nc.vector.tensor_copy(core.ident_bf[:], core.ident[:])


def store_stage(core, out):
    nc = core.nc
    with Stage(core) as st:
        stored = st.sem("stored")
        with nc.Block() as block:

            @block.sync
            def _(sp):
                sp.dma_start(out, core.x[:]).then_inc(stored, 16)
                sp.wait_ge(stored, 16)


def norm_stage(core, early_loads=(), depth=4, eps=1e-5):
    nc, x = core.nc, core.x
    DEPTH, PART, BY_DVE = depth, 2 * QT, B // 2
    with Stage(core) as st:
        stats = st.sb("stats", [P, TILES, 6])
        meanvar = st.sb("meanvar", [P, TILES, 2])
        var_eps = st.sb("var_eps", [P, TILES])
        minus_half = st.sb("minus_half", [P, TILES])
        normed = [st.sb("normed", [P, QT, C]) for _ in range(DEPTH)]
        stats_ready, meanvar_ready = st.sem("stats_ready"), st.sem("meanvar_ready")
        pool_step, rstd_ready, shift_ready = st.sem("pool_step"), st.sem("rstd_ready"), st.sem("shift_ready")
        normed_by_dve, normed_by_act, transposed = st.sem("normed_by_dve"), st.sem("normed_by_act"), st.sem("transposed")
        high_ready, low_ready = st.sem("high_ready"), st.sem("low_ready")
        bank = core.bank

        def columns(t, b):
            return t[:, :, b * S:(b + 1) * S]

        with nc.Block() as block:

            @block.sync
            def _(sp):
                for target, source, semaphore in early_loads:
                    sp.dma_start(target, source).then_inc(semaphore, 16)

            @block.gpsimd
            def _(pool):
                nc.gpsimd.memset(minus_half[:], -0.5).then_inc(pool_step, 1)
                for n in range(TILES // PART):
                    part = slice(n * PART, (n + 1) * PART)
                    pool.wait_ge(meanvar_ready, (n + 1) * PART)
                    nc.gpsimd.tensor_scalar(var_eps[:, part], meanvar[:, part, 1], 1.0, float(eps), ALU.mult, ALU.add)\
                        .then_inc(pool_step, 1)
                    pool.wait_ge(pool_step, n + 2)
                    nc.gpsimd.tensor_tensor(core.rstd[:, part], var_eps[:, part], minus_half[:, part], ALU.pow)\
                        .then_inc(rstd_ready, 1)

            @block.vector
            def _(dve):
                def statistics(n):
                    tiles = range(n * PART, (n + 1) * PART)
                    for t in tiles:
                        nc.vector.bn_stats(stats[:, t, :], x[:, t, :]).then_inc(stats_ready, 1)
                    for t in tiles:
                        dve.wait_ge(stats_ready, t + 1)
                        nc.vector.bn_aggr(meanvar[:, t, :], stats[:, t, :]).then_inc(meanvar_ready, 1)

                def shift(n):
                    part = slice(n * PART, (n + 1) * PART)
                    dve.wait_ge(rstd_ready, n + 1)
                    nc.vector.scalar_tensor_tensor(core.shift[:, part], meanvar[:, part, 0], -1.0,
                                                   core.rstd[:, part], ALU.mult, ALU.mult).then_inc(shift_ready, 1)

                def apply(b):
                    dve.wait_ge(shift_ready, b // 2 + 1)
                    dve.wait_ge(transposed, b - DEPTH + 1)
                    t = b * QT
                    nc.vector.tensor_scalar(normed[b % DEPTH][:, 0, :], x[:, t, :], core.rstd[:, t:t + 1], core.shift[:, t:t + 1],
                                            ALU.mult, ALU.add).then_inc(normed_by_dve, 1)

                def low(b):
                    dve.wait_ge(high_ready, b + 1)
                    nc.vector.tensor_tensor(columns(core.norm_t_low, b), bank[b % DEPTH][:].rearrange("p (k t) -> p k t", k=KT),
                                            columns(core.norm_t_high, b).bitcast(F32), ALU.subtract).then_inc(low_ready, 1)

                statistics(0)
                statistics(1)
                shift(0)
                statistics(2)
                shift(1)
                statistics(3)
                shift(2)
                low(0)
                shift(3)
                low(1)
                apply(4)
                low(2)
                for b in range(3, B):
                    if b + 2 < B:
                        apply(b + 2)
                    low(b)

            @block.tensor
            def _(pe):
                for b in range(B):
                    pe.wait_ge(normed_by_act, b + 1)
                    if b >= BY_DVE:
                        pe.wait_ge(normed_by_dve, b - BY_DVE + 1)
                    need(pe, low_ready, b - DEPTH + 1)
                    for t in range(QT):
                        for k in range(KT):
                            ins = nc.tensor.transpose(bank[b % DEPTH][:, k * S + t * P:k * S + (t + 1) * P],
                                                      normed[b % DEPTH][:, t, k * P:(k + 1) * P], core.ident[:])
                    ins.then_inc(transposed, 1)

            @block.scalar
            def _(act):
                def apply(b):
                    act.wait_ge(shift_ready, b // 2 + 1)
                    need(act, transposed, b - DEPTH + 1)
                    for t in range(1 if b >= BY_DVE else 0, QT):
                        tile = b * QT + t
                        ins = nc.scalar.activation(normed[b % DEPTH][:, t, :], x[:, tile, :], ACT.Identity,
                                                   bias=core.shift[:, tile:tile + 1], scale=core.rstd[:, tile:tile + 1])
                    ins.then_inc(normed_by_act, 1)

                apply(0)
                apply(1)
                for b in range(B):
                    if b + 2 < B:
                        apply(b + 2)
                    act.wait_ge(transposed, b + 1)
                    nc.scalar.activation(columns(core.norm_t_high, b), bank[b % DEPTH][:].rearrange("p (k t) -> p k t", k=KT),
                                         ACT.Copy).then_inc(high_ready, 1)


def score_columns(causal, t):
    if causal:
        return slice(0, P) if t == 0 else slice(P, P + S)
    return slice(t * S, (t + 1) * S)


def make_masks(nc, masks_bf, mask):
    nc.vector.memset(masks_bf[:, P:2 * P], 0.0)
    nc.vector.tensor_copy(masks_bf[:, 0:P], mask[:])
    return nc.vector.tensor_copy(masks_bf[:, 2 * P:3 * P], mask[:])


class WideAttention:

    def __init__(self, heads, groups, shared_kv, rope, causal, scale):
        self.HG, self.G, self.rope, self.causal, self.scale = heads, groups, rope, causal, scale
        self.shared_kv, self.KV = shared_kv, 1 if shared_kv else heads
        widths = [2 * P, heads * P, self.KV * P, self.KV * P] if rope else [heads * P, P, P]
        scales = [1.0, scale, 1.0, 1.0] if rope else [scale, 1.0, 1.0]
        names = ["rope", "q", "k", "v"] if rope else ["q", "k", "v"]
        at, self.segment, self.parts = 0, {}, []
        for name, width, s in zip(names, widths, scales):
            self.segment[name] = (len(self.parts), at, width)
            self.parts.append((at, at + KT * width, s))
            at += KT * width
        self.wo_at, self.width = at, at + heads * C
        self.parts.append((at, self.width, 1.0))
        if rope:
            self.pieces = [("q", False, ["q"]), ("k", False, ["k"]), ("v", False, ["v"]), ("rope", True, ["rope"])]
            self.before = {0: [0], 1: [2]}
            self.after = {0: [1], 1: [3]}
        else:
            self.pieces = [("q", True, ["q"]), ("q2", True, ["q"]), ("kv", True, ["k", "v"])]
            self.before = {}
            self.after = {0: [0], 1: [1], 2: [2]}
        self.ahead = 1 if rope else 0
        self.sums = [i for i, p in enumerate(self.pieces) if p[1]]


def wide_attention_stage(core, cfg, w_in, consts_in):
    nc, x, bank = core.nc, core.x, core.bank
    norm_t = (core.norm_t_high, core.norm_t_low)
    HG, G, KV, rope, causal = cfg.HG, cfg.G, cfg.KV, cfg.rope, cfg.causal
    NP, NS, NW, AHEAD = len(cfg.pieces), len(cfg.sums), len(cfg.parts), cfg.ahead
    assert B % 2 == 0 and HG % 2 == 0
    p_bank, s_bank, t_bank, o_bank, y_bank = bank[0:2], bank[2:4], bank[4], bank[5], bank[6:8]
    NB = S + P if causal else QT * S

    with Stage(core) as st:
        staged = st.sb("staged", [P, cfg.width])
        w = [st.sb("w", [P, cfg.width], F32R) for _ in range(2)]
        z, q, k, v = (
            [[st.sb(name, shape, F32R) for _ in range(2)] for _ in range(2)]
            for name, shape in (("z", [P, KT, S]), ("q", [P, HG, S]), ("k", [P, KV, S]), ("v", [P, QT, KV * P])))
        if rope:
            tables = st.sb("tables", [P, 2, 2 * S])
            consts = [tables]
            turned = st.sb("turned", [P, 2, 2 * S])
            summed = [st.sb("summed", [P, 2 * S]) for _ in range(2)]
            halves = st.sb("halves", [P, 2, 2, S], F32R)
            rotated = [st.sb("rotated", [P, 2, 2, S], F32R) for _ in range(2)]
            moved = [st.sem("moved") for _ in range(2)]
            halves_high, halves_low = st.sem("halves_high"), st.sem("halves_low")
            MOVES = 8
        else:
            position = st.sb("position", [P, S])
            bias = st.sb("bias", [P, G, HG + 1])
            v_bias = st.sb("v_bias", [P, G, P])
            mask = st.sb("mask", [P, P])
            consts = [position, bias, v_bias, mask]
            scaled_position = st.sb("scaled_position", [P, S])
            scaled_bias = st.sb("scaled_bias", [P, G, HG])
            masks_bf = st.sb("masks_bf", [P, S + P], BF16)
            summed = [st.sb("summed", [P, 2 * S]) for _ in range(2)]
        probs = [st.sb("probs", [P, QT, S]) for _ in range(2)]
        probs_t = [[st.sb("probs_t", [P, NB], F32R) for _ in range(2)] for _ in range(2)]
        out_t = [[st.sb("out_t", [P, S], F32R) for _ in range(2)] for _ in range(2)]
        neg_max = [st.sb("neg_max", [P, QT]) for _ in range(2)]
        sums = [st.sb("sums", [P, QT]) for _ in range(2)]
        inv = [st.sb("inv", [P, QT]) for _ in range(2)]

        consts_loaded, consts_ready = st.sem("consts_loaded"), st.sem("consts_ready")
        w_loaded, w_high, w_low = st.sem("w_loaded"), st.sem("w_high"), st.sem("w_low")
        z_loaded = [st.sem("z_loaded") for _ in range(2)]
        piece_done, piece_read, piece_high = st.sem("piece_done"), st.sem("piece_read"), st.sem("piece_high")
        sum_ready, sum_low = st.sem("sum_ready"), st.sem("sum_low")
        scores_done, max_ready, probs_ready = st.sem("scores_done"), st.sem("max_ready"), st.sem("probs_ready")
        t_done, t_high, t_low = st.sem("t_done"), st.sem("t_high"), st.sem("t_low")
        o_done, o_high, o_low = st.sem("o_done"), st.sem("o_high"), st.sem("o_low")
        y_done, y_added, inv_ready = st.sem("y_done"), st.sem("y_added"), st.sem("inv_ready")

        class Unit:

            def __init__(self, g, i, parity, first=False, last=False):
                self.g, self.i, self.parity, self.first, self.last = g, i, parity, first, last
                self.b = 2 * i + parity
                self.n = g * B + self.b
                self.opens = isinstance(i, int) and i == 0 and parity == 0
                self.closes = isinstance(i, int) and i == PAIRS - 1 and parity == 1
                self.in_last_group = isinstance(g, int) and g == G - 1

            def next(self):
                if self.closes:
                    return Unit(self.g + 1, 0, 0)
                return Unit(self.g, self.i, 1) if self.parity == 0 else Unit(self.g, self.i + 1, 0)

            def before(self):
                if self.opens:
                    return Unit(self.g - 1, PAIRS - 1, 1)
                return Unit(self.g, self.i, 0) if self.parity == 1 else Unit(self.g, self.i - 1, 1)

            def slot(self, j):
                return self.n * HG + j

        def over_units(eng, work):
            def group(g, first=False, last=False):
                work(Unit(g, 0, 0, first=first))
                work(Unit(g, 0, 1))
                with eng.Fori(1, PAIRS - 1) as i:
                    work(Unit(g, i, 0))
                    work(Unit(g, i, 1))
                work(Unit(g, PAIRS - 1, 0))
                work(Unit(g, PAIRS - 1, 1, last=last))
            group(0, first=True)
            with eng.Fori(1, G - 1) as g:
                group(g)
            group(G - 1, last=True)

        def next_slot(u, j):
            return (u, j + 1) if j + 1 < HG else (u.next(), 0)

        def slot_before(u, j):
            return (u, j - 1) if j else (u.before(), HG - 1)

        def over_slots(eng, piece, value, transposed, score, output, slot_start=None, later_pieces_last=False,
                       finish=None):
            if rope:
                piece(Unit(-1, PAIRS - 1, 1), NP - 1)
                if finish:
                    finish(Unit(0, 0, 0))
            for i in range(NP):
                piece(Unit(0, 0, 0), i)
            score(Unit(0, 0, 0), 0)

            def work(u):
                for j in range(HG):
                    if slot_start:
                        slot_start(u, j)
                    if finish and j == 0 and not u.last:
                        finish(u.next())
                    if not u.last:
                        for i in cfg.before.get(j, []):
                            piece(u.next(), i)
                    if not (u.first and j == 0):
                        value(*slot_before(u, j))
                    if later_pieces_last:
                        transposed(u, j)
                    if not u.last:
                        for i in cfg.after.get(j, []):
                            if not (cfg.pieces[i][0] == "rope" and u.next().closes and u.in_last_group):
                                piece(u.next(), i)
                    if not later_pieces_last:
                        transposed(u, j)
                    if not (u.last and j == HG - 1):
                        score(*next_slot(u, j))
                    if not (u.first and j == 0):
                        output(*slot_before(u, j))

            over_units(eng, work)
            end = Unit(G - 1, PAIRS - 1, 1)
            value(end, HG - 1)
            output(end, HG - 1)

        def piece_number(u, i):
            return u.n * NP + i + 1 + AHEAD

        def piece_bank(u, i):
            return p_bank[(u.parity * NP + i) % 2]

        def sum_number(u, i):
            s = cfg.sums.index(i)
            if rope:
                u = u.next()
            return u.n * NS + s, summed[(u.parity * NS + s) % 2]

        def destination(u, i, part):
            name = cfg.pieces[i][0]
            if name == "q":
                return [(q[u.parity][part][:, 0:2, :], slice(0, 2 * S))]
            if name == "q2":
                return [(q[u.parity][part][:, 2:4, :], slice(0, 2 * S))]
            if name == "k":
                return [(k[u.parity][part][:, 0:2, :], slice(0, 2 * S))]
            if name == "v":
                return [(v[u.parity][part][:], slice(0, 2 * S))]
            return [(k[u.parity][part][:, 0, :], slice(0, S)), (v[u.parity][part][:], slice(S, 2 * S))]

        def shaped(source, target):
            return source.rearrange("p (a c) -> p a c", a=target.shape[1]) if len(target.shape) == 3 else source

        def wait_destination_free(eng, u, i):
            need(eng, scores_done, (u.n - 1) * HG)
            if "v" in cfg.pieces[i][2]:
                need(eng, o_done, (u.n - 1) * HG)

        def wait_moved(eng, u):
            if isinstance(u.n, int) and u.n < 0:
                return
            eng.wait_ge(moved[u.parity], (u.g * PAIRS + u.i + 1) * MOVES * 16)

        def wait_weights_free(eng, g, part):
            if part < NW - 1:
                last = part if rope else (2 if part == 0 else 3)
                need(eng, piece_done, (g * B - 1) * NP + AHEAD + last)
            else:
                need(eng, y_done, g * B * HG)

        def split_parts_at(u, j):
            if not u.in_last_group:
                if u.next().closes:
                    parts = ({0: [0], 1: [1, 2]} if rope else {2: [0], 3: [1, 2]}).get(j, [])
                    return u.g + 1, parts
                if rope and u.closes and j == 0:
                    return u.g + 1, [3]
            if u.opens and not u.first and j == 1:
                return u.g, [NW - 1]
            return None, []

        norm_stage(core, [(t[:], source, consts_loaded) for t, source in zip(consts, consts_in)]
                   + [(staged[:], w_in[0], w_loaded)])

        with nc.Block() as block:

            @block.sync
            def _(sp):
                def load_z(u):
                    need(sp, piece_done, (u.n - 1) * NP)
                    for part, source in enumerate((core.norm_t_high, core.norm_t_low)):
                        sp.dma_start(z[u.parity][part][:].bitcast(F32), source[:, :, bass.ds(u.b * S, S)].bitcast(F32))\
                            .then_inc(z_loaded[u.parity], 16)

                def move(u):
                    sp.wait_ge(halves_low, u.n + 1)
                    for half in range(2):
                        for side in range(2):
                            for head in range(2):
                                at, to = (side * 2 + head) * 32, (head * 2 + half) * 32
                                sp.dma_start(rotated[u.parity][to:to + 32, side, :, :].bitcast(F32),
                                             halves[at:at + 32, half, :, :].bitcast(F32)).then_inc(moved[u.parity], 16)

                load_z(Unit(0, 0, 0))
                if rope:
                    move(Unit(0, 0, 0))

                def work(u):
                    if not u.last:
                        load_z(u.next())
                        if rope:
                            move(u.next())
                    if u.opens and not (isinstance(u.g, int) and u.g == G - 1):
                        sp.wait_ge(w_low, (u.g + 1) * NW)
                        sp.dma_start(staged[:], w_in[bass.ds(u.g + 1, 1)].rearrange("a p n -> p (a n)"))\
                            .then_inc(w_loaded, 16)

                over_units(sp, work)

            @block.tensor
            def _(pe):
                pe.wait_ge(consts_ready, 1)

                def weights(part, name, kt, first, width):
                    _, at, whole = cfg.segment[name]
                    at += kt * whole + first
                    return w[part][:, at:at + width]

                def group_of_passes(out, operands):
                    n = len(operands)
                    for kt, (stationary, moving) in enumerate(operands):
                        for m, (a, c) in enumerate(((0, 0), (0, 1), (1, 0))):
                            ins = nc.tensor.matmul(out, stationary(a), moving(c), start=(kt == 0 and m == 0),
                                                   stop=(kt == n - 1 and m == 2))
                    return ins

                def piece(u, i):
                    name, _, segments = cfg.pieces[i]
                    p = piece_bank(u, i)
                    need(pe, piece_read, piece_number(u, i) - 2)
                    if name == "rope":
                        u = u.next()
                    if "v" in segments:
                        pe.wait_ge(z_loaded[u.parity], (u.g * PAIRS + u.i + 1) * 32)
                    if u.opens:
                        for s in segments:
                            pe.wait_ge(w_low, u.g * NW + cfg.segment[s][0] + 1)
                    zz = z[u.parity]
                    if name != "v":
                        s = segments[0]
                        for c in range(1 if name == "kv" else 2):
                            first = (c + (2 if name == "q2" else 0)) * P
                            ins = group_of_passes(p[:, c * S:(c + 1) * S], [
                                (lambda a, kt=kt: weights(a, s, kt, first, P), lambda c_, kt=kt: norm_t[c_][:, kt, bass.ds(u.b * S, S)])
                                for kt in range(KT)])
                    if "v" in segments:
                        at = S if name == "kv" else 0
                        for t in range(QT):
                            ins = group_of_passes(p[:, at + t * KV * P:at + (t + 1) * KV * P], [
                                (lambda a, kt=kt: zz[a][:, kt, t * P:(t + 1) * P],
                                 lambda c_, kt=kt: weights(c_, "v", kt, 0, KV * P)) for kt in range(KT)])
                    ins.then_inc(piece_done, 1)

                def score(u, j):
                    if j == 0:
                        if rope:
                            pe.wait_ge(piece_read, piece_number(u, 1))
                            wait_moved(pe, u)
                        else:
                            pe.wait_ge(sum_low, (u.n + 1) * NS)
                    need(pe, probs_ready, u.slot(j) - 1)
                    s = s_bank[j % 2]
                    qq, kk, kj = q[u.parity], k[u.parity], 0 if cfg.shared_kv else j
                    if causal:
                        nc.tensor.matmul(s[:, 0:S + P], core.ident_bf[:], masks_bf[:], start=True, stop=False)
                    for t in range(QT):
                        width = P if causal and t == 0 else S
                        operands = [(qq[a][:, j, t * P:(t + 1) * P], kk[c][:, kj, 0:width])
                                    for a, c in ((0, 0), (0, 1), (1, 0))]
                        if rope:
                            rows = slice(64 * j, 64 * j + 64)
                            r = rotated[u.parity]
                            operands += [(r[rows, 0, a, t * P:(t + 1) * P], r[rows, 1, c, 0:width])
                                         for a, c in ((0, 0), (0, 1), (1, 0))]
                        for n, (a, c) in enumerate(operands):
                            ins = nc.tensor.matmul(s[:, score_columns(causal, t)], a, c, start=(n == 0 and not causal),
                                                   stop=(n == len(operands) - 1 and (t == QT - 1 or not causal)))
                    ins.then_inc(scores_done, 1)

                def transposed(u, j):
                    pe.wait_ge(probs_ready, u.slot(j) + 1)
                    need(pe, t_low, u.slot(j))
                    for kt in range(QT):
                        for t in range(kt if causal else 0, QT):
                            at = kt * S + t * P - (P if causal and kt else 0)
                            ins = nc.tensor.transpose(t_bank[:, at:at + P], probs[j % 2][:, t, kt * P:(kt + 1) * P],
                                                      core.ident[:])
                    ins.then_inc(t_done, 1)

                def value(u, j):
                    m = u.slot(j)
                    pe.wait_ge(t_low, m + 1)
                    need(pe, o_low, m)
                    if j == 0 and rope:
                        pe.wait_ge(piece_read, piece_number(u, 2))
                    jv, vv, pp = 0 if cfg.shared_kv else j, v[u.parity], probs_t[j % 2]
                    for kt in range(QT):
                        to = slice(P, S) if causal and kt else slice(0, S)
                        of = slice(kt * S, NB if kt else S)
                        for n, (a, c) in enumerate(((0, 0), (0, 1), (1, 0))):
                            ins = nc.tensor.matmul(o_bank[:, to], vv[a][:, kt, jv * P:(jv + 1) * P], pp[c][:, of],
                                                   start=(kt == 0 and n == 0), stop=(kt == QT - 1 and n == 2))
                    ins.then_inc(o_done, 1)

                def output(u, j):
                    m = u.slot(j)
                    pe.wait_ge(o_low, m + 1)
                    need(pe, y_added, m - 1)
                    if u.opens:
                        pe.wait_ge(w_low, (u.g + 1) * NW)
                    for t in range(QT):
                        ins = group_of_passes(y_bank[j % 2][:, t * C:(t + 1) * C], [
                            (lambda a: out_t[j % 2][a][:, t * P:(t + 1) * P],
                             lambda c: w[c][:, cfg.wo_at + j * C:cfg.wo_at + (j + 1) * C])])
                    ins.then_inc(y_done, 1)

                over_slots(pe, piece, value, transposed, score, output)

            @block.scalar
            def _(act):
                def split_high(g, parts):
                    for part in parts:
                        first, end, scale = cfg.parts[part]
                        act.wait_ge(w_loaded, (g + 1) * 16)
                        wait_weights_free(act, g, part)
                        nc.scalar.activation(w[0][:, first:end], staged[:, first:end], ACT.Copy, scale=float(scale))\
                            .then_inc(w_high, 1)

                split_high(0, range(NW))

                def slot_start(u, j):
                    split_high(*split_parts_at(u, j))

                def piece(u, i):
                    if cfg.pieces[i][0] == "rope":
                        return
                    wait_destination_free(act, u, i)
                    if cfg.pieces[i][1]:
                        number, source = sum_number(u, i)
                        act.wait_ge(piece_read, piece_number(u, i))
                    else:
                        source = piece_bank(u, i)
                        act.wait_ge(piece_done, piece_number(u, i))
                    for target, columns in destination(u, i, 0):
                        ins = nc.scalar.activation(target, shaped(source[:, columns], target), ACT.Copy)
                    ins.then_inc(piece_high, 1)

                def finish(u):
                    wait_moved(act, u.before())
                    act.wait_ge(sum_ready, u.n + 1)
                    nc.scalar.activation(halves[:, :, 0, :], summed[u.parity][:].rearrange("p (h c) -> p h c", h=2), ACT.Copy)\
                        .then_inc(halves_high, 1)

                def score(u, j):
                    m = u.slot(j)
                    act.wait_ge(max_ready, m + 1)
                    need(act, t_done, m - 1)
                    need(act, inv_ready, m - 1)
                    for t in range(QT):
                        width = P if causal and t == 0 else S
                        ins = nc.scalar.activation(probs[j % 2][:, t, 0:width], s_bank[j % 2][:, score_columns(causal, t)],
                                                   ACT.Exp, bias=neg_max[j % 2][:, t:t + 1],
                                                   accum_out=sums[j % 2][:, t:t + 1])
                    ins.then_inc(probs_ready, 1)

                def transposed(u, j):
                    act.wait_ge(t_done, u.slot(j) + 1)
                    need(act, o_done, u.slot(j) - 1)
                    nc.scalar.activation(probs_t[j % 2][0][:], t_bank[:, 0:NB], ACT.Copy).then_inc(t_high, 1)

                def value(u, j):
                    act.wait_ge(o_done, u.slot(j) + 1)
                    need(act, y_done, u.slot(j) - 1)
                    nc.scalar.activation(out_t[j % 2][0][:], o_bank[:, 0:S], ACT.Copy).then_inc(o_high, 1)

                over_slots(act, piece, value, transposed, score, lambda u, j: None, slot_start=slot_start,
                           later_pieces_last=True, finish=finish if rope else None)

            @block.vector
            def _(dve):
                dve.wait_ge(consts_loaded, 16 * len(consts))
                if rope:
                    nc.vector.memset(sums[0][:], 0.0).then_inc(consts_ready, 1)
                else:
                    make_masks(nc, masks_bf, mask)
                    nc.vector.tensor_scalar(scaled_position[:], position[:], float(cfg.scale), None, ALU.mult)
                    nc.vector.tensor_scalar(scaled_bias[:], bias[:, :, 0:HG], float(cfg.scale), None, ALU.mult)\
                        .then_inc(consts_ready, 1)
                dve.wait_ge(consts_ready, 1)

                def split_low(g, parts):
                    for part in parts:
                        first, end, scale = cfg.parts[part]
                        dve.wait_ge(w_high, g * NW + part + 1)
                        nc.vector.scalar_tensor_tensor(w[1][:, first:end], staged[:, first:end], float(scale),
                                                       w[0][:, first:end].bitcast(F32), ALU.mult, ALU.subtract)\
                            .then_inc(w_low, 1)

                split_low(0, range(NW))

                def slot_start(u, j):
                    split_low(*split_parts_at(u, j))

                def piece(u, i):
                    name, through_sum, _ = cfg.pieces[i]
                    p = piece_bank(u, i)
                    if not through_sum:
                        dve.wait_ge(piece_high, u.n * (NP - AHEAD) + i + 1)
                        (target, columns), (high, _) = destination(u, i, 1)[0], destination(u, i, 0)[0]
                        nc.vector.tensor_tensor(target, shaped(p[:, columns], target), high.bitcast(F32), ALU.subtract)\
                            .then_inc(piece_read, 1)
                        return
                    dve.wait_ge(piece_done, piece_number(u, i))
                    number, target = sum_number(u, i)
                    if rope:
                        need(dve, sum_ready, number)
                        for half in range(2):
                            ins = nc.vector.tensor_tensor(turned[:, half, :], p[:], tables[:, half, :], ALU.mult)
                        ins.then_inc(piece_read, 1)
                        return
                    need(dve, sum_low, number - 1)
                    for c in range(1 if name == "kv" else 2):
                        head = c + (2 if name == "q2" else 0)
                        b_ap = bias[:, bass.ds(u.g, 1), HG:HG + 1] if name == "kv" else scaled_bias[:, bass.ds(u.g, 1), head:head + 1]
                        ins = nc.vector.scalar_tensor_tensor(
                            target[:, c * S:(c + 1) * S], p[:, c * S:(c + 1) * S], b_ap.rearrange("p a c -> p (a c)"),
                            (position if name == "kv" else scaled_position)[:], ALU.add, ALU.add)
                    if name == "kv":
                        b_ap = v_bias[:, bass.ds(u.g, 1), :].to_broadcast([P, QT, P])
                        ins = nc.vector.tensor_tensor(target[:, S:2 * S].rearrange("p (a c) -> p a c", a=QT),
                                                      p[:, S:2 * S].rearrange("p (a c) -> p a c", a=QT), b_ap, ALU.add)
                    ins.then_inc(piece_read, 1)

                def score(u, j):
                    m = u.slot(j)
                    dve.wait_ge(scores_done, m + 1)
                    need(dve, probs_ready, m - 1)
                    s = s_bank[j % 2]
                    if causal:
                        for t in range(QT):
                            ins = nc.vector.tensor_reduce(neg_max[j % 2][:, t:t + 1], s[:, score_columns(causal, t)], AX.X,
                                                          ALU.max, negate=True)
                    else:
                        ins = nc.vector.tensor_reduce(neg_max[j % 2][:], s[:].rearrange("p (a c) -> p a c", a=QT), AX.X,
                                                      ALU.max, negate=True)
                    ins.then_inc(max_ready, 1)

                def transposed(u, j):
                    dve.wait_ge(t_high, u.slot(j) + 1)
                    nc.vector.tensor_tensor(probs_t[j % 2][1][:], t_bank[:, 0:NB], probs_t[j % 2][0][:].bitcast(F32),
                                            ALU.subtract).then_inc(t_low, 1)

                def value(u, j):
                    dve.wait_ge(o_high, u.slot(j) + 1)
                    nc.vector.tensor_tensor(out_t[j % 2][1][:], o_bank[:, 0:S], out_t[j % 2][0][:].bitcast(F32),
                                            ALU.subtract).then_inc(o_low, 1)

                def output(u, j):
                    m = u.slot(j)
                    dve.wait_ge(probs_ready, m + 1)
                    need(dve, y_added, m - 1)
                    nc.vector.reciprocal(inv[j % 2][:], sums[j % 2][:]).then_inc(inv_ready, 1)
                    dve.wait_ge(inv_ready, m + 1)
                    dve.wait_ge(y_done, m + 1)
                    need(dve, y_added, m)
                    for t in range(QT):
                        tile = x[:, bass.ds(u.b * QT + t, 1), :].rearrange("p a c -> p (a c)")
                        ins = nc.vector.scalar_tensor_tensor(tile, y_bank[j % 2][:, t * C:(t + 1) * C],
                                                             inv[j % 2][:, t:t + 1], tile, ALU.mult, ALU.add)
                    ins.then_inc(y_added, 1)

                def finish(u):
                    dve.wait_ge(halves_high, u.n + 1)
                    nc.vector.tensor_tensor(halves[:, :, 1, :], summed[u.parity][:].rearrange("p (h c) -> p h c", h=2),
                                            halves[:, :, 0, :].bitcast(F32), ALU.subtract).then_inc(halves_low, 1)

                over_slots(dve, piece, value, transposed, score, output, slot_start=slot_start,
                           finish=finish if rope else None)

            @block.gpsimd
            def _(pool):
                def piece(u, i):
                    if not cfg.pieces[i][1]:
                        return
                    number, total = sum_number(u, i)
                    if rope:
                        pool.wait_ge(piece_read, piece_number(u, i))
                        need(pool, halves_low, number - 1)
                        nc.gpsimd.tensor_tensor(total[:].rearrange("p (h c) -> p h c", h=2), turned[:, :, 0:S],
                                                turned[:, :, S:2 * S], ALU.add).then_inc(sum_ready, 1)
                        return
                    pool.wait_ge(piece_high, u.n * NP + i + 1)
                    wait_destination_free(pool, u, i)
                    for (target, columns), (high, _) in zip(destination(u, i, 1), destination(u, i, 0)):
                        ins = nc.gpsimd.tensor_tensor(target, shaped(total[:, columns], target), high.bitcast(F32), ALU.subtract)
                    ins.then_inc(sum_low, 1)

                none = lambda *a: None
                over_slots(pool, piece, none, none, none, none)


class NarrowAttention:

    def __init__(self, heads, causal):
        self.H, self.causal = heads, causal
        self.D = C // heads
        self.rows = 4 * self.D
        self.per_tile = P // self.rows
        self.stacks = heads // self.per_tile
        self.block = 32 // self.D
        self.pair = 2 * self.block
        self.banks = heads // self.pair
        self.scale = (1 if causal else -1) / math.sqrt(self.D)
        pairs = [(kind, i) for i in range(self.stacks // 2) for kind in ("q_stack", "k_stack")]
        self.steps = [("q", 0), ("k", 0), ("v", 0)] + pairs
        self.chunks = heads // 4
        self.output_slot = self.chunks + 4
        self.after_output = 7 if heads == 16 else 3
        self.at = {}
        for first, end, spaces in ((0, self.after_output, range(self.output_slot)),
                                   (self.after_output, len(self.steps), range(self.output_slot + 1, heads - 3))):
            for n in range(first, end):
                self.at.setdefault(spaces[(n - first) * len(spaces) // (end - first)], []).append(n)


def narrow_attention_stage(core, cfg, w_in, select_in, consts_in):
    nc, x, bank = core.nc, core.x, core.bank
    H, D, causal, NSTEP = cfg.H, cfg.D, cfg.causal, len(cfg.steps)
    p_bank, s_bank, t_bank, o_bank = bank[0:2], bank[2:4], bank[4:6], bank[6:8]
    NB = S + P if causal else QT * S
    W = KT * C
    RELATIVE = S + P

    WINDOW, AT, ONES_AT = 64, 32 - D, 64 - D
    FULL = QT * H * WINDOW
    BANKS, PAIR, ROWS = cfg.banks, cfg.pair, 32
    ACT_STEPS = sum(kind == "q_stack" for kind, _ in cfg.steps)
    assert NSTEP % 2 == 1

    with Stage(core) as st:
        w = [st.sb("w", [P, 4 * W], F32R) for _ in range(2)]
        select = st.sb("select", [P, 2, 4, 2, P], F32R)
        z = [st.sb("z", [P, KT, S], F32R) for _ in range(2)]
        qk = [[st.sb("qk", [P, KT, S], F32R) for _ in range(2)] for _ in range(2)]
        stack = [[st.sb("stack", [P, cfg.stacks, S], F32R) for _ in range(2)] for _ in range(2)]
        values = [[st.sb("values", [P, QT, H, D], F32R) for _ in range(2)] for _ in range(2)]
        unit = st.sb("unit", [P, 1])
        windows = [st.sb("windows", [P, FULL + WINDOW], F32R) for _ in range(2)]
        scores_space, sums_space = st.sb("scores_space", [P, 4, QT * S]), st.sb("sums_space", [P, 4, KT * S])
        staged = sums_space[:].rearrange("p a n -> p (a n)")
        select_staged = scores_space[:].rearrange("p a n -> p (a n)")
        probs = [scores_space[:, par, :].rearrange("p (t k) -> p t k", t=QT) for par in range(2)]
        probs_t = [[st.sb("probs_t", [P, NB], F32R) for _ in range(2)] for _ in range(4)]
        bound = [st.sb("bound", [P, QT]) for _ in range(2)]
        weighted = [sums_space[:, par, :] for par in range(2)]
        totals = [sums_space[:, 2 + par, :] for par in range(2)]
        out_t = [st.sb("out_t", [P, KT, S], F32R) for _ in range(2)]
        if causal:
            mask, bias_row = st.sb("mask", [P, P]), st.sb("bias_row", [1, C])
            masks_bf, ones_row = st.sb("masks_bf", [P, S + P], BF16), st.sb("ones_row", [1, P])
            consts = [mask, bias_row]
        else:
            table = st.sb("table", [P, RELATIVE // 2, D])
            neg_bias = st.sb("neg_bias", [P, RELATIVE])
            neg_scores = [scores_space[:, 2 + par, :].rearrange("p (t k) -> p t k", t=QT) for par in range(2)]
            carrier = [st.sb("carrier", [1, 1]) for _ in range(2)]
            consts = [table]
            consts_in = [consts_in[0][:, half * RELATIVE // 2:(half + 1) * RELATIVE // 2, :] for half in range(2)]

        consts_loaded, w_loaded, z_loaded = st.sem("consts_loaded"), st.sem("w_loaded"), st.sem("z_loaded")
        w_high, w_low = st.sem("w_high"), st.sem("w_low")
        select_loaded, select_ready = st.sem("select_loaded"), st.sem("select_ready")
        consts_step, consts_ready = st.sem("consts_step"), st.sem("consts_ready")
        step_done, step_high, step_read = st.sem("step_done"), st.sem("step_high"), st.sem("step_read")
        stack_by_act = st.sem("stack_by_act")
        scores_done, bound_ready, probs_ready = st.sem("scores_done"), st.sem("bound_ready"), st.sem("probs_ready")
        t_done, t_high, t_low = st.sem("t_done"), st.sem("t_high"), st.sem("t_low")
        spread, windows_ready = st.sem("spread"), st.sem("windows_ready")
        o_done, o_copied, inv_ready, out_ready = st.sem("o_done"), st.sem("o_copied"), st.sem("inv_ready"), st.sem("out_ready")
        out_t_high, out_t_low = st.sem("out_t_high"), st.sem("out_t_low")
        y_done, y_added = st.sem("y_done"), st.sem("y_added")

        LAG = 2
        CHUNKS, Y_SLOT = cfg.chunks, cfg.output_slot
        FIRST_CHUNK, SPLIT_SLOT = 2, CHUNKS + 2

        class Batch:

            def __init__(self, i, parity, first=False, last=False):
                self.i, self.parity, self.first, self.last = i, parity, first, last
                self.b = 2 * i + parity

            def next(self):
                return Batch(self.i, 1) if self.parity == 0 else Batch(self.i + 1, 0)

            def before(self):
                return Batch(self.i, 0) if self.parity == 1 else Batch(self.i - 1, 1)

            def slot(self, h):
                return self.b * H + h

        def over_batches(eng, work):
            work(Batch(0, 0, first=True))
            work(Batch(0, 1))
            with eng.Fori(1, PAIRS - 1) as i:
                work(Batch(i, 0))
                work(Batch(i, 1))
            work(Batch(PAIRS - 1, 0))
            work(Batch(PAIRS - 1, 1, last=True))

        def over_slots(eng, step, transposed, score, value, finish, split_out, project_out,
                       invert=lambda u, n: None, score_first=False, late_step="no"):
            start = Batch(0, 0)
            for n in range(NSTEP):
                step(start, n)
            score(start, 0)
            score(start, 1)

            def steps_of(u, h):
                if not u.last:
                    for n in cfg.at.get(h, []):
                        step(u.next(), n)

            def work(u):
                for h in range(H):
                    if late_step == "start":
                        steps_of(u, h - 1)
                    if not score_first:
                        transposed(u, h)
                    if not (u.last and h >= H - 2):
                        score(*((u, h + 2) if h < H - 2 else (u.next(), h + 2 - H)))
                    if score_first:
                        transposed(u, h)
                    if late_step == "no":
                        steps_of(u, h)
                    if h >= LAG or not u.first:
                        v, n = (u, h - LAG) if h >= LAG else (u.before(), H + h - LAG)
                        value(v, n)
                        if n % PAIR == PAIR - 1:
                            finish(v, n // PAIR)
                    if late_step == "end":
                        steps_of(u, h - 1)
                    if not u.first:
                        if FIRST_CHUNK <= h < FIRST_CHUNK + CHUNKS:
                            invert(u.before(), h - FIRST_CHUNK)
                        if h == SPLIT_SLOT:
                            split_out(u.before())
                        if h == Y_SLOT:
                            project_out(u.before())

            over_batches(eng, work)
            end = Batch(PAIRS - 1, 1)
            for h in range(H - LAG, H):
                value(end, h)
            finish(end, BANKS - 1)
            for n in range(CHUNKS):
                invert(end, n)
            split_out(end)
            project_out(end)

        def as_tiles(t):
            return t.rearrange("p (k t) -> p k t", k=KT)

        def read_by_act(n):
            return cfg.steps[n][0] == "q_stack"

        def wait_step_read(eng, b, n):
            if read_by_act(n):
                need(eng, stack_by_act, b * ACT_STEPS + sum(map(read_by_act, range(n + 1))))
            else:
                need(eng, step_read, b * (NSTEP - ACT_STEPS) + n + 1 - sum(map(read_by_act, range(n + 1))))

        def over_pairs(u, h):
            return u.b * BANKS + h // PAIR

        norm_stage(core, [(staged, w_in, w_loaded), (select_staged, select_in.rearrange("p a b c d -> p (a b c d)"), select_loaded)]
                   + [(t[:], source, consts_loaded) for t, source in zip(consts, consts_in)], depth=4 if causal else 3)

        with nc.Block() as block:

            @block.sync
            def _(sp):
                def load_z(u):
                    need(sp, step_done, (u.b - 1) * NSTEP + 3)
                    for part, source in enumerate((core.norm_t_high, core.norm_t_low)):
                        sp.dma_start(z[part][:].bitcast(F32), source[:, :, bass.ds(u.b * S, S)].bitcast(F32))\
                            .then_inc(z_loaded, 16)

                load_z(Batch(0, 0))
                if not causal:
                    sp.wait_ge(consts_step, 1)
                    sp.dma_start(table[:], consts_in[1]).then_inc(consts_loaded, 16)
                over_batches(sp, lambda u: None if u.last else load_z(u.next()))

            @block.tensor
            def _(pe):
                def three_passes(out, operands, close=True):
                    n = len(operands)
                    for kt, (stationary, moving) in enumerate(operands):
                        for m, (a, c) in enumerate(((0, 0), (0, 1), (1, 0))):
                            ins = nc.tensor.matmul(out, stationary(a), moving(c), start=(kt == 0 and m == 0),
                                                   stop=(close and kt == n - 1 and m == 2))
                    return ins

                pe.wait_ge(w_low, 2)
                pe.wait_ge(select_ready, 1)
                pe.wait_ge(windows_ready, 2)
                if causal:
                    pe.wait_ge(consts_ready, 1)

                def step(u, n):
                    kind, i = cfg.steps[n]
                    if n >= 2:
                        wait_step_read(pe, u.b, n - 2)
                    else:
                        wait_step_read(pe, u.b - 1, (NSTEP - 1, NSTEP - 2)[n])
                    if n == cfg.after_output:
                        need(pe, y_added, u.b - 1)
                    p = p_bank[n % 2]
                    norm_t = (core.norm_t_high, core.norm_t_low)
                    if kind == "v":
                        pe.wait_ge(z_loaded, (u.b + 1) * 32)
                    if kind in ("q", "k"):
                        at = 0 if kind == "q" else W
                        for c in range(KT):
                            ins = three_passes(p[:, c * S:(c + 1) * S], [
                                (lambda a, kt=kt: w[a][:, at + kt * C + c * P:at + kt * C + (c + 1) * P],
                                 lambda c_, kt=kt: norm_t[c_][:, kt, bass.ds(u.b * S, S)]) for kt in range(KT)])
                    elif kind == "v":
                        for t in range(QT):
                            ins = three_passes(p[:, t * C:(t + 1) * C], [
                                (lambda a, kt=kt: z[a][:, kt, t * P:(t + 1) * P],
                                 lambda c_, kt=kt: w[c_][:, 2 * W + kt * C:2 * W + (kt + 1) * C]) for kt in range(KT)])
                    else:
                        which = 0 if kind == "q_stack" else 1
                        wait_step_read(pe, u.b, which)
                        for c in range(2):
                            tile = 2 * i + c
                            for part in range(2):
                                ins = nc.tensor.matmul(p[:, c * S:(c + 1) * S], select[:, which, tile % 4, part, :],
                                                       qk[which][part][:, tile // 4, :], start=(part == 0), stop=(part == 1))
                    ins.then_inc(step_done, 1)

                def score(u, h):
                    m = u.slot(h)
                    tile, row = h // cfg.per_tile, (h % cfg.per_tile) * cfg.rows
                    if tile % 2 == 0 and row == 0:
                        wait_step_read(pe, u.b, cfg.steps.index(("q_stack", tile // 2)))
                        wait_step_read(pe, u.b, cfg.steps.index(("k_stack", tile // 2)))
                    need(pe, probs_ready, m - 1)
                    rows = slice(row, row + cfg.rows)
                    qs, ks = stack[0][u.parity], stack[1][u.parity]
                    if causal:
                        nc.tensor.matmul(s_bank[h % 2][:, 0:S + P], core.ident_bf[:], masks_bf[:], start=True, stop=False)
                    for t in range(QT):
                        width = P if causal and t == 0 else S
                        ins = nc.tensor.matmul(s_bank[h % 2][:, score_columns(causal, t)], qs[rows, tile, t * P:(t + 1) * P],
                                               ks[rows, tile, 0:width], start=not causal, stop=(t == QT - 1 or not causal))
                    ins.then_inc(scores_done, 1)

                def transposed(u, h):
                    pe.wait_ge(probs_ready, u.slot(h) + 1)
                    need(pe, t_low, u.slot(h) - 1)
                    for kt in range(QT):
                        for t in range(kt if causal else 0, QT):
                            at = kt * S + t * P - (P if causal and kt else 0)
                            ins = nc.tensor.transpose(t_bank[h % 2][:, at:at + P], probs[h % 2][:, t, kt * P:(kt + 1) * P],
                                                      core.ident[:])
                    ins.then_inc(t_done, 1)

                def value(u, h):
                    pe.wait_ge(t_low, u.slot(h) + 1)
                    if h % PAIR == 0:
                        need(pe, o_copied, over_pairs(u, h) - 1)
                        pe.wait_ge(spread, over_pairs(u, h) + 1)
                    block, inner = h // cfg.block, h % cfg.block
                    at_bank = (block % 2) * S
                    for kt in range(QT):
                        to = slice(at_bank + (P if causal and kt else 0), at_bank + S)
                        of = slice(kt * S, NB if kt else S)
                        at = (kt * H + h) * WINDOW + AT - inner * D
                        for n, (a, c) in enumerate(((0, 0), (0, 1), (1, 0))):
                            ins = nc.tensor.matmul(
                                o_bank[(block // 2) % 2][0:WINDOW, to], windows[a][:, at:at + WINDOW], probs_t[h % 4][c][:, of],
                                start=(inner == 0 and kt == 0 and n == 0),
                                stop=(inner == cfg.block - 1 and kt == QT - 1 and n == 2))
                    ins.then_inc(o_done, 1)

                def project_out(u):
                    pe.wait_ge(out_t_low, u.b + 1)
                    b = u.b
                    if isinstance(b, int) and b >= B - 2:
                        wait_step_read(pe, B - 1, NSTEP - 2)
                    else:
                        wait_step_read(pe, b + 2, cfg.after_output - 2)
                    need(pe, y_added, b)
                    for t in range(QT):
                        to = p_bank[1][:, t * C:(t + 1) * C]
                        ins = three_passes(to, [
                            (lambda a, kt=kt: out_t[a][:, kt, t * P:(t + 1) * P],
                             lambda c_, kt=kt: w[c_][:, 3 * W + kt * C:3 * W + (kt + 1) * C]) for kt in range(KT)],
                            close=not causal)
                        if causal:
                            ins = nc.tensor.matmul(to, ones_row[:], bias_row[:], start=False, stop=True)
                    ins.then_inc(y_done, 1)

                over_slots(pe, step, transposed, score, value, lambda u, bp: None, lambda u: None, project_out, score_first=True)

            @block.scalar
            def _(act):
                act.wait_ge(w_loaded, 16)
                nc.scalar.activation(w[0][:, 0:W], staged[:, 0:W], ACT.Copy, scale=float(cfg.scale)).then_inc(w_high, 1)
                nc.scalar.activation(w[0][:, W:4 * W], staged[:, W:4 * W], ACT.Copy).then_inc(w_high, 1)
                act.wait_ge(select_loaded, 16)
                nc.scalar.activation(select[:].rearrange("p a b c d -> p (a b c d)"), select_staged, ACT.Copy).then_inc(select_ready, 1)

                def step(u, n):
                    kind, i = cfg.steps[n]
                    if kind == "v":
                        act.wait_ge(step_done, u.b * NSTEP + n + 1)
                        need(act, spread, (u.b - 1) * BANKS)
                        nc.scalar.activation(values[u.parity][0][:], p_bank[n % 2][:].rearrange("p (t h d) -> p t h d", t=QT, h=H),
                                             ACT.Copy).then_inc(step_high, 1)
                    elif kind == "q_stack":
                        act.wait_ge(step_done, u.b * NSTEP + n + 1)
                        need(act, scores_done, (u.b - 1) * H)
                        nc.scalar.activation(stack[0][u.parity][:, 2 * i:2 * i + 2, :],
                                             p_bank[n % 2][:].rearrange("p (k t) -> p k t", k=2), ACT.Copy)\
                            .then_inc(stack_by_act, 1)
                    elif n < 2:
                        act.wait_ge(step_done, u.b * NSTEP + n + 1)
                        need(act, step_done, u.b * NSTEP)
                        nc.scalar.activation(qk[n][0][:], p_bank[n][:].rearrange("p (k t) -> p k t", k=KT), ACT.Copy)\
                            .then_inc(step_high, 1)

                def score(u, h):
                    m = u.slot(h)
                    act.wait_ge(bound_ready, m + 1)
                    need(act, t_done, m - 1)
                    for t in range(QT):
                        width = P if causal and t == 0 else S
                        source = s_bank[h % 2][:, score_columns(causal, t)] if causal else neg_scores[h % 2][:, t, :]
                        ins = nc.scalar.activation(probs[h % 2][:, t, 0:width], source, ACT.Exp,
                                                   bias=bound[h % 2][:, t:t + 1], scale=1.0 if causal else -1.0)
                    ins.then_inc(probs_ready, 1)

                def transposed(u, h):
                    act.wait_ge(t_done, u.slot(h) + 1)
                    need(act, o_done, u.slot(h) - 3)
                    nc.scalar.activation(probs_t[h % 4][0][:], t_bank[h % 2][:, 0:NB], ACT.Copy).then_inc(t_high, 1)

                def finish(u, bp):
                    act.wait_ge(o_done, u.b * H + (bp + 1) * PAIR)
                    if bp == 0:
                        need(act, out_t_low, u.b - 1)
                    rows = slice(bp * ROWS, (bp + 1) * ROWS)
                    nc.scalar.activation(weighted[u.parity][rows, :], o_bank[bp % 2][0:ROWS, :], ACT.Copy)
                    nc.scalar.activation(totals[u.parity][rows, :], o_bank[bp % 2][ROWS:2 * ROWS, :], ACT.Copy)\
                        .then_inc(o_copied, 1)

                def split_out(u):
                    act.wait_ge(out_ready, u.b + 1)
                    need(act, y_done, u.b)
                    nc.scalar.activation(out_t[0][:], as_tiles(weighted[u.parity]), ACT.Copy).then_inc(out_t_high, 1)

                none = lambda *a: None
                over_slots(act, step, transposed, score, none, finish, split_out, none, late_step="start")

            @block.vector
            def _(dve):
                for n, (first, end, scale) in enumerate(((0, W, cfg.scale), (W, 4 * W, 1.0))):
                    dve.wait_ge(w_high, n + 1)
                    nc.vector.scalar_tensor_tensor(w[1][:, first:end], staged[:, first:end], float(scale),
                                                   w[0][:, first:end].bitcast(F32), ALU.mult, ALU.subtract).then_inc(w_low, 1)
                dve.wait_ge(consts_loaded, 16 * len(consts))
                if causal:
                    nc.vector.memset(ones_row[:], 1.0)
                    make_masks(nc, masks_bf, mask).then_inc(consts_ready, 1)
                else:
                    for half in range(2):
                        dve.wait_ge(consts_loaded, 16 * (half + 1))
                        at = slice(half * RELATIVE // 2, (half + 1) * RELATIVE // 2)
                        nc.vector.tensor_reduce(neg_bias[:, at], table[:], AX.X, ALU.add, negate=True).then_inc(consts_step, 1)
                    dve.wait_ge(consts_step, 2)
                    nc.vector.tensor_scalar(neg_bias[:], neg_bias[:], 1.0 / D, None, ALU.mult).then_inc(consts_ready, 1)
                    dve.wait_ge(consts_ready, 1)

                def step(u, n):
                    kind, i = cfg.steps[n]
                    if kind == "q_stack":
                        return
                    dve.wait_ge(step_done, u.b * NSTEP + n + 1)
                    p = p_bank[n % 2]
                    if kind in ("q", "k"):
                        dve.wait_ge(step_high, u.b * 3 + n + 1)
                        nc.vector.tensor_tensor(qk[n][1][:], p[:].rearrange("p (k t) -> p k t", k=KT),
                                                qk[n][0][:].bitcast(F32), ALU.subtract).then_inc(step_read, 1)
                    elif kind == "v":
                        dve.wait_ge(step_high, u.b * 3 + n + 1)
                        high, low = values[u.parity]
                        nc.vector.tensor_tensor(low[:], p[:].rearrange("p (t h d) -> p t h d", t=QT, h=H),
                                                high[:].bitcast(F32), ALU.subtract).then_inc(step_read, 1)
                    else:
                        need(dve, scores_done, (u.b - 1) * H)
                        nc.vector.tensor_copy(stack[1][u.parity][:, 2 * i:2 * i + 2, :], p[:].rearrange("p (k t) -> p k t", k=2))\
                            .then_inc(step_read, 1)

                def score(u, h):
                    m = u.slot(h)
                    dve.wait_ge(scores_done, m + 1)
                    need(dve, probs_ready, m - 1)
                    if not causal:
                        nc.vector.memset(carrier[h % 2][:], 0.0)
                    for t in range(QT):
                        s = s_bank[h % 2][:, score_columns(causal, t)]
                        if causal:
                            ins = nc.vector.tensor_reduce(bound[h % 2][:, t:t + 1], s, AX.X, ALU.max, negate=True)
                        else:
                            at = P * (1 - t)
                            ins = nc.vector.tensor_tensor_reduce(
                                out=neg_scores[h % 2][:, t, :], in0=s, in1=neg_bias[:, at:at + S], scale=1.0, scalar=BIG,
                                op0=ALU.add, op1=ALU.min, accum_out=bound[h % 2][:, t:t + 1])
                    ins.then_inc(bound_ready, 1)

                def transposed(u, h):
                    dve.wait_ge(t_high, u.slot(h) + 1)
                    nc.vector.tensor_tensor(probs_t[h % 4][1][:], t_bank[h % 2][:, 0:NB], probs_t[h % 4][0][:].bitcast(F32),
                                            ALU.subtract).then_inc(t_low, 1)

                def invert(u, n):
                    dve.wait_ge(o_copied, (u.b + 1) * BANKS)
                    at = slice(n * KT * S // CHUNKS, (n + 1) * KT * S // CHUNKS)
                    nc.vector.reciprocal(totals[u.parity][:, at], totals[u.parity][:, at]).then_inc(inv_ready, 1)
                    if n == CHUNKS - 1:
                        dve.wait_ge(inv_ready, (u.b + 1) * CHUNKS)
                        nc.vector.tensor_tensor(weighted[u.parity][:], weighted[u.parity][:], totals[u.parity][:], ALU.mult).then_inc(out_ready, 1)

                def split_out(u):
                    dve.wait_ge(out_t_high, u.b + 1)
                    nc.vector.tensor_tensor(out_t[1][:], as_tiles(weighted[u.parity]), out_t[0][:].bitcast(F32), ALU.subtract).then_inc(out_t_low, 1)

                def project_out(u):
                    dve.wait_ge(y_done, u.b + 1)
                    tiles = x[:, bass.ds(u.b * QT, QT), :]
                    nc.vector.tensor_tensor(tiles, p_bank[1][:].rearrange("p (t c) -> p t c", t=QT), tiles, ALU.add)\
                        .then_inc(y_added, 1)

                over_slots(dve, step, transposed, score, lambda u, h: None, lambda u, bp: None, split_out, project_out,
                           invert=invert, score_first=True, late_step="end")

            @block.gpsimd
            def _(pool):
                def of_heads(t, first, columns):
                    return t[:, 0:FULL].rearrange("p (t h w) -> p t h w", t=QT, w=WINDOW)[:, :, first[0]:first[1], columns:columns + D]

                nc.gpsimd.memset(unit[:], 1.0)
                for part in range(2):
                    ins = nc.gpsimd.memset(windows[part][:].bitcast(F32), 0.0)
                ins.then_inc(windows_ready, 1)
                pool.wait_ge(windows_ready, 1)
                nc.gpsimd.memset(of_heads(windows[0], (0, H), ONES_AT).bitcast(F32), 1.0).then_inc(windows_ready, 1)
                pool.wait_ge(windows_ready, 2)

                one = unit[:].rearrange("p (a b c) -> p a b c", a=1, b=1).to_broadcast([P, QT, PAIR, D])

                def work(u):
                    for bp in range(BANKS):
                        heads = (bp * PAIR, (bp + 1) * PAIR)
                        if bp == 0:
                            wait_step_read(pool, u.b, 2)
                        need(pool, o_done, (u.b - 1) * H + heads[1])
                        for part in range(2):
                            source = values[u.parity][part][:, :, heads[0]:heads[1], :].bitcast(F32)
                            ins = nc.gpsimd.tensor_tensor(of_heads(windows[part], heads, AT), source, one, ALU.mult)
                        ins.then_inc(spread, 1)

                over_batches(pool, work)


HALF_ROWS = P // 2


class Experts:

    def __init__(self, experts, top, groups, gated, act, router, capacity=None):
        self.E, self.top, self.NG, self.gated, self.act = experts, top, groups, gated, act
        self.router, self.capacity = router, capacity
        self.up = (2 if gated else 1) * KT * P
        self.down_at = self.up
        self.pick_at = self.up + C
        self.ones_row = experts < HALF_ROWS
        self.width = self.pick_at + P


def route_stage(core, cfg, w_in, gates_t, consts_in, early_loads):
    nc, bank, E = core.nc, core.bank, cfg.E
    FILL = 8 - cfg.top
    CHUNK = 512
    NC_ = TILES * P // CHUNK
    TC = CHUNK // P
    GROUPS_OF = 4 if cfg.router == "limited" else 0
    with Stage(core) as st:
        staged = st.sb("staged", [P, KT, E])
        w = [st.sb("w", [P, KT, E], F32R) for _ in range(2)]
        logits_t = [st.sb("logits_t", [E, CHUNK]) for _ in range(2)]
        logits = st.sb("logits", [P, TILES, E])
        scored = st.sb("scored", [P, TILES, E])
        padded = st.sb("padded", [P, TILES, E + FILL])
        replaced = st.sb("replaced", [P, TILES, E + FILL])
        best = st.sb("best", [P, TILES, 8])
        chosen = st.sb("chosen", [P, TILES, E])
        total, inv, tile_max = (st.sb(n, [P, TILES]) for n in ("total", "inv", "tile_max"))
        gates = st.sb("gates", [P, TILES, P])
        w_loaded, w_high, w_low = st.sem("w_loaded"), st.sem("w_high"), st.sem("w_low")
        t_done, t_copied = st.sem("t_done"), st.sem("t_copied")
        logits_done, logits_ready = st.sem("logits_done"), st.sem("logits_ready")
        scored_ready, chain, gates_ready = st.sem("scored_ready"), st.sem("chain"), st.sem("gates_ready")
        g_done, g_high, g_low = st.sem("g_done"), st.sem("g_high"), st.sem("g_low")
        shifted_ready = st.sem("shifted_ready")
        if cfg.capacity:
            before = st.sb("before", [P, P])
            before_bf, ones_bf = st.sb("before_bf", [P, P], BF16), st.sb("ones_bf", [P, P], BF16)
            chosen_bf, earlier_bf = st.sb("chosen_bf", [P, TILES, E], BF16), st.sb("earlier_bf", [P, TILES, E], BF16)
            chosen_ready, position_done = st.sem("chosen_ready"), st.sem("position_done")
        if GROUPS_OF:
            group_values = st.sb("group_values", [P, TILES, 8 + 6])
            group_replaced = st.sb("group_replaced", [P, TILES, 8 + 6])
            group_chosen = st.sb("group_chosen", [P, TILES, GROUPS_OF])

        norm_stage(core, [(staged[:], w_in, w_loaded)] + ([(before[:], consts_in[0], w_loaded)] if cfg.capacity else [])
                   + early_loads)

        with nc.Block() as block:

            @block.tensor
            def _(pe):
                pe.wait_ge(w_low, 1)

                def project(c, par):
                    need(pe, t_copied, c - 1)
                    n = 0
                    for kt in range(KT):
                        for a, m in ((0, 0), (0, 1), (1, 0)):
                            zz = (core.norm_t_high, core.norm_t_low)[m]
                            ins = nc.tensor.matmul(bank[par][0:E, :], w[a][:, kt, :], zz[:, kt, bass.ds(c * CHUNK, CHUNK)],
                                                   start=(n == 0), stop=(n == 5))
                            n += 1
                    ins.then_inc(t_done, 1)

                def back(c, par):
                    pe.wait_ge(t_copied, c + 1)
                    need(pe, logits_ready, c - 1)
                    for t in range(TC):
                        ins = nc.tensor.transpose(bank[2 + par][:, t * E:(t + 1) * E], logits_t[par][:, t * P:(t + 1) * P],
                                                  core.ident[0:E, 0:E])
                    ins.then_inc(logits_done, 1)

                project(0, 0)
                for c in range(NC_):
                    if c + 1 < NC_:
                        project(c + 1, (c + 1) % 2)
                    back(c, c % 2)
                if cfg.capacity:
                    pe.wait_ge(chosen_ready, 1)
                    for t in range(TILES):
                        to = bank[4 + t // 8][:, (t % 8) * E:(t % 8 + 1) * E]
                        nc.tensor.matmul(to, before_bf[:], chosen_bf[:, t, :], start=True, stop=False)
                        ins = nc.tensor.matmul(to, ones_bf[:], earlier_bf[:, t, :], start=False, stop=True)
                    ins.then_inc(position_done, 1)
                pe.wait_ge(gates_ready, 1)
                for t in range(TILES):
                    b = t // 4
                    need(pe, g_low, b - 1)
                    ins = nc.tensor.transpose(bank[b % 2][:, (t % 4) * P:(t % 4 + 1) * P], gates[:, t, :], core.ident[:])
                    if t % 4 == 3:
                        ins.then_inc(g_done, 1)

            @block.scalar
            def _(act):
                act.wait_ge(w_loaded, 16 * (2 if cfg.capacity else 1))
                nc.scalar.activation(w[0][:], staged[:], ACT.Copy).then_inc(w_high, 1)
                for c in range(NC_):
                    act.wait_ge(t_done, c + 1)
                    need(act, logits_done, c - 1)
                    nc.scalar.activation(logits_t[c % 2][:], bank[c % 2][0:E, :], ACT.Copy).then_inc(t_copied, 1)
                if cfg.router == "softmax":
                    act.wait_ge(shifted_ready, 1)
                    nc.scalar.activation(scored[:], scored[:], ACT.Exp).then_inc(scored_ready, 1)
                else:
                    act.wait_ge(logits_ready, NC_)
                    nc.scalar.activation(scored[:], logits[:], ACT.Sigmoid).then_inc(scored_ready, 1)
                for b in range(TILES // 4):
                    act.wait_ge(g_done, b + 1)
                    nc.scalar.activation(gates_t[:, b * 512:(b + 1) * 512], bank[b % 2][:], ACT.Copy).then_inc(g_high, 1)

            @block.vector
            def _(dve):
                steps = [0]

                def after(ins):
                    steps[0] += 1
                    ins.then_inc(chain, 1)
                    dve.wait_ge(chain, steps[0])

                def spread(t, n):
                    return t.rearrange("p (t a) -> p t a", a=1).to_broadcast([P, TILES, n])

                def choose(values, without, chosen_of, n, k):
                    low = max(n, 8)
                    for t in range(TILES):
                        ins = nc.vector.max(best[:, t, :], values[:, t, 0:low])
                    after(ins)
                    after(nc.vector.tensor_copy(best[:, :, k:8], values[:, :, low:low + 8 - k]))
                    for t in range(TILES):
                        ins = nc.vector.match_replace(without[:, t, :], best[:, t, :], values[:, t, :], -BIG)
                    after(ins)
                    after(nc.vector.tensor_tensor(chosen_of[:], without[:, :, 0:n], values[:, :, 0:n], ALU.not_equal))

                dve.wait_ge(w_high, 1)
                nc.vector.tensor_tensor(w[1][:], staged[:], w[0][:].bitcast(F32), ALU.subtract).then_inc(w_low, 1)
                after(nc.vector.memset(gates[:], 0.0))
                nc.vector.memset(padded[:], BIG)
                if GROUPS_OF:
                    after(nc.vector.memset(group_values[:], BIG))
                    nc.vector.memset(group_values[:, :, GROUPS_OF:8], -BIG)
                if cfg.ones_row:
                    nc.vector.memset(gates[:, :, E:E + 1], 1.0)
                for c in range(NC_):
                    dve.wait_ge(logits_done, c + 1)
                    nc.vector.tensor_copy(logits[:, c * TC:(c + 1) * TC, :],
                                          bank[2 + c % 2][:, 0:TC * E].rearrange("p (t e) -> p t e", t=TC)).then_inc(logits_ready, 1)
                dve.wait_ge(logits_ready, NC_)
                if cfg.router == "softmax":
                    after(nc.vector.tensor_reduce(tile_max[:], logits[:], AX.X, ALU.max))
                    nc.vector.tensor_tensor(scored[:], logits[:], spread(tile_max[:], E), ALU.subtract).then_inc(shifted_ready, 1)
                if GROUPS_OF:
                    after(nc.vector.tensor_reduce(group_values[:, :, 0:GROUPS_OF],
                                                  logits[:].rearrange("p t (g n) -> p t g n", g=GROUPS_OF), AX.X, ALU.max))
                    choose(group_values, group_replaced, group_chosen, GROUPS_OF, 2)
                    after(nc.vector.tensor_scalar(group_chosen[:], group_chosen[:], -MASKED, MASKED, ALU.mult, ALU.add))
                    after(nc.vector.tensor_tensor(
                        padded[:, :, 0:E].rearrange("p t (g n) -> p t g n", g=GROUPS_OF),
                        logits[:].rearrange("p t (g n) -> p t g n", g=GROUPS_OF),
                        group_chosen[:].rearrange("p t (g a) -> p t g a", a=1).to_broadcast([P, TILES, GROUPS_OF, E // GROUPS_OF]),
                        ALU.add))
                else:
                    after(nc.vector.tensor_copy(padded[:, :, 0:E], logits[:]))
                choose(padded, replaced, chosen, E, cfg.top)
                if cfg.capacity:
                    nc.vector.tensor_copy(before_bf[:], before[:])
                    nc.vector.memset(ones_bf[:], 1.0)
                    after(nc.vector.memset(earlier_bf[:, 0, :], 0.0))
                    after(nc.vector.tensor_copy(chosen_bf[:], chosen[:]))
                    for t in range(1, TILES):
                        ins = nc.vector.tensor_tensor(earlier_bf[:, t, :], earlier_bf[:, t - 1, :], chosen_bf[:, t - 1, :], ALU.add)
                        if t < TILES - 1:
                            after(ins)
                    ins.then_inc(chosen_ready, 1)
                dve.wait_ge(scored_ready, 1)
                if cfg.router == "softmax":
                    after(nc.vector.tensor_reduce(total[:], scored[:], AX.X, ALU.add))
                    after(nc.vector.tensor_tensor(chosen[:], chosen[:], scored[:], ALU.mult))
                else:
                    after(nc.vector.tensor_tensor(chosen[:], chosen[:], scored[:], ALU.mult))
                    after(nc.vector.tensor_reduce(total[:], chosen[:], AX.X, ALU.add))
                after(nc.vector.reciprocal(inv[:], total[:]))
                if cfg.capacity:
                    after(nc.vector.tensor_tensor(chosen[:], chosen[:], spread(inv[:], E), ALU.mult))
                    dve.wait_ge(position_done, 1)
                    for half, at in ((0, 0), (1, 0), (0, HALF_ROWS), (1, HALF_ROWS)):
                        rows = slice(8 * half, 8 * half + 8)
                        ins = nc.vector.scalar_tensor_tensor(
                            gates[:, rows, at:at + E], bank[4 + half][:].rearrange("p (t e) -> p t e", e=E), float(cfg.capacity),
                            chosen[:, rows, :], ALU.is_lt, ALU.mult)
                    ins.then_inc(gates_ready, 1)
                else:
                    for at in (0, HALF_ROWS):
                        ins = nc.vector.tensor_tensor(gates[:, :, at:at + E], chosen[:], spread(inv[:], E), ALU.mult)
                    ins.then_inc(gates_ready, 1)
                for b in range(TILES // 4):
                    dve.wait_ge(g_high, b + 1)
                    at = slice(b * 512, (b + 1) * 512)
                    low = gates_t[HALF_ROWS:P, at]
                    nc.vector.tensor_tensor(low, bank[b % 2][HALF_ROWS:P, :], low.bitcast(F32), ALU.subtract).then_inc(g_low, 1)


def experts_stage(core, cfg, w_in, gates_t, staged, w_loaded):
    nc, x, bank, NG = core.nc, core.x, core.bank, cfg.NG
    HALF, STEP = TILES * P // 2, 512
    a_bank, up_bank, pick_bank, y_bank = bank[0:2], bank[2], bank[3], bank[4:8]
    with Stage(core) as st:
        w_high = [st.sb("w_high", [P, cfg.width], F32R) for _ in range(2)]
        w_low = [st.sb("w_low", [P, cfg.pick_at], F32R) for _ in range(2)]
        acted, hidden = ([st.sb(name, [P, STEP]) for _ in range(2)] for name in ("acted", "hidden"))
        hidden_parts = [[st.sb("hidden_parts", [P, STEP], F32R) for _ in range(2)] for _ in range(2)]
        zeros = st.sb("zeros", [P, STEP], BF16)
        ones = st.sb("ones", [1, STEP], BF16)
        high_ready, low_ready, zeros_ready = st.sem("high_ready"), st.sem("low_ready"), st.sem("zeros_ready")
        a_done, up_done, pick_done = st.sem("a_done"), st.sem("up_done"), st.sem("pick_done")
        acted_ready, gated_ready, hidden_ready = st.sem("acted_ready"), st.sem("gated_ready"), st.sem("hidden_ready")
        hidden_high, hidden_low = st.sem("hidden_high"), st.sem("hidden_low")
        down_done, y_done, y_read = st.sem("down_done"), st.sem("y_done"), st.sem("y_read")

        class Group:

            def __init__(self, c, i, k):
                self.c, self.i, self.k = c, i, k
                self.j = 2 * i + k
                self.u = c * NG + self.j
                self.parity = (c * NG + k) % 2
                self.turn = i + (c * NG + k) // 2
                known = isinstance(i, int)
                self.first, self.last = known and self.j == 0, known and self.j == NG - 1
                self.very_last = self.last and c == 1

            def next(self):
                return Group(self.c + 1, 0, 0) if self.last else Group(self.c, self.i, self.k + 1)

            def before(self):
                return Group(self.c - 1, 0, NG - 1) if self.first else Group(self.c, self.i, self.k - 1)

            def step(self, s):
                return 2 * self.u + s

        def over_groups(eng, work):
            for c in range(2):
                work(Group(c, 0, 0))
                pairs = (NG - 2) // 2
                with eng.Fori(0, pairs) as i:
                    work(Group(c, i, 1))
                    work(Group(c, i, 2))
                for k in range(2 * pairs + 1, NG):
                    work(Group(c, 0, k))

        with nc.Block() as block:

            @block.sync
            def _(sp):
                def work(g):
                    if not g.very_last:
                        need(sp, low_ready, g.u)
                        source = w_in[0] if g.last else w_in[bass.ds(g.j + 1, 1)].rearrange("a p n -> p (a n)")
                        sp.dma_start(staged[1 - g.parity][:], source).then_inc(w_loaded[1 - g.parity], 16)

                over_groups(sp, work)

            @block.tensor
            def _(pe):
                def passes(out, operands, start=True, stop=True):
                    n = len(operands)
                    for i, (a, c) in enumerate(operands):
                        ins = nc.tensor.matmul(out, a, c, start=(start and i == 0), stop=(stop and i == n - 1))
                    return ins

                z = (core.norm_t_high, core.norm_t_low)

                def up(g, s):
                    r = g.step(s)
                    if s == 0:
                        pe.wait_ge(low_ready, g.u + 1)
                    tokens = slice(g.c * HALF + s * STEP, g.c * HALF + (s + 1) * STEP)
                    w = (w_high[g.parity], w_low[g.parity])

                    def product(out, at):
                        return passes(out, [(w[a][:, at + kt * P:at + (kt + 1) * P], z[b][:, kt, tokens])
                                            for kt in range(KT) for a, b in ((0, 0), (0, 1), (1, 0))])

                    need(pe, acted_ready, r - 1)
                    product(a_bank[s][:], 0).then_inc(a_done, 1)
                    if cfg.gated:
                        need(pe, gated_ready, r)
                        product(up_bank[:], KT * P).then_inc(up_done, 1)
                    need(pe, hidden_ready, r)
                    if g.last and not cfg.ones_row:
                        pick = (ones[:, 0:P], ones[:])
                    else:
                        pick = (w[0][:, cfg.pick_at:cfg.pick_at + P], gates_t[:, tokens])
                    passes(pick_bank[:], [pick]).then_inc(pick_done, 1)

                def down(g, s):
                    r = g.step(s)
                    pe.wait_ge(hidden_low, r + 1)
                    if g.first and s == 0:
                        need(pe, y_read, g.c)
                        for y in y_bank:
                            nc.tensor.matmul(y[:], zeros[:, 0:P], zeros[:], start=True, stop=False)
                    for t in range(STEP // P):
                        y = y_bank[2 * s + t // 2][:, (t % 2) * C:(t % 2 + 1) * C]
                        tokens = slice(t * P, (t + 1) * P)
                        ins = passes(y, [(hidden_parts[s][a][:, tokens],
                                          (w_high, w_low)[b][g.parity][:, cfg.down_at:cfg.down_at + C])
                                         for a, b in ((0, 0), (0, 1), (1, 0))], start=False, stop=False)
                    ins.then_inc(down_done, 1)
                    if g.last and s == 1:
                        for y in y_bank:
                            ins = nc.tensor.matmul(y[:], zeros[:, 0:P], zeros[:], start=False, stop=True)
                        ins.then_inc(y_done, 1)

                pe.wait_ge(zeros_ready, 1)

                def work(g):
                    up(g, 0)
                    if not (g.first and g.c == 0):
                        down(g.before(), 1)
                    up(g, 1)
                    down(g, 0)

                over_groups(pe, work)
                down(Group(1, 0, NG - 1), 1)

            @block.scalar
            def _(act):
                def split(g):
                    act.wait_ge(w_loaded[g.parity], (g.turn + 1) * 16)
                    need(act, down_done, 2 * (g.u - 1))
                    nc.scalar.activation(w_high[g.parity][:], staged[g.parity][:], ACT.Copy).then_inc(high_ready, 1)

                split(Group(0, 0, 0))

                def work(g):
                    for s in range(2):
                        r = g.step(s)
                        act.wait_ge(a_done, r + 1)
                        need(act, hidden_ready, r - 1)
                        nc.scalar.activation(acted[s][:], a_bank[s][:], cfg.act).then_inc(acted_ready, 1)
                        act.wait_ge(hidden_ready, r + 1)
                        need(act, down_done, r - 1)
                        nc.scalar.activation(hidden_parts[s][0][:], hidden[s][:], ACT.Copy).then_inc(hidden_high, 1)
                        if s == 0 and not g.very_last:
                            split(g.next())

                over_groups(act, work)

            @block.vector
            def _(dve):
                nc.vector.memset(ones[:], 1.0)
                nc.vector.memset(zeros[:], 0.0).then_inc(zeros_ready, 1)

                def split(g):
                    dve.wait_ge(high_ready, g.u + 1)
                    nc.vector.tensor_tensor(w_low[g.parity][:], staged[g.parity][:, 0:cfg.pick_at],
                                            w_high[g.parity][:, 0:cfg.pick_at].bitcast(F32), ALU.subtract).then_inc(low_ready, 1)

                split(Group(0, 0, 0))

                def add_to_x(c):
                    dve.wait_ge(y_done, c + 1)
                    for i, y in enumerate(y_bank):
                        tile = c * TILES // 2 + 2 * i
                        tiles = x[:, tile:tile + 2, :]
                        ins = nc.vector.tensor_tensor(tiles, y[:].rearrange("p (t c) -> p t c", t=2), tiles, ALU.add)
                    ins.then_inc(y_read, 1)

                def work(g):
                    for s in range(2):
                        r = g.step(s)
                        dve.wait_ge(acted_ready, r + 1)
                        source = acted[s]
                        need(dve, hidden_high, r - 1)
                        need(dve, hidden_low, r - 1)
                        if cfg.gated:
                            dve.wait_ge(up_done, r + 1)
                            nc.vector.tensor_tensor(hidden[s][:], acted[s][:], up_bank[:], ALU.mult).then_inc(gated_ready, 1)
                            dve.wait_ge(gated_ready, r + 1)
                            source = hidden[s]
                        dve.wait_ge(pick_done, r + 1)
                        nc.vector.tensor_tensor(hidden[s][:], source[:], pick_bank[:], ALU.mult).then_inc(hidden_ready, 1)
                        if s == 1 and g.first and g.c == 1:
                            add_to_x(0)
                        dve.wait_ge(hidden_high, r + 1)
                        dve.wait_ge(hidden_ready, r + 1)
                        nc.vector.tensor_tensor(hidden_parts[s][1][:], hidden[s][:], hidden_parts[s][0][:].bitcast(F32),
                                                ALU.subtract).then_inc(hidden_low, 1)
                        if s == 0 and not g.very_last:
                            split(g.next())

                over_groups(dve, work)
                add_to_x(1)


def thought_stage(core, w_in, gate_w_in, rows_in, columns_in, wide_rows_in, steps=4, hidden=1024, eps=1e-6):
    nc, x, bank = core.nc, core.x, core.bank
    HB = hidden // P
    AGG, BC, D1, D2 = 0, KT * C, 2 * KT * C, 2 * KT * C + KT * hidden
    with Stage(core) as st:
        w = st.sb("w", [P, D2 + HB * C])
        gate_staged = st.sb("gate_staged", [P, KT, C])
        gate_w = [st.sb("gate_w", [P, KT, C], F32R) for _ in range(2)]
        rows = st.sb("rows", [B, 6, C])
        columns = st.sb("columns", [P, HB + 2 * KT])
        wide_rows = st.sb("wide_rows", [P, 2, C])
        gate = st.sb("gate", [P, KT, TILES * P])
        last, current, thought, thought_bias = (st.sb(n, [B, C]) for n in ("last", "current", "thought", "thought_bias"))
        stats8, meanvar8, rstd8 = st.sb("stats8", [B, 6]), st.sb("meanvar8", [B, 2]), st.sb("rstd8", [B, 1])
        half8, half = st.sb("half8", [B, 1]), st.sb("half", [P, QT])
        var8, eps_tile = st.sb("var8", [B, 1]), st.sb("eps_tile", [P, QT])
        current_t, act_in, acted = st.sb("current_t", [P, KT, B]), st.sb("act_in", [P, HB, B]), st.sb("acted", [P, HB, B])
        message_t = st.sb("message_t", [P, KT, B])
        AHEAD = 4
        sent = [st.sb("sent", [P, KT, S]) for _ in range(AHEAD)]
        z = st.sb("z", [P, TILES, C])
        stats, meanvar = st.sb("stats", [P, TILES, 6]), st.sb("meanvar", [P, TILES, 2])
        var_eps, rstd, shift = (st.sb(n, [P, TILES]) for n in ("var_eps", "rstd", "shift"))

        loaded, last_loaded = st.sem("loaded"), st.sem("last_loaded")
        gate_high, gate_low, gate_done, gate_ready = st.sem("gate_high"), st.sem("gate_low"), st.sem("gate_done"), st.sem("gate_ready")
        chain, var8_ready, rstd8_ready, pool_chain = st.sem("chain"), st.sem("var8_ready"), st.sem("rstd8_ready"), st.sem("pool_chain")
        current_ready, current_t_done, current_t_ready = st.sem("current_ready"), st.sem("current_t_done"), st.sem("current_t_ready")
        product_done, act_in_ready, acted_ready = st.sem("product_done"), st.sem("act_in_ready"), st.sem("acted_ready")
        message_ready, sent_ready, sent_t_done, mixed_ready = st.sem("message_ready"), st.sem("sent_ready"), st.sem("sent_t_done"), st.sem("mixed_ready")
        var_ready, rstd_ready, half_ready = st.sem("var_ready"), st.sem("rstd_ready"), st.sem("half_ready")
        z_ready, beta_added, stats_ready, shift_ready = st.sem("z_ready"), st.sem("beta_added"), st.sem("stats_ready"), st.sem("shift_ready")
        z_normed, gamma_ready, x_written = st.sem("z_normed"), st.sem("gamma_ready"), st.sem("x_written")
        ROUNDS = 3 + steps
        t_bank, wide_bank, row_bank = bank[4], bank[5], bank[6]

        norm_stage(core, [(last[:], x[P - 1:P, QT - 1::QT, :], last_loaded), (gate_staged[:], gate_w_in, last_loaded)] + [
            (t[:], source, loaded) for t, source in ((rows, rows_in), (columns, columns_in), (w, w_in), (wide_rows, wide_rows_in))])

        def tiles(t, b):
            return t[:, b * QT:(b + 1) * QT]

        with nc.Block() as block:

            @block.gpsimd
            def _(pool):
                nc.gpsimd.memset(half8[:], -0.5)
                nc.gpsimd.memset(eps_tile[:], eps)
                nc.gpsimd.memset(half[:], -0.5).then_inc(half_ready, 1)
                pool.wait_ge(half_ready, 1)
                for n in range(2 + steps):
                    pool.wait_ge(var8_ready, n + 1)
                    nc.gpsimd.tensor_scalar(var8[:], meanvar8[:, 1:2], 1.0, 1e-5 if n == 0 else eps, ALU.mult, ALU.add)\
                        .then_inc(pool_chain, 1)
                    pool.wait_ge(pool_chain, n + 1)
                    nc.gpsimd.tensor_tensor(rstd8[:], var8[:], half8[:], ALU.pow).then_inc(rstd8_ready, 1)

                pool.wait_ge(loaded, 64)
                pool.wait_ge(z_ready, B)
                for b in range(B):
                    nc.gpsimd.tensor_tensor(tiles(x, b), tiles(x, b), wide_rows[:, 1:2, :].to_broadcast([P, QT, C]), ALU.add)\
                        .then_inc(beta_added, 1)
                for b in range(B):
                    pool.wait_ge(var_ready, b + 1)
                    nc.gpsimd.tensor_tensor(tiles(var_eps, b), tiles(meanvar, b)[:, :, 1], eps_tile[:], ALU.add)\
                        .then_inc(pool_chain, 1)
                    pool.wait_ge(pool_chain, 2 + steps + b + 1)
                    nc.gpsimd.tensor_tensor(tiles(rstd, b), tiles(var_eps, b), half[:], ALU.pow).then_inc(rstd_ready, 1)

            @block.tensor
            def _(pe):
                pe.wait_ge(gate_low, 1)

                def gates(i):
                    for par in range(2):
                        b = 2 * i + par
                        need(pe, gate_ready, b - 1)
                        for c in range(KT):
                            n = 0
                            for kt in range(KT):
                                for a, m in ((0, 0), (0, 1), (1, 0)):
                                    z = (core.norm_t_high, core.norm_t_low)[m]
                                    ins = nc.tensor.matmul(bank[par][:, c * S:(c + 1) * S], gate_w[a][:, kt, c * P:(c + 1) * P],
                                                           z[:, kt, bass.ds(b * S, S)], start=(n == 0), stop=(n == 5))
                                    n += 1
                        ins.then_inc(gate_done, 1)

                gates(0)
                with pe.Fori(1, PAIRS) as i:
                    gates(i)

                pe.wait_ge(loaded, 64)

                def transpose_current(n):
                    pe.wait_ge(current_ready, n + 1)
                    for kt in range(KT):
                        ins = nc.tensor.transpose(t_bank[:, kt * B:(kt + 1) * B], current[:, kt * P:(kt + 1) * P],
                                                  core.ident[0:B, 0:B])
                    ins.then_inc(current_t_done, 1)
                    pe.wait_ge(current_t_ready, n + 1)

                def by_rows(at, operands, count):
                    for kt in range(count):
                        ins = nc.tensor.matmul(row_bank[0:B, 0:C], operands[:, kt, :], w[:, at + kt * C:at + (kt + 1) * C],
                                               start=(kt == 0), stop=(kt == count - 1))
                    ins.then_inc(product_done, 1)

                def by_columns(at, width):
                    for c in range(width // P):
                        for kt in range(KT):
                            ins = nc.tensor.matmul(wide_bank[:, c * B:(c + 1) * B],
                                                   w[:, at + kt * width + c * P:at + kt * width + (c + 1) * P],
                                                   current_t[:, kt, :], start=(kt == 0), stop=(kt == KT - 1))
                    ins.then_inc(product_done, 1)

                transpose_current(0)
                by_rows(AGG, current_t, KT)
                for n in range(steps):
                    transpose_current(1 + n)
                    by_columns(D1, hidden)
                    pe.wait_ge(acted_ready, n + 1)
                    by_rows(D2, acted, HB)
                transpose_current(1 + steps)
                by_columns(BC, C)

                def back(i):
                    for par in range(AHEAD):
                        b = AHEAD * i + par
                        pe.wait_ge(sent_ready, b + 1)
                        need(pe, mixed_ready, b - AHEAD + 1)
                        for t in range(QT):
                            for kt in range(KT):
                                ins = nc.tensor.transpose(bank[par][:, t * C + kt * P:t * C + (kt + 1) * P],
                                                          sent[par][:, kt, t * P:(t + 1) * P], core.ident[:])
                        ins.then_inc(sent_t_done, 1)

                back(0)
                with pe.Fori(1, B // AHEAD) as i:
                    back(i)

            @block.scalar
            def _(act):
                act.wait_ge(last_loaded, 32)
                nc.scalar.activation(gate_w[0][:], gate_staged[:], ACT.Copy).then_inc(gate_high, 1)
                act.wait_ge(loaded, 64)
                with act.Fori(0, PAIRS) as i:
                    for par in range(2):
                        b = 2 * i + par
                        act.wait_ge(gate_done, b + 1)
                        for c in range(KT):
                            ins = nc.scalar.activation(gate[:, c, bass.ds(b * S, S)], bank[par][:, c * S:(c + 1) * S],
                                                       ACT.Sigmoid, bias=columns[:, HB + c:HB + c + 1])
                        ins.then_inc(gate_ready, 1)
                for b in range(B):
                    for t in (b * QT, b * QT + 1):
                        ins = nc.scalar.activation(z[:, t, :], x[:, t, :], ACT.Identity, bias=core.shift[:, t:t + 1],
                                                   scale=core.rstd[:, t:t + 1])
                    ins.then_inc(z_ready, 1)
                for n in range(steps):
                    act.wait_ge(act_in_ready, n + 1)
                    nc.scalar.activation(acted[:], act_in[:], ACT.Gelu).then_inc(acted_ready, 1)

                def send(b):
                    need(act, sent_t_done, b - AHEAD + 1)
                    for kt in range(KT):
                        ins = nc.scalar.activation(sent[b % AHEAD][:, kt, :], gate[:, kt, b * S:(b + 1) * S], ACT.Copy,
                                                   scale=message_t[:, kt, b:b + 1])
                    ins.then_inc(sent_ready, 1)

                act.wait_ge(message_ready, 1)
                act.wait_ge(gate_ready, B)
                for b in range(AHEAD):
                    send(b)
                for b in range(B):
                    act.wait_ge(shift_ready, b + 1)
                    for t in (b * QT, b * QT + 1):
                        ins = nc.scalar.activation(z[:, t, :], z[:, t, :], ACT.Identity, bias=shift[:, t:t + 1], scale=rstd[:, t:t + 1])
                    ins.then_inc(z_normed, 1)
                    if b + AHEAD < B:
                        send(b + AHEAD)

            @block.vector
            def _(dve):
                count = [0]

                def after(ins):
                    count[0] += 1
                    ins.then_inc(chain, 1)
                    dve.wait_ge(chain, count[0])

                dve.wait_ge(gate_high, 1)
                nc.vector.tensor_tensor(gate_w[1][:], gate_staged[:], gate_w[0][:].bitcast(F32), ALU.subtract).then_inc(gate_low, 1)
                dve.wait_ge(last_loaded, 32)
                dve.wait_ge(loaded, 64)

                def norm8(source, target, n, gamma=None, beta=None):
                    after(nc.vector.bn_stats(stats8[:], source[:]))
                    nc.vector.bn_aggr(meanvar8[:], stats8[:]).then_inc(var8_ready, 1)
                    dve.wait_ge(var8_ready, n + 1)
                    dve.wait_ge(rstd8_ready, n + 1)
                    ins = nc.vector.tensor_scalar(target[:], source[:], meanvar8[:, 0:1], rstd8[:, 0:1], ALU.subtract, ALU.mult)
                    if gamma is None:
                        after(ins)
                        return
                    after(ins)
                    after(nc.vector.tensor_tensor(target[:], target[:], rows[:, gamma, :], ALU.mult))
                    nc.vector.tensor_tensor(target[:], target[:], rows[:, beta, :], ALU.add).then_inc(current_ready, 1)

                def copy_transposed(n):
                    dve.wait_ge(current_t_done, n + 1)
                    nc.vector.tensor_copy(current_t[:], t_bank[:, 0:KT * B].rearrange("p (k b) -> p k b", k=KT)).then_inc(current_t_ready, 1)

                norm8(last, last, 0)
                norm8(last, current, 1, 0, 1)
                copy_transposed(0)
                dve.wait_ge(product_done, 1)
                after(nc.vector.tensor_tensor(thought[:], row_bank[0:B, 0:C], rows[:, 2, :], ALU.add))
                for n in range(steps):
                    norm8(thought, current, 2 + n, 3, 4)
                    copy_transposed(1 + n)
                    after(nc.vector.tensor_tensor(thought_bias[:], thought[:], rows[:, 5, :], ALU.add))
                    dve.wait_ge(product_done, 2 + 2 * n)
                    nc.vector.tensor_tensor(act_in[:], wide_bank[:, 0:HB * B].rearrange("p (h b) -> p h b", h=HB),
                                            columns[:, 0:HB].rearrange("p (h a) -> p h a", a=1).to_broadcast([P, HB, B]),
                                            ALU.add).then_inc(act_in_ready, 1)
                    dve.wait_ge(product_done, 3 + 2 * n)
                    after(nc.vector.tensor_tensor(thought[:], row_bank[0:B, 0:C], thought_bias[:], ALU.add))
                nc.vector.tensor_copy(current[:], thought[:]).then_inc(current_ready, 1)
                copy_transposed(1 + steps)
                dve.wait_ge(product_done, 2 + 2 * steps)
                nc.vector.tensor_tensor(message_t[:], wide_bank[:, 0:KT * B].rearrange("p (k b) -> p k b", k=KT),
                                        columns[:, HB + KT:HB + 2 * KT].rearrange("p (k a) -> p k a", a=1).to_broadcast([P, KT, B]),
                                        ALU.add).then_inc(message_ready, 1)
                dve.wait_ge(z_ready, B)

                def mix(b):
                    dve.wait_ge(sent_t_done, b + 1)
                    nc.vector.tensor_tensor(tiles(z, b), tiles(z, b), bank[b % AHEAD][:].rearrange("p (t c) -> p t c", t=QT), ALU.add)\
                        .then_inc(mixed_ready, 1)
                    dve.wait_ge(mixed_ready, b + 1)
                    for t in (b * QT, b * QT + 1):
                        ins = nc.vector.bn_stats(stats[:, t, :], z[:, t, :])
                    ins.then_inc(stats_ready, 1)
                    dve.wait_ge(stats_ready, b + 1)
                    for t in (b * QT, b * QT + 1):
                        ins = nc.vector.bn_aggr(meanvar[:, t, :], stats[:, t, :])
                    ins.then_inc(var_ready, 1)

                def make_shift(b):
                    dve.wait_ge(rstd_ready, b + 1)
                    nc.vector.scalar_tensor_tensor(tiles(shift, b), tiles(meanvar, b)[:, :, 0], -1.0, tiles(rstd, b),
                                                   ALU.mult, ALU.mult).then_inc(shift_ready, 1)

                def finish(b):
                    dve.wait_ge(z_normed, b + 1)
                    nc.vector.tensor_tensor(tiles(z, b), tiles(z, b), wide_rows[:, 0:1, :].to_broadcast([P, QT, C]), ALU.mult)\
                        .then_inc(gamma_ready, 1)
                    dve.wait_ge(gamma_ready, b + 1)
                    dve.wait_ge(beta_added, b + 1)
                    nc.vector.tensor_tensor(tiles(x, b), tiles(x, b), tiles(z, b), ALU.add).then_inc(x_written, 1)

                for b in range(B + 2):
                    if b < B:
                        mix(b)
                    if 1 <= b <= B:
                        make_shift(b - 1)
                    if b >= 2:
                        finish(b - 2)


def four_layers_kernel(nc, d, out):
    narrow = (NarrowAttention(16, causal=True), NarrowAttention(32, causal=False))
    wide = {2: WideAttention(4, 4, shared_kv=True, rope=False, causal=True, scale=1 / math.sqrt(P)),
            3: WideAttention(2, 8, shared_kv=False, rope=True, causal=False, scale=1 / math.sqrt(P))}
    experts = {0: Experts(64, 6, d["experts_0"].shape[0], True, ACT.Silu, "sigmoid", capacity=128),
               2: Experts(16, 2, d["experts_2"].shape[0], False, ACT.Gelu, "softmax"),
               3: Experts(32, 6, d["experts_3"].shape[0], True, ACT.Silu, "limited")}

    with ExitStack() as stack:
        core = Core(nc, stack)
        load_stage(core, d["x"], d["ident"])

        def feed_forward(layer):
            cfg, weights = experts[layer], d[f"experts_{layer}"]
            with Stage(core) as held:
                gates_t = held.sb("gates_t", [P, TILES * P], F32R)
                staged = [held.sb("staged", [P, cfg.width]) for _ in range(2)]
                w_loaded = [held.sem("w_loaded") for _ in range(2)]
                route_stage(core, cfg, d[f"router_{layer}"], gates_t, [d["earlier"]], [(staged[0][:], weights[0], w_loaded[0])])
                experts_stage(core, cfg, weights, gates_t, staged, w_loaded)

        narrow_attention_stage(core, narrow[0], d["attention_0"], d["select_0"], [d["mask"], d["out_bias_0"]])
        feed_forward(0)
        narrow_attention_stage(core, narrow[1], d["attention_1"], d["select_1"], [d["relative_1"]])
        thought_stage(core, d["thought_w"], d["thought_gate_w"], d["thought_rows"], d["thought_columns"], d["thought_wide_rows"])
        wide_attention_stage(core, wide[2], d["attention_2"], [d["position"], d["bias_2"], d["value_bias_2"], d["mask"]])
        feed_forward(2)
        wide_attention_stage(core, wide[3], d["attention_3"], [d["rotation"]])
        feed_forward(3)
        store_stage(core, out)



def by_contraction(w):
    return np.concatenate([w[at:at + P] for at in range(0, w.shape[0], P)], axis=1)


def narrow_weights(i, layer):
    wq, wk, wv, wo = (i[f"{layer}_attn_{n}"].T for n in ("wq", "wk", "wv", "wo"))
    wo = wo.reshape(4, 2, 32, C).transpose(1, 0, 2, 3).reshape(C, C)
    return np.concatenate([by_contraction(w) for w in (wq, wk, wv, wo)], axis=1)


def stack_selection(heads):
    dim = C // heads
    rows = 4 * dim
    per = P // rows
    s = np.zeros((P, 2, 4, 2, P), np.float32)
    for which, blocks in enumerate(((0, 1, 0, 1), (0, 0, 1, 1))):
        for tile in range(4):
            for head in range(per):
                for block, part in enumerate(blocks):
                    n = np.arange(dim)
                    s[(tile * per + head) * dim + n, which, tile, part, head * rows + block * dim + n] = 1
    return s


def relative_table(rel_pos):
    relative = np.arange(S + P)[None] - np.arange(P)[:, None] - P
    return rel_pos[np.clip(relative + 63, 0, 126)]


def position_encoding():
    ang = np.arange(S, dtype=np.float32)[:, None] * np.exp(-(np.log(np.float32(10000.0)) * np.arange(0, P, 2, dtype=np.float32) / np.float32(P)))
    pe = np.zeros((S, P), np.float32)
    pe[:, 0::2], pe[:, 1::2] = np.sin(ang), np.cos(ang)
    return pe.T


def rotation_table():
    inv = 1.0 / np.float32(10000.0) ** (np.arange(0, 64, 2, dtype=np.float32) / np.float32(64))
    angle = np.arange(S, dtype=np.float32)[:, None] * inv[None]
    c, s = np.cos(angle).T.astype(np.float32), np.sin(angle).T.astype(np.float32)
    table = np.stack([np.concatenate([c, -s], axis=1), np.concatenate([s, c], axis=1)], axis=1)
    scale = np.float32(1 / 8)
    return np.concatenate([table * scale, table * scale, table, table])


def wide_weights_2(i):
    wq, wkv, wo = (i[f"L2_attn_{n}"] for n in ("wq", "wkv", "wo"))
    return np.stack([np.concatenate([
        by_contraction(wq[:, g * 512:(g + 1) * 512]), by_contraction(wkv[:, g * 256:g * 256 + P]),
        by_contraction(wkv[:, g * 256 + P:(g + 1) * 256]), by_contraction(wo[g * 512:(g + 1) * 512])], axis=1) for g in range(4)])


def wide_biases_2(i):
    kv = i["L2_attn_bkv"].reshape(4, 2, P)
    columns = np.concatenate([i["L2_attn_bq"].reshape(4, 4, P), kv[:, :1]], axis=1).transpose(2, 0, 1)
    return columns, np.broadcast_to(kv[:, 1], (P, 4, P))


def wide_weights_3(i):
    wq, wk, wv, wo = (i[f"L3_attn_{n}"] for n in ("Wq", "Wk", "Wv", "Wo"))
    blocks = []
    for g in range(8):
        turned = np.stack([w[2048 + g * P:2048 + (g + 1) * P] for w in (wq, wk)]).reshape(4, 2, 32, C)
        parts = [by_contraction(turned.transpose(1, 0, 2, 3).reshape(2 * P, C).T)]
        parts += [by_contraction(w[g * 256:(g + 1) * 256].T) for w in (wq, wk)]
        parts += [by_contraction(wv[g * 256:(g + 1) * 256].T), by_contraction(wo.T[g * 256:(g + 1) * 256])]
        blocks.append(np.concatenate(parts, axis=1))
    return np.stack(blocks)


def hidden_groups(ups, down, owner):
    rows = down.shape[0]
    whole = -(-rows // P) * P
    ups = [np.concatenate([u, np.zeros((C, whole - rows), u.dtype)], axis=1) for u in ups]
    down = np.concatenate([down, np.zeros((whole - rows, C), down.dtype)])
    owner = np.concatenate([owner, np.full(whole - rows, owner[-1])])
    groups = []
    for at in range(0, whole, P):
        pick = np.zeros((P, P), np.float32)
        for half in (0, 64):
            pick[owner[at:at + P] % 64 + half, np.arange(P)] = 1
        groups.append(np.concatenate([by_contraction(u[:, at:at + P]) for u in ups] + [down[at:at + P], pick], axis=1))
    return groups


def flat(w):
    return w.transpose(1, 0, 2).reshape(C, -1)


def expert_weights(i):
    def get(layer, *names):
        return (i[f"L{layer}_ffn_{n}"] for n in names)
    up, down, shared_up, shared_down = get(0, "w_up", "w_down", "w_shared_up", "w_shared_down")
    first = hidden_groups([flat(up[:, :, :32]), flat(up[:, :, 32:])], down.reshape(-1, C), np.repeat(np.arange(64), 32))
    first += hidden_groups([shared_up[:, 64:], shared_up[:, :64]], shared_down, np.full(64, 64))
    up, down, shared_up, shared_down = get(2, "Wrt_up", "Wrt_down", "Wsh_up", "Wsh_down")
    second = hidden_groups([flat(up)], down.reshape(-1, C), np.repeat(np.arange(16), 128))
    second += hidden_groups([flat(shared_up)], shared_down.reshape(-1, C), np.full(256, 16))
    gate, up, down, shared_gate, shared_up, shared_down = get(3, "w_gate", "w_up", "w_down", "sw_gate", "sw_up", "sw_down")
    third = hidden_groups([flat(gate), flat(up)], down.reshape(-1, C), np.repeat(np.arange(32), 176))
    third += hidden_groups([shared_gate, shared_up], shared_down, np.full(352, 32))
    return {"experts_0": np.stack(first), "experts_2": np.stack(second), "experts_3": np.stack(third)}


def layouts(i):
    def thought(n):
        return i[f"L1_ffn_{n}"]

    def by_tile(w):
        return w.reshape(KT, P, -1).transpose(1, 0, 2)

    n = np.arange(P)
    bias_2, value_bias_2 = wide_biases_2(i)
    return {
        "x": i["L0_attn_x"].reshape(TILES, P, C).transpose(1, 0, 2),
        "ident": np.eye(P, dtype=np.float32),
        "mask": np.where(n[None] > n[:, None], np.float32(MASKED), np.float32(0)),
        "earlier": np.where(n[:, None] < n[None], np.float32(1), np.float32(0)),
        "attention_0": narrow_weights(i, "L0"), "select_0": stack_selection(16), "out_bias_0": i["L0_attn_bo"][None],
        "attention_1": narrow_weights(i, "L1"), "select_1": stack_selection(32),
        "relative_1": relative_table(i["L1_attn_rel_pos"]),
        "attention_2": wide_weights_2(i), "bias_2": bias_2, "value_bias_2": value_bias_2, "position": position_encoding(),
        "attention_3": wide_weights_3(i), "rotation": rotation_table(),
        "router_0": by_tile(i["L0_ffn_w_gate"]), "router_2": by_tile(i["L2_ffn_W_router"]), "router_3": by_tile(i["L3_ffn_gate_w"]),
        **expert_weights(i),
        "thought_w": np.concatenate([by_contraction(thought(w)) for w in ("agg_w", "bc_w", "d1_w", "d2_w")], axis=1),
        "thought_gate_w": by_tile(thought("gate_w")),
        "thought_rows": np.broadcast_to(np.stack([thought(w) for w in ("in_gamma", "in_beta", "agg_b", "pn_gamma", "pn_beta", "d2_b")]), (B, 6, C)),
        "thought_columns": np.concatenate([thought(w).reshape(-1, P) for w in ("d1_b", "gate_b", "bc_b")]).T,
        "thought_wide_rows": np.broadcast_to(np.stack([thought(w) for w in ("out_gamma", "out_beta")]), (P, 2, C)),
    }


def kernel(**inputs):
    import concourse.bacc as bacc
    from concourse.bass_utils import run_bass_kernel_spmd

    arrays = {f"in_{name}": np.ascontiguousarray(a) for name, a in layouts({k: np.asarray(v) for k, v in inputs.items()}).items()}
    nc = bacc.Bacc("TRN2", target_bir_lowering=False, num_devices=1)
    d = {name[3:]: nc.dram_tensor(name, a.shape, mybir.dt.from_np(a.dtype), kind="ExternalInput").ap() for name, a in arrays.items()}
    out = nc.dram_tensor("out", (P, TILES, C), F32, kind="ExternalOutput").ap()
    four_layers_kernel(nc, d, out)
    result = run_bass_kernel_spmd(nc, [arrays], core_ids=[0])
    return result.results[0]["out"].transpose(1, 0, 2).reshape(B, S, C)
```
